# Optimizing a Trainium2 kernel written in Bass

```python
import numpy as np
import jax
import jax.numpy as jnp

def _softmax(x, axis=-1):
    return jax.nn.softmax(x, axis=axis)

def _gelu(x):
    return jax.nn.gelu(x, approximate=True)

def _silu(x):
    return jax.nn.silu(x)

def _sigmoid(x):
    return jax.nn.sigmoid(x)

def _layernorm(x, axis=-1, eps=1e-05):
    m = jnp.mean(x, axis=axis, keepdims=True)
    v = jnp.var(x, axis=axis, keepdims=True)
    return (x - m) / jnp.sqrt(v + eps)

def _scatter_add(tgt, idx, src, axis=0):
    return tgt.at[idx].add(src)

def _segment_sum(src, seg, n):
    return jax.ops.segment_sum(src, seg, n)
kernel_name = 'mk_decoder_postln_d1_seqx_r8_835e7f'

def setup_inputs(seed: int=0):
    np.random.seed(seed)
    _w = jnp.asarray

    def _rec_inputs():
        import jax
        import jax.numpy as jnp
        _rk = jax.random.key(seed)
        x = -0.0002928 + 1 * jax.random.normal(jax.random.fold_in(_rk, 1), (8, 256, 128), jnp.float32)
        _lenS = 256 - jax.random.randint(jax.random.fold_in(_rk, 7), (8,), 0, max(1, 256 // 4) + 1, jnp.int32)
        _lenS2 = 256 - jax.random.randint(jax.random.fold_in(_rk, 8), (8,), 0, max(1, 256 // 4) + 1, jnp.int32)
        _ctx_1024P = jax.random.normal(jax.random.fold_in(_rk, 11), (8, 16, 128), jnp.float32)
        _ctx_1024c = jax.random.dirichlet(jax.random.fold_in(_rk, 511), 0.3 * jnp.ones((16,), jnp.float32), (8, 256))
        _ctx_1024t = jnp.einsum('bsk,bkd->bsd', _ctx_1024c, _ctx_1024P)
        _ctx_1024t = _ctx_1024t * jax.lax.rsqrt(jnp.mean(jnp.square(_ctx_1024t)) + 1e-12) * 0.953939
        ctx_1024 = -1.39393e-06 + 0.999914 * (_ctx_1024t + 0.3 * jax.random.normal(jax.random.fold_in(_rk, 611), (8, 256, 128), jnp.float32))
        _validS = jnp.arange(256)[None, :] < _lenS[:, None]
        _validS2 = jnp.arange(256)[None, :] < _lenS2[:, None]
        _causal = jnp.tril(jnp.ones((256, 256), dtype=bool))
        mask_BxS2_bf1 = jnp.ones((8, 256), dtype=bool)
        return (x, ctx_1024, mask_BxS2_bf1)
    x, ctx_1024, mask_BxS2_bf1 = _rec_inputs()

    def _L0_attn_setup():
        import jax, jax.numpy as jnp
        import numpy as np
        D_MODEL = 128
        N_HEADS = 16
        ORDER = 6
        M = 2 * ORDER - 1
        D_HEAD = D_MODEL // N_HEADS

        def _collapsed_beta() -> np.ndarray:
            j = np.arange(ORDER, dtype=np.float64)
            alpha = (j + 1.0) ** (-1.5)
            tail = np.cumsum(alpha[::-1])[::-1]
            beta = np.concatenate([[0.0], tail[1:], np.zeros(ORDER - 1)])
            return (beta / beta.sum()).astype(np.float32)

        def _cheb_features(x, m):
            ts = [jnp.ones_like(x), x]
            for _ in range(m - 2):
                ts.append(2.0 * x * ts[-1] - ts[-2])
            return jnp.stack(ts[:m], axis=-1)
        key = jax.random.key(seed)
        k1, k2, k3 = jax.random.split(key, 3)
        B, S = (2, 512)
        x = jax.random.normal(k1, (B, S, D_MODEL), dtype=jnp.float32)
        w_in = jax.random.normal(k2, (3 * D_MODEL, D_MODEL), dtype=jnp.float32) * D_MODEL ** (-0.5)
        w_out = jax.random.normal(k3, (D_MODEL, D_MODEL), dtype=jnp.float32) * D_MODEL ** (-0.5)
        beta = jnp.tile(jnp.asarray(_collapsed_beta())[None, :], (N_HEADS, 1))
        return {'x': x, 'w_in': w_in, 'w_out': w_out, 'beta': beta}
    _L0_attn_all = _L0_attn_setup()
    _L0_attn_in = {k: v for k, v in _L0_attn_all.items() if k in ('w_in', 'w_out', 'beta')}
    del _L0_attn_all

    def _L0_xattn_setup():
        import jax, jax.numpy as jnp
        import numpy as np
        DIM = 128
        HEADS = 16
        HEAD_DIM = DIM // HEADS
        ROPE_BASE = 10000.0

        def _rope_cos_sin(seq_len, head_dim, dtype=jnp.float32):
            inv_freq = 1.0 / ROPE_BASE ** (jnp.arange(0, head_dim, 2, dtype=jnp.float32) / head_dim)
            t = jnp.arange(seq_len, dtype=jnp.float32)
            freqs = jnp.outer(t, inv_freq)
            emb = jnp.concatenate([freqs, freqs], axis=-1)
            return (jnp.cos(emb).astype(dtype), jnp.sin(emb).astype(dtype))

        def _rotate_half(x):
            x1, x2 = jnp.split(x, 2, axis=-1)
            return jnp.concatenate([-x2, x1], axis=-1)

        def _apply_rope(x, cos, sin):
            return x * cos[None, None, :, :] + _rotate_half(x) * sin[None, None, :, :]
        key = jax.random.key(seed)
        ks = jax.random.split(key, 10)
        B, L, K = (2, 256, 256)
        s = 1.0 / np.sqrt(DIM)
        inp = {'target': jax.random.normal(ks[0], (B, L, DIM), jnp.float32), 'context': jax.random.normal(ks[1], (B, K, DIM), jnp.float32), 'target_mask': jnp.ones((B, L), dtype=bool), 'context_mask': jnp.ones((B, K), dtype=bool), 'Wq': jax.random.normal(ks[2], (DIM, DIM), jnp.float32) * s, 'bq': jnp.zeros((DIM,), jnp.float32), 'Wk': jax.random.normal(ks[3], (DIM, DIM), jnp.float32) * s, 'bk': jnp.zeros((DIM,), jnp.float32), 'Wv': jax.random.normal(ks[4], (DIM, DIM), jnp.float32) * s, 'bv': jnp.zeros((DIM,), jnp.float32), 'Wp': jax.random.normal(ks[5], (DIM, DIM), jnp.float32) * s, 'bp': jnp.zeros((DIM,), jnp.float32)}
        return inp
    _L0_xattn_all = _L0_xattn_setup()
    _L0_xattn_in = {k: v for k, v in _L0_xattn_all.items() if k in ('Wq', 'bq', 'Wk', 'bk', 'Wv', 'bv', 'Wp', 'bp')}
    del _L0_xattn_all

    def _L0_ffn_setup():
        import math
        import jax, jax.numpy as jnp
        import numpy as np
        TOP_K = 2
        CAP_FACTOR = 1.25
        CLAMP = 10000.0
        key = jax.random.key(seed)
        k1, k2, k3, k4, k5 = jax.random.split(key, 5)
        B, S, D, F, E = (4, 256, 128, 512, 8)
        std = 0.02
        return {'x': jax.random.normal(k1, (B, S, D), dtype=jnp.float32), 'Wr': jax.random.normal(k2, (D, E), dtype=jnp.float32) * std, 'W1': jax.random.normal(k3, (E, D, F), dtype=jnp.float32) * std, 'W3': jax.random.normal(k4, (E, D, F), dtype=jnp.float32) * std, 'W2': jax.random.normal(k5, (E, F, D), dtype=jnp.float32) * std}
    _L0_ffn_all = _L0_ffn_setup()
    _L0_ffn_in = {k: v for k, v in _L0_ffn_all.items() if k in ('Wr', 'W1', 'W3', 'W2')}
    del _L0_ffn_all
    return {'x': x, 'ctx_1024': ctx_1024, 'mask_BxS2_bf1': mask_BxS2_bf1, 'L0_attn_w_in': _L0_attn_in['w_in'], 'L0_attn_w_out': _L0_attn_in['w_out'], 'L0_attn_beta': _L0_attn_in['beta'], 'L0_xattn_Wq': _L0_xattn_in['Wq'], 'L0_xattn_bq': _L0_xattn_in['bq'], 'L0_xattn_Wk': _L0_xattn_in['Wk'], 'L0_xattn_bk': _L0_xattn_in['bk'], 'L0_xattn_Wv': _L0_xattn_in['Wv'], 'L0_xattn_bv': _L0_xattn_in['bv'], 'L0_xattn_Wp': _L0_xattn_in['Wp'], 'L0_xattn_bp': _L0_xattn_in['bp'], 'L0_ffn_Wr': _L0_ffn_in['Wr'], 'L0_ffn_W1': _L0_ffn_in['W1'], 'L0_ffn_W3': _L0_ffn_in['W3'], 'L0_ffn_W2': _L0_ffn_in['W2']}

def reference(x, ctx_1024, mask_BxS2_bf1, L0_attn_w_in, L0_attn_w_out, L0_attn_beta, L0_xattn_Wq, L0_xattn_bq, L0_xattn_Wk, L0_xattn_bk, L0_xattn_Wv, L0_xattn_bv, L0_xattn_Wp, L0_xattn_bp, L0_ffn_Wr, L0_ffn_W1, L0_ffn_W3, L0_ffn_W2):
    import jax
    import jax.numpy as jnp

    def _L0_attn_ref(x, w_in, w_out, beta):
        import jax, jax.numpy as jnp
        import numpy as np
        D_MODEL = 128
        N_HEADS = 16
        ORDER = 6
        M = 2 * ORDER - 1
        D_HEAD = D_MODEL // N_HEADS

        def _collapsed_beta() -> np.ndarray:
            j = np.arange(ORDER, dtype=np.float64)
            alpha = (j + 1.0) ** (-1.5)
            tail = np.cumsum(alpha[::-1])[::-1]
            beta = np.concatenate([[0.0], tail[1:], np.zeros(ORDER - 1)])
            return (beta / beta.sum()).astype(np.float32)

        def _cheb_features(x, m):
            ts = [jnp.ones_like(x), x]
            for _ in range(m - 2):
                ts.append(2.0 * x * ts[-1] - ts[-2])
            return jnp.stack(ts[:m], axis=-1)
        B, S, _ = x.shape
        qkv = x @ w_in.T
        q, k, v = jnp.split(qkv, 3, axis=-1)

        def to_heads(t):
            return t.reshape(B, S, N_HEADS, D_HEAD).transpose(0, 2, 1, 3)
        q, k, v = (to_heads(q), to_heads(k), to_heads(v))
        scale = D_HEAD ** (-0.5)
        q = jnp.clip(q * scale, -1.0, 1.0)
        k = jnp.clip(k * scale, -1.0, 1.0)
        tq = _cheb_features(q, M)
        tk = _cheb_features(k, M)
        tq = tq * beta[None, :, None, None, :]
        kv = jnp.einsum('bhskm,bhsv->bhkmv', tk, v)
        out = jnp.einsum('bhsdm,bhdmv->bhsv', tq, kv)
        out = out.transpose(0, 2, 1, 3).reshape(B, S, D_MODEL)
        return out @ w_out.T

    def _L0_xattn_ref(target, context, target_mask, context_mask, Wq, bq, Wk, bk, Wv, bv, Wp, bp):
        import jax, jax.numpy as jnp
        import numpy as np
        DIM = 128
        HEADS = 16
        HEAD_DIM = DIM // HEADS
        ROPE_BASE = 10000.0

        def _rope_cos_sin(seq_len, head_dim, dtype=jnp.float32):
            inv_freq = 1.0 / ROPE_BASE ** (jnp.arange(0, head_dim, 2, dtype=jnp.float32) / head_dim)
            t = jnp.arange(seq_len, dtype=jnp.float32)
            freqs = jnp.outer(t, inv_freq)
            emb = jnp.concatenate([freqs, freqs], axis=-1)
            return (jnp.cos(emb).astype(dtype), jnp.sin(emb).astype(dtype))

        def _rotate_half(x):
            x1, x2 = jnp.split(x, 2, axis=-1)
            return jnp.concatenate([-x2, x1], axis=-1)

        def _apply_rope(x, cos, sin):
            return x * cos[None, None, :, :] + _rotate_half(x) * sin[None, None, :, :]
        B, L, C = target.shape
        K = context.shape[1]
        H, D = (HEADS, HEAD_DIM)
        q = (target @ Wq.T + bq).reshape(B, L, H, D).transpose(0, 2, 1, 3)
        k = (context @ Wk.T + bk).reshape(B, K, H, D).transpose(0, 2, 1, 3)
        v = (context @ Wv.T + bv).reshape(B, K, H, D).transpose(0, 2, 1, 3)
        cos_q, sin_q = _rope_cos_sin(L, D)
        cos_k, sin_k = _rope_cos_sin(K, D)
        q = _apply_rope(q, cos_q, sin_q)
        k = _apply_rope(k, cos_k, sin_k)
        scale = D ** (-0.5)
        attn = jnp.einsum('bhld,bhkd->bhlk', q, k) * scale
        attn = jnp.where(context_mask[:, None, None, :], attn, -jnp.inf)
        attn = jax.nn.softmax(attn, axis=-1)
        x = jnp.einsum('bhlk,bhkd->bhld', attn, v)
        x = x.transpose(0, 2, 1, 3).reshape(B, L, C)
        x = x @ Wp.T + bp
        x = x * target_mask[:, :, None].astype(x.dtype)
        return x

    def _L0_ffn_ref(x, Wr, W1, W3, W2):
        import math
        import jax, jax.numpy as jnp
        import numpy as np
        TOP_K = 2
        CAP_FACTOR = 1.25
        CLAMP = 10000.0
        B, S, D = x.shape
        E = Wr.shape[1]
        K = TOP_K
        T = B * S
        cap = max(1, math.ceil(T * K * CAP_FACTOR / E))
        xf = x.reshape(T, D)
        logits = jnp.clip(xf @ Wr, -CLAMP, CLAMP)
        top_v, top_i = jax.lax.top_k(logits, K)
        m = jnp.max(top_v, axis=-1, keepdims=True)
        expv = jnp.exp(top_v - m)
        top_p = expv / (jnp.sum(expv, axis=-1, keepdims=True) + 1e-12)
        Sp = T * K
        experts = top_i.reshape(Sp)
        weights = top_p.reshape(Sp)
        tokens = jnp.repeat(jnp.arange(T), K)
        oh = experts[:, None] == jnp.arange(E)[None, :]
        pos = jnp.sum(jnp.cumsum(oh.astype(jnp.int32), axis=0) * oh, axis=-1) - 1
        kept = pos < cap
        pos_safe = jnp.where(kept, pos, cap)
        xe = jnp.zeros((E, cap + 1, D), x.dtype).at[experts, pos_safe].set(xf[tokens])[:, :cap]
        h = jax.nn.silu(jnp.einsum('ecd,edf->ecf', xe, W1)) * jnp.einsum('ecd,edf->ecf', xe, W3)
        ye = jnp.einsum('ecf,efd->ecd', h, W2)
        yp = ye[experts, jnp.minimum(pos_safe, cap - 1)]
        wk = weights * kept.astype(weights.dtype)
        out = jnp.zeros((T, D), x.dtype).at[tokens].add(wk[:, None] * yp)
        return out.reshape(B, S, D)
    x = _layernorm(x + _L0_attn_ref(x, L0_attn_w_in, L0_attn_w_out, L0_attn_beta), axis=-1)
    x = _layernorm(x + _L0_xattn_ref(x, ctx_1024, mask_BxS2_bf1, mask_BxS2_bf1, L0_xattn_Wq, L0_xattn_bq, L0_xattn_Wk, L0_xattn_bk, L0_xattn_Wv, L0_xattn_bv, L0_xattn_Wp, L0_xattn_bp), axis=-1)
    x = _layernorm(x + _L0_ffn_ref(x, L0_ffn_Wr, L0_ffn_W1, L0_ffn_W3, L0_ffn_W2), axis=-1)
    return x

_drawn_inputs = setup_inputs


def setup_inputs(seed=0):
    import zlib

    import numpy as np

    out = dict(_drawn_inputs(seed))
    spreads = {'L0_xattn_bq': (0.0, 0.416),
     'L0_xattn_bk': (0.0, 0.8),
     'L0_xattn_bv': (0.0, 0.1),
     'L0_xattn_bp': (0.0, 0.1)}
    factors = {'L0_ffn_Wr': 8.0, 'L0_ffn_W1': 7.698, 'L0_ffn_W3': 7.449, 'L0_ffn_W2': 7.502}
    for name, (base, spread) in spreads.items():
        noise = np.random.default_rng([zlib.crc32(name.encode()), seed]).standard_normal(out[name].shape)
        drawn = base * np.exp(spread * noise) if base else spread * noise
        out[name] = jnp.asarray(drawn.astype(out[name].dtype))
    for name, factor in factors.items():
        out[name] = (out[name] * factor).astype(out[name].dtype)
    return out
```

```python
from contextlib import ExitStack

import numpy as np

import concourse.bass as bass
from concourse import mybir

ALU = mybir.AluOpType
ACT = mybir.ActivationFunctionType
AX = mybir.AxisListType
F32 = mybir.dt.float32
BF16 = mybir.dt.bfloat16
U32 = mybir.dt.uint32
U8 = mybir.dt.uint8

P = 128
NB, S, D = 8, 256, 128
T = NB * S
NT = S // P
H, DH = 16, 8
M = 11
SC = float(np.float32(DH ** -0.5))
E, K, F = 8, 2, 512
CAP = 640
CT = CAP // P
FT = F // P
HALF = CAP // 2
ROW = D + 2
NROWS = E * CAP
EPS = 1e-5
CLAMP = 10000.0
FAR = 1.0e6
NOWHERE = 1 << 20
MASKED = 1.0e30
NSLOT = 8
QK_BUFS = 3
X_BUFS = 4
R2 = float(np.sqrt(2.0))
PRODS = 6
Q_PUT = ((0, 0, 3, 1), (1, 3, 5, 1), (2, 5, 6, 1))
K_PUT = ((0, 0, 5, 4), (0, 5, 6, 1), (2, 1, 2, 1), (1, 2, 4, 1))
PUTS = 16 * (len(Q_PUT) + len(K_PUT))
MASK_ROW = 6 * DH
MAX_ROW = MASK_ROW + 1

C_ID, C_COS, C_SIN, C_TRI, C_BLK, C_SGN, C_IOTA, C_SGNC = 0, 128, 384, 640, 768, 800, 928, 960
NCONST = 961
W_Q, W_KV, W_O, W_XQ, W_XQR, W_XK, W_XKR, W_XV, W_XP = (128 * i for i in (0, 1, 3, 4, 5, 6, 7, 8, 9))
NWA = 128 * 11


def constants():
    c = np.zeros((P, NCONST), np.float32)
    p = np.arange(P)
    c[:, C_ID:C_ID + P] = np.eye(P)
    inv = (1.0 / np.float32(10000.0) ** (np.arange(0, DH, 2, dtype=np.float32) / np.float32(DH))).astype(np.float32)
    fr = np.outer(np.arange(S, dtype=np.float32), inv).astype(np.float32)
    ang = np.concatenate([fr, fr], axis=1).T[p % DH]
    c[:, C_COS:C_COS + S] = np.cos(ang.astype(np.float64))
    c[:, C_SIN:C_SIN + S] = np.sin(ang.astype(np.float64))
    c[:, C_TRI:C_TRI + P] = p[:, None] < p[None, :]
    c[:, C_BLK:C_BLK + 32] = (p[:, None] % 32) // DH == np.arange(32)[None, :] // DH
    c[:, C_SGN:C_SGN + P] = np.where(p % DH < DH // 2, -1.0, 1.0)[None, :]
    c[:, C_IOTA:C_IOTA + 32] = np.arange(32)[None, :] % E
    c[:, C_SGNC] = np.where(p % DH < DH // 2, -1.0, 1.0)
    b, t, k = np.meshgrid(np.arange(NB), np.arange(NT), np.arange(K), indexing="ij")
    dest = (k * T + b * S + t * P)[None] + p[:, None, None, None]
    return c, dest.reshape(P, -1).astype(np.uint32)


def build(nc, x_d, ctx_d, mrow_d, mcol_d, beta_d, wa_d, bias_d, brow_d, wr_d, w1_d, w3_d, w2_d, const_d, dest_d,
          rows_d, out_d):
    ctx = ExitStack()
    with ctx:
        def sb(name, shape, dt=F32):
            return ctx.enter_context(nc.sbuf_tensor(name, shape, dt))

        def sem(name):
            return ctx.enter_context(nc.semaphore(name))

        def dram(name, shape, dt=F32):
            return nc.dram_tensor(name, shape, dt, kind="Internal").ap()

        packed_d = dram("packed_scratch", [NB, 2, H * DH, PRODS, S], BF16)
        xe_d = dram("xe_scratch", [NROWS, ROW])
        yb_d = dram("y_scratch", [K * T, D])

        banks = [ctx.enter_context(nc.psum_tensor(f"bank{i}", [P, 512], F32)) for i in range(2)]
        pairs = [ctx.enter_context(nc.psum_tensor(f"pair{i}", [P, 1024], F32)) for i in range(3)]
        BK = [banks[0][:, :], banks[1][:, :]] + [pairs[i // 2][:, 512 * (i % 2):512 * (i % 2) + 512] for i in range(6)]

        cn = sb("cn", [P, NCONST])
        wa = sb("wa", [P, NWA])
        wr = sb("wr", [P, E])
        bias = sb("bias", [P, 4])
        brow = sb("brow", [P, 2 * D])
        betas = sb("betas", [P, M])
        bm = sb("bm", [P, M, 32])
        mrow8 = sb("mrow8", [NB, S], U8)
        maskb = sb("maskb", [NB, S], BF16)
        mcol8 = sb("mcol8", [P, NB * NT], U8)
        tmask = sb("tmask", [P, NB * NT])
        dest = sb("dest", [P, NB, NT, K], U32)
        idb = sb("idb", [P, P], BF16)
        trib = sb("trib", [P, P], BF16)
        onesb = sb("onesb", [P, P], BF16)
        halfs = sb("halfs", [P, 16])
        minus1 = sb("minus1", [P, 1])
        zrow = sb("zrow", [P, 4 * ROW])
        ident = cn[:, C_ID:C_ID + P]

        xin = [sb(f"xin{i}", [P, NT, D]) for i in range(X_BUFS)]
        xres = sb("xres", [P, NB, NT, D])
        cin = [sb(f"cin{i}", [P, NT, D]) for i in range(2)]
        xT = sb("xT", [P, S])
        cT = sb("cT", [P, S])
        x1T = sb("x1T", [P, S])
        feat = [sb(f"feat{i}", [P, M, 2, S]) for i in range(2)]
        sq = sb("sq", [P, 2, 2 * S])
        val = [sb(f"val{i}", [P, NT, D]) for i in range(2)]
        kvt = sb("kvt", [P, M, 32])
        wq_ = sb("wcomb", [P, M, 32])
        tmp32 = sb("tmp32", [P, 3, 32])
        wbd = [sb(f"wbd{i}", [P, M, P]) for i in range(2)]
        oT = sb("oT", [P, S])
        ypre = sb("ypre", [P, NT, D])
        st6 = sb("st6", [P, NT, 6])
        mv = sb("mv", [P, NT, 2])
        ve = sb("ve", [P, NT])
        rstd = sb("rstd", [P, NT])
        v2 = sb("v2", [P, NB, NT, D])
        rc = sb("rc", [P, 2, S])
        rs = sb("rs", [P, 2, S])
        rsum = sb("rsum", [P, 2, S])
        rr = sb("rr", [P, 2, S])
        parts = [sb(f"parts{i}", [P, 3, 2, S], BF16) for i in range(2)]

        qb = [sb(f"qb{i}", [P, H, S], BF16) for i in range(QK_BUFS)]
        kb = [sb(f"kb{i}", [P, H, S], BF16) for i in range(QK_BUFS)]
        mx = [sb(f"mx{i}", [P, NT, H]) for i in range(2)]
        mr = sb("mr", [P, NT, H])
        nm = sb("nm", [P, NT, 3, H], BF16)
        mT = [sb(f"mT{i}", [3 * H, S], BF16) for i in range(2)]
        pr = [sq[:, :, :].rearrange("p a (g s) -> p (a g) s", g=2), sb("pr1", [P, 4, S])]
        vp = [sb(f"vp{i}", [P, NT, H, 32]) for i in range(2)]
        ot = sb("ot", [P, 16, 32])
        on = sb("on", [P, 16, 32])
        rden = sb("rden", [P, 16, 2])
        odn = sb("odn", [P, 512])
        u1 = sb("u1", [P, NT, D])
        x2p = sb("x2p", [P, NT, D])
        st6b = sb("st6b", [P, NT, 6])
        mvb = sb("mvb", [P, NT, 2])
        veb = sb("veb", [P, NT])
        rstdb = sb("rstdb", [P, NT])
        x2 = sb("x2", [P, NB, NT, D])
        x2T = sb("x2T", [P, S])
        lg = sb("lg", [P, NT, E])
        v8 = sb("v8", [P, NT, 8])
        i8 = sb("i8", [P, NT, 8], U32)
        idf = sb("idf", [P, NT, K])
        oh = sb("oh", [P, NT, K, E])
        ohs = sb("ohs", [P, NT, E], BF16)
        cnt = [sb(f"cnt{i}", [P, E], BF16) for i in range(2)]
        ohsum = sb("ohsum", [P, E], BF16)
        dv = sb("dv", [P, NT])
        ev = sb("ev", [P, NT])
        ev1 = sb("ev1", [P, NT])
        pm = sb("pm", [P, NT * K, E])
        pos = sb("pos", [P, NT * K])
        over = sb("over", [P, NT * K])
        slf = sb("slf", [P, NT * K])
        slot = [sb(f"slot{i}", [P, NT * K], U32) for i in range(2)]
        xp = [sb(f"xp{i}", [P, NT, K, ROW]) for i in range(2)]

        def carve(tile, at, n):
            return tile[:, :, :, :].rearrange("p a b c -> p (a b c)")[:, at:at + n]
        xe = [carve(feat[i], 0, CT * ROW).rearrange("p (c r) -> p c r", c=CT) for i in range(2)]
        xeT = [carve(feat[i], 700, CAP) for i in range(2)]
        hid = [carve(feat[i], 1400, FT * CAP).rearrange("p (f c) -> p f c", f=FT) for i in range(2)]
        ye = [carve(feat[i], 4000, CT * D).rearrange("p (c d) -> p c d", c=CT) for i in range(2)]
        sil = [carve(feat[i], 4700, HALF) for i in range(2)]
        w2 = [carve(feat[i], 5100, F).rearrange("p (f d) -> p f d", f=FT) for i in range(2)]
        w1 = [wbd[i][:, 0:4, :].rearrange("p m n -> p (m n)") for i in range(2)]
        w3 = [wbd[i][:, 4:8, :].rearrange("p m n -> p (m n)") for i in range(2)]

        def spare(tile, at):
            f32 = tile[:, :, :].rearrange("p h s -> p (h s)").bitcast(F32)
            return f32[:, at * 4 * D:(at + 1) * 4 * D].rearrange("p (t d) -> p t d", d=D)
        yl = [[spare(qb[0], 2 * i + k) for k in range(K)] for i in range(2)]
        fin = [spare(qb[1], i) for i in range(2)]
        st6d = sb("st6d", [P, 16, 6])
        mvd = sb("mvd", [P, 16, 2])
        ved = sb("ved", [P, 16])
        rstdd = sb("rstdd", [P, 16])

        names = {}

        def s_(name):
            if name not in names:
                names[name] = sem(name)
            return names[name]

        par = lambda b: b % 2

        def fl(b, m):
            return feat[par(b)][:, m].rearrange("p a s -> p (a s)")

        LAG = 2
        A_STEPS = range(-3, NB + LAG)

        block = ctx.enter_context(nc.Block())

        @block.sync
        def _(sp):
            def load_x(b):
                if b >= X_BUFS:
                    sp.wait_ge(s_("x1_sum"), b - X_BUFS + 1)
                sp.dma_start(xin[b % X_BUFS][:, :, :], x_d[b * S:(b + 1) * S, :].rearrange("(t p) d -> p t d", p=P)) \
                    .then_inc(s_(f"x_in{b % X_BUFS}"), 16)

            def load_c(b):
                if b >= 2:
                    sp.wait_ge(s_("cT_mm"), b - 1)
                sp.dma_start(cin[par(b)][:, :, :], ctx_d[b * S:(b + 1) * S, :].rearrange("(t p) d -> p t d", p=P)) \
                    .then_inc(s_(f"c_in{par(b)}"), 16)

            def store_parts(b):
                sp.wait_ge(s_("rope_hi"), b + 1)
                sp.wait_ge(s_("rope_mid"), b + 1)
                sp.wait_ge(s_("rope_lo"), b + 1)
                for w, puts in enumerate((Q_PUT, K_PUT)):
                    for part, first, end, step in puts:
                        dst = packed_d[b, w, :, first:end:step, :]
                        sp.dma_start(dst, parts[par(b)][:, part, w, None, :].to_broadcast(list(dst.shape))) \
                            .then_inc(s_(f"parts_out{par(b)}"), 16)

            def pack(b):
                qd, kd = qb[b % QK_BUFS], kb[b % QK_BUFS]
                if b == 0:
                    sp.wait_ge(s_("qk_rows"), 32 * QK_BUFS)
                    sp.wait_ge(s_("maskb_set"), 1)
                if b >= QK_BUFS:
                    sp.wait_ge(s_("e_mm"), NSLOT * (b - QK_BUFS + 1))
                sp.wait_ge(s_(f"parts_out{par(b)}"), PUTS * (b // 2 + 1))
                for w, dst in enumerate((qd, kd)):
                    src = packed_d[b, w].rearrange("(h d) r s -> h (d r) s", d=DH).rearrange("h p s -> p h s")
                    sp.dma_start(dst[0:MASK_ROW, :, :], src).then_inc(s_(f"packed{b % QK_BUFS}"), 16)
                sp.dma_start(qd[MAX_ROW:MAX_ROW + 3, :, :].rearrange("p h s -> p (h s)"), rows_d[3:6, :]) \
                    .then_inc(s_(f"packed{b % QK_BUFS}"), 16)
                sp.dma_start(kd[MASK_ROW:MASK_ROW + 1, :, :], maskb[b:b + 1, None, :].to_broadcast([1, H, S])) \
                    .then_inc(s_(f"packed{b % QK_BUFS}"), 16)

            load_x(0)
            sp.dma_start(cn[:, :], const_d).then_inc(s_("const_in"), 16)
            sp.dma_start(wa[:, :], wa_d).then_inc(s_("wa_in"), 16)
            load_x(1)
            for tile, src in ((bias, bias_d), (brow, brow_d), (betas, beta_d), (mrow8, mrow_d), (mcol8, mcol_d),
                              (wr, wr_d)):
                sp.dma_start(tile[:, :], src).then_inc(s_("small_in"), 16)
            sp.dma_start(dest[:, :, :, :].rearrange("p b t k -> p (b t k)"), dest_d).then_inc(s_("small_in"), 16)
            load_x(2)
            load_x(3)
            load_c(0)
            load_c(1)
            sp.wait_ge(s_("zrow_set"), 2)
            for i in range(NROWS // (P * 4)):
                sp.dma_start(xe_d[i * 4 * P:(i + 1) * 4 * P, :].rearrange("(p r) n -> p (r n)", p=P), zrow[:, :]) \
                    .then_inc(s_("xe_cleared"), 16)
            for i in range(K * T // (P * 4)):
                sp.dma_start(yb_d[i * 4 * P:(i + 1) * 4 * P, :].rearrange("(p r) n -> p r n", p=P),
                             zrow[:, :].rearrange("p (r n) -> p r n", r=4)[:, :, 0:D]).then_inc(s_("y_cleared"), 16)
            sp.wait_ge(s_("qk_cleared"), 2 * QK_BUFS)
            for i in range(QK_BUFS):
                sp.dma_start(qb[i][MASK_ROW:MASK_ROW + 1, :, :].rearrange("p h s -> p (h s)"), rows_d[0:1, :]) \
                    .then_inc(s_("qk_rows"), 16)
                sp.dma_start(kb[i][MAX_ROW:MAX_ROW + 3, :, :].rearrange("p h s -> p (h s)"), rows_d[0:3, :]) \
                    .then_inc(s_("qk_rows"), 16)

            def put_max(b):
                sp.wait_ge(s_("mT_ev"), b + 1)
                sp.wait_ge(s_("m_mm"), NSLOT * (b + 1))
                for r in range(3):
                    sp.dma_start(qb[b % QK_BUFS][MAX_ROW + r:MAX_ROW + r + 1, :, :], mT[par(b)][H * r:H * r + H, :]) \
                        .then_inc(s_(f"max_put{b % QK_BUFS}"), 16)

            for i in A_STEPS:
                if 4 <= i + 4 < NB:
                    load_x(i + 4)
                if 2 <= i - LAG + 2 < NB:
                    load_c(i - LAG + 2)
                if 0 <= i - LAG < NB:
                    store_parts(i - LAG)
                if 0 <= i - LAG - 1 < QK_BUFS:
                    pack(i - LAG - 1)

            put_max(0)
            for b in range(NB):
                if b + 1 < NB:
                    put_max(b + 1)
                if b + QK_BUFS < NB:
                    pack(b + QK_BUFS)

            def load_w(e):
                if e >= 2:
                    sp.wait_ge(s_("ye_mm"), CT * (e - 1))
                sm = s_(f"w_in{par(e)}")
                sp.dma_start(w1[par(e)], w1_d[e]).then_inc(sm, 16)
                sp.dma_start(w3[par(e)], w3_d[e]).then_inc(sm, 16)
                sp.dma_start(w2[par(e)][:, :, :], w2_d[e].rearrange("(f p) d -> p f d", p=P)).then_inc(sm, 16)

            def load_xe(e):
                if e >= 2:
                    sp.wait_ge(s_(f"ye_out{par(e)}"), 16 * CT * (e // 2))
                sp.dma_start(xe[par(e)], xe_d[e * CAP:(e + 1) * CAP, :].rearrange("(c p) r -> p c r", p=P)) \
                    .then_inc(s_(f"xe_in{par(e)}"), 16)

            load_w(0)
            load_w(1)
            sp.wait_ge(s_("rows_out0"), 8 * NB * NT * K)
            sp.wait_ge(s_("rows_out1"), 8 * NB * NT * K)
            load_xe(0)
            load_xe(1)
            for e in range(2, E):
                load_w(e)
                load_xe(e)
            sp.wait_ge(s_("ye_out0"), 8 * CT * E)
            sp.wait_ge(s_("ye_out1"), 8 * CT * E)

            def load_y(c):
                for k in range(K):
                    r = k * T + c * 4 * P
                    sp.dma_start(yl[par(c)][k][:, :, :], yb_d[r:r + 4 * P, :].rearrange("(t p) d -> p t d", p=P)) \
                        .then_inc(s_(f"y_in{par(c)}"), 16)

            load_y(0)
            load_y(1)
            for c in range(4):
                if c + 2 < 4:
                    sp.wait_ge(s_("y_sum"), c + 1)
                    load_y(c + 2)
            for c in range(4):
                sp.wait_ge(s_("fin_done"), 4 * (c + 1))
                sp.dma_start(out_d[c * 4 * P:(c + 1) * 4 * P, :].rearrange("(t p) d -> p t d", p=P), fin[par(c)][:, :, :]) \
                    .then_inc(s_(f"out_done{par(c)}"), 16)
            sp.wait_ge(s_("out_done0"), 32)
            sp.wait_ge(s_("out_done1"), 32)
            sp.wait_ge(s_("xe_cleared"), 16 * (NROWS // (4 * P)))
            sp.wait_ge(s_("y_cleared"), 16 * (K * T // (4 * P)))

        @block.tensor
        def _(pe):
            b_T, b_Q, b_KV, b_V2, b_ST, b_O, b_R1, b_R2 = BK

            def mm(out, lhsT, rhs, start=True, stop=True):
                return pe.matmul(out, lhsT, rhs, start=start, stop=stop)

            def transposes(i):
                if 0 <= i + 3 < NB:
                    b = i + 3
                    pe.wait_ge(s_(f"x_in{b % X_BUFS}"), 16 * (b // X_BUFS + 1))
                    if b == 0:
                        pe.wait_ge(s_("const_in"), 16)
                    else:
                        pe.wait_ge(s_("xT_ev"), b)
                    if b >= 3 + LAG:
                        pe.wait_ge(s_("cT_ev"), b - 2 - LAG)
                    for t in range(NT):
                        ins = pe.transpose(b_T[:, t * P:(t + 1) * P], xin[b % X_BUFS][:, t, :], ident)
                    ins.then_inc(s_("xT_mm"), 1)
                if 0 <= i + 1 - LAG < NB:
                    b = i + 1 - LAG
                    pe.wait_ge(s_(f"c_in{par(b)}"), 16 * (b // 2 + 1))
                    pe.wait_ge(s_("xT_ev"), min(NB, b + LAG + 1))
                    if b >= 1:
                        pe.wait_ge(s_("cT_ev"), b)
                    for t in range(NT):
                        ins = pe.transpose(b_T[:, 256 + t * P:256 + (t + 1) * P], cin[par(b)][:, t, :], ident)
                    ins.then_inc(s_("cT_mm"), 1)

            def x1_transpose(i):
                if 0 <= i + 1 - LAG < NB:
                    b = i + 1 - LAG
                    pe.wait_ge(s_("x1_done"), NT * (b + 1))
                    pe.wait_ge(s_("y_clip"), 2 * min(NB, b + LAG + 2))
                    for t in range(NT):
                        ins = pe.transpose(b_Q[:, t * P:(t + 1) * P], xres[:, b, t, :], ident)
                    ins.then_inc(s_("x1T_mm"), 1)

            def out_features(b):
                pe.wait_ge(s_("wbd_set"), 4 * (b + 1))
                if b >= 1:
                    pe.wait_ge(s_("oT_ev"), b)
                for m in range(M):
                    ins = mm(b_O[:, 0:S], wbd[par(b)][:, m, :], feat[par(b)][:, m, 0, :], m == 0, m == M - 1)
                ins.then_inc(s_("out_mm"), 1)

            def key_value(b):
                pe.wait_ge(s_("f_dve"), 4 * (b + 1))
                pe.wait_ge(s_("f_pool"), 2 * (b + 1))
                pe.wait_ge(s_("f8"), b + 1)
                pe.wait_ge(s_("val_ev"), b + 1)
                if b >= 1:
                    pe.wait_ge(s_("kvt_ev"), b)
                for t in range(NT):
                    for g in range(4):
                        ins = mm(b_ST[32 * g:32 * g + 32, 0:32 * M].rearrange("p (j v) -> p j v", j=M),
                                 val[par(b)][:, t, 32 * g:32 * g + 32],
                                 feat[par(b)][:, :, 1, t * P + 32 * g:t * P + 32 * g + 32], t == 0, t == NT - 1)
                ins.then_inc(s_("kv_mm"), 1)

            def project(b):
                pe.wait_ge(s_("xT_ev"), b + 1)
                if b == 0:
                    pe.wait_ge(s_("wa_in"), 16)
                if b >= 2 + LAG:
                    pe.wait_ge(s_("x1T_ev"), b - 1 - LAG)
                if b >= 1:
                    pe.wait_ge(s_("y_clip"), 2 * b)
                    pe.wait_ge(s_("val_ev"), b)
                mm(b_Q[:, 0:S], wa[:, W_Q:W_Q + D], xT[:, :])
                for t in range(NT):
                    ins = mm(b_KV[:, t * 256:(t + 1) * 256], xT[:, t * P:(t + 1) * P], wa[:, W_KV:W_KV + 2 * D])
                ins.then_inc(s_("qkv_mm"), 1)

            def rope_project(b):
                pe.wait_ge(s_("cT_ev"), b + 1)
                pe.wait_ge(s_("x1_sum"), min(NB, b + LAG))
                if b == 0:
                    pe.wait_ge(s_("rot_signs"), 2)
                else:
                    pe.wait_ge(s_("v2_ev"), b)
                for t in range(NT):
                    ins = mm(b_V2[:, t * P:(t + 1) * P], cT[:, t * P:(t + 1) * P], wa[:, W_XV:W_XV + D])
                ins.then_inc(s_("v2_mm"), 1)
                if b >= 1:
                    pe.wait_ge(s_("rope_mul"), 4 * b)
                mm(b_R1[:, S:2 * S], wa[:, W_XK:W_XK + D], cT[:, :])
                mm(b_R2[:, S:2 * S], wa[:, W_XKR:W_XKR + D], cT[:, :])
                pe.wait_ge(s_("x1T_ev"), b + 1)
                mm(b_R1[:, 0:S], wa[:, W_XQ:W_XQ + D], x1T[:, :])
                mm(b_R2[:, 0:S], wa[:, W_XQR:W_XQR + D], x1T[:, :]).then_inc(s_("rope_mm"), 1)

            def out_project(b):
                pe.wait_ge(s_("oT_ev"), b + 1)
                if b >= 1:
                    pe.wait_ge(s_("x1_sum"), b)
                if b >= LAG:
                    pe.wait_ge(s_("v2_ev"), b - LAG + 1)
                for t in range(NT):
                    ins = mm(b_V2[:, t * P:(t + 1) * P], oT[:, t * P:(t + 1) * P], wa[:, W_O:W_O + D])
                ins.then_inc(s_("y_mm"), 1)

            for i in A_STEPS:
                if 0 <= i < NB:
                    out_features(i)
                if 0 <= i + 2 < NB:
                    project(i + 2)
                if 0 <= i + 1 < NB:
                    key_value(i + 1)
                if 0 <= i - LAG < NB:
                    rope_project(i - LAG)
                transposes(i)
                x1_transpose(i)
                if 0 <= i < NB:
                    out_project(i)

            od, gb = BK[0], BK[1]
            m_pair, e_pair = pairs[0:2], pairs[2]

            def m_slot(n):
                b, k = divmod(n, NSLOT)
                c, hq = divmod(k, 4)
                if n == 0:
                    pe.wait_ge(s_("rope_mul"), 4 * NB)
                    pe.wait_ge(s_("v2_ev"), NB)
                    pe.wait_ge(s_("x1_sum"), NB)
                if k == 0:
                    pe.wait_ge(s_(f"packed{b % QK_BUFS}"), 16 * 4 * (b // QK_BUFS + 1))
                if n >= 2:
                    pe.wait_ge(s_("max_done"), n - 1)
                for g in range(4):
                    h = 4 * hq + g
                    ins = mm(m_pair[n % 2][:, g * S:(g + 1) * S], qb[b % QK_BUFS][:, h, c * P:(c + 1) * P],
                             kb[b % QK_BUFS][:, h, :])
                ins.then_inc(s_("m_mm"), 1)

            def max_transpose(b):
                pe.wait_ge(s_("nm_done"), b + 1)
                g_free(("mt", b))
                for c in range(NT):
                    ins = pe.transpose(gb[0:3 * H, :].bitcast(BF16)[:, c * P:(c + 1) * P],
                                       nm[:, c, :, :].rearrange("p r h -> p (r h)"), idb[:, :])
                ins.then_inc(s_("mT_mm"), 1)

            def e_slot(n):
                b, k = divmod(n, NSLOT)
                hq, kc = divmod(k, 2)
                if k == 0:
                    pe.wait_ge(s_(f"max_put{b % QK_BUFS}"), 48 * (b // QK_BUFS + 1))
                if n >= 1:
                    pe.wait_ge(s_("exp_done"), n)
                for g in range(4):
                    h = 4 * hq + g
                    ins = mm(e_pair[:, g * S:(g + 1) * S], kb[b % QK_BUFS][:, h, kc * P:(kc + 1) * P],
                             qb[b % QK_BUFS][:, h, :])
                ins.then_inc(s_("e_mm"), 1)

            def pv_slot(n):
                b, k = divmod(n, NSLOT)
                hq, kc = divmod(k, 2)
                tt, j = divmod(hq, 2)
                pe.wait_ge(s_("exp_done"), n + 1)
                if k == 0:
                    pe.wait_ge(s_("vp_set"), 2 * (b + 1))
                    if b >= 1:
                        pe.wait_ge(s_("od_read"), b)
                for g in range(4):
                    ins = mm(od[32 * g:32 * g + 32, tt * S:(tt + 1) * S], vp[par(b)][:, kc, 4 * hq + g, :],
                             pr[n % 2][:, g, :], j == 0 and kc == 0, j == 1 and kc == 1)
                ins.then_inc(s_("pv_mm"), 1)

            readers = {"mt": ("mT_ev", 1), "x2t": ("x2T_ev", 1), "log": ("lg_done", 1), "pos": ("pm_done", 1),
                       "wp": ("u1_done", 1)}
            last = [None]

            def g_free(use):
                if last[0] is not None:
                    name, c = last[0]
                    pe.wait_ge(s_(readers[name][0]), readers[name][1] * (c + 1))
                last[0] = use

            def wp(b):
                pe.wait_ge(s_("odn_done"), b + 1)
                g_free(("wp", b))
                for t in range(NT):
                    for tt in range(2):
                        ins = mm(gb[:, t * P:(t + 1) * P], odn[:, tt * S + t * P:tt * S + (t + 1) * P],
                                 wa[:, W_XP + tt * D:W_XP + (tt + 1) * D], tt == 0, tt == 1)
                ins.then_inc(s_("wp_mm"), 1)

            def x2_transpose(b):
                pe.wait_ge(s_("x2_done"), NT * (b + 1))
                g_free(("x2t", b))
                for t in range(NT):
                    ins = pe.transpose(gb[:, t * P:(t + 1) * P], x2[:, b, t, :], ident)
                ins.then_inc(s_("x2T_mm"), 1)

            def logits(b):
                pe.wait_ge(s_("x2T_ev"), b + 1)
                g_free(("log", b))
                for t in range(NT):
                    ins = mm(gb[:, t * E:(t + 1) * E], x2T[:, t * P:(t + 1) * P], wr[:, :])
                ins.then_inc(s_("lg_mm"), 1)

            def positions(b):
                pe.wait_ge(s_("ohs_done"), b + 1)
                if b == 0:
                    pe.wait_ge(s_("cnt_done"), 1)
                else:
                    pe.wait_ge(s_("cnt_next"), b)
                g_free(("pos", b))
                for t in range(NT):
                    mm(gb[:, t * E:(t + 1) * E], trib[:, :], ohs[:, t, :], True, False)
                    if t == 1:
                        mm(gb[:, t * E:(t + 1) * E], onesb[:, :], ohs[:, 0, :], False, False)
                    ins = mm(gb[:, t * E:(t + 1) * E], onesb[:, :], cnt[par(b)][:, :], False, True)
                ins.then_inc(s_("pos_mm"), 1)

            for n in range(NSLOT * (NB + 3)):
                b, k = divmod(n, NSLOT)
                if n < NSLOT * NB:
                    m_slot(n)
                if k == 1 and 0 <= b - 1 < NB:
                    max_transpose(b - 1)
                if 0 <= n - 12 < NSLOT * NB:
                    e_slot(n - 12)
                if 0 <= n - 13 < NSLOT * NB:
                    pv_slot(n - 13)
                if k == 6 and 0 <= b - 2 < NB:
                    wp(b - 2)
                if k == 2 and 0 <= b - 3 < NB:
                    x2_transpose(b - 3)
                if k == 3 and 0 <= b - 3 < NB:
                    logits(b - 3)
                if k == 5 and 0 <= b - 3 < NB:
                    positions(b - 3)

            def xe_transpose(e):
                pe.wait_ge(s_(f"xe_in{par(e)}"), 16 * (e // 2 + 1))
                if e == 0:
                    pe.wait_ge(s_("pm_done"), NB)
                else:
                    pe.wait_ge(s_("xeT_ev"), 2 * e)
                for c in range(CT):
                    ins = pe.transpose(BK[c // 4][:, (c % 4) * P:(c % 4 + 1) * P], xe[par(e)][:, c, 0:D], ident)
                    if c >= 3:
                        ins.then_inc(s_("xeT_mm"), 1)

            def hidden(e):
                for f in range(FT):
                    for half in range(2):
                        n = (e * FT + f) * 2 + half
                        if f == 0 and half == 0:
                            pe.wait_ge(s_(f"w_in{par(e)}"), 48 * (e // 2 + 1))
                            pe.wait_ge(s_("xeT_ev"), 2 * (e + 1))
                        if n >= 2:
                            pe.wait_ge(s_("hid_done"), n - 1)
                        gu = pairs[n % 2]
                        r = xeT[par(e)][:, half * HALF:(half + 1) * HALF]
                        mm(gu[:, 0:HALF], w1[par(e)][:, f * P:(f + 1) * P], r)
                        mm(gu[:, 512:512 + HALF], w3[par(e)][:, f * P:(f + 1) * P], r).then_inc(s_("gu_mm"), 1)

            def down(e):
                pe.wait_ge(s_("hid_done"), 2 * FT * (e + 1))
                for c in range(CT):
                    if c % 4 == 0 and e >= 1:
                        pe.wait_ge(s_("ye_ev"), CT * e - (1 if c == 0 else 0))
                    o = pairs[2][:, c * P:(c + 1) * P]
                    for f in range(FT):
                        ins = mm(o, hid[par(e)][:, f, c * P:(c + 1) * P], w2[par(e)][:, f, :], f == 0, f == FT - 1)
                    ins.then_inc(s_("ye_mm"), 1)

            xe_transpose(0)
            for e in range(E):
                hidden(e)
                if e + 1 < E:
                    xe_transpose(e + 1)
                down(e)

        @block.scalar
        def _(act):
            b_T, b_Q, b_KV, b_V2, b_ST, b_O, b_R1, b_R2 = BK

            for i in A_STEPS:
                f, r = i + 2, i - LAG
                if 0 <= i < NB:
                    act.wait_ge(s_("out_mm"), i + 1)
                    if i >= 1:
                        act.wait_ge(s_("y_mm"), i)
                    act.copy(oT[:, :], b_O[:, 0:S]).then_inc(s_("oT_ev"), 1)
                if 0 <= f < NB:
                    act.wait_ge(s_("qkv_mm"), f + 1)
                    act.wait_ge(s_("y_clip"), 2 * (f + 1))
                    act.activation(sq[:, 0, :], fl(f, 1), ACT.Square, scale=0.5).then_inc(s_("sq2"), 1)
                    act.copy(val[par(f)][:, :, :],
                             b_KV.rearrange("p (t k n) -> p t k n", t=NT, k=2)[:, :, 1, :]).then_inc(s_("val_ev"), 1)
                    act.wait_ge(s_("sq2"), f + 1)
                    if f == 0:
                        act.wait_ge(s_("halfs_set"), 2)
                    act.activation(fl(f, 2), sq[:, 0, :], ACT.Identity, bias=minus1[:, :]).then_inc(s_("t2"), 1)
                if 0 <= f < NB:
                    act.wait_ge(s_("t2"), f + 1)
                    act.activation(sq[:, 1, :], fl(f, 2), ACT.Square, scale=R2).then_inc(s_("sq4"), 1)
                if 0 <= f < NB:
                    act.wait_ge(s_("sq4"), f + 1)
                    act.activation(fl(f, 4), sq[:, 1, :], ACT.Identity, bias=minus1[:, :]).then_inc(s_("t4"), 1)
                    act.wait_ge(s_("t4"), f + 1)
                    act.activation(fl(f, 8), fl(f, 4), ACT.Square, scale=R2).then_inc(s_("f8"), 1)
                if 0 <= i + 1 < NB:
                    b = i + 1
                    act.wait_ge(s_("w_done"), b + 1)
                    for g in range(4):
                        act.copy(wbd[par(b)][32 * g:32 * g + 32, :, 32 * g:32 * g + 32], wq_[32 * g:32 * g + 32, :, :]) \
                            .then_inc(s_("wbd_set"), 1)
                if 0 <= i + 3 < NB:
                    b = i + 3
                    act.wait_ge(s_("xT_mm"), b + 1)
                    if b >= 2 + LAG:
                        act.wait_ge(s_("cT_mm"), b - 1 - LAG)
                    if b >= 1:
                        act.wait_ge(s_("qkv_mm"), b)
                    act.copy(xT[:, :], b_T[:, 0:S]).then_inc(s_("xT_ev"), 1)
                if 0 <= r + 1 < NB:
                    act.wait_ge(s_("cT_mm"), r + 2)
                    if r + 1 >= 1:
                        act.wait_ge(s_("rope_mm"), r + 1)
                    act.copy(cT[:, :], b_T[:, S:2 * S]).then_inc(s_("cT_ev"), 1)
                    act.wait_ge(s_("x1T_mm"), r + 2)
                    act.copy(x1T[:, :], b_Q[:, 0:S]).then_inc(s_("x1T_ev"), 1)
                if 0 <= r < NB:
                    act.wait_ge(s_("rope_sum"), r + 1)
                    if r >= 2:
                        act.wait_ge(s_(f"parts_out{par(r)}"), PUTS * (r // 2))
                    act.copy(parts[par(r)][:, 0], rsum[:, :, :]).then_inc(s_("rope_hi"), 1)
                    act.wait_ge(s_("rope_r"), r + 1)
                    act.copy(parts[par(r)][:, 1], rr[:, :, :]).then_inc(s_("rope_mid"), 1)

            gb = BK[1]
            for n in range(NSLOT * (NB + 3)):
                b, k = divmod(n, NSLOT)
                if k == 1 and 0 <= b - 1 < NB:
                    c = b - 1
                    act.wait_ge(s_("mT_mm"), c + 1)
                    if c >= QK_BUFS:
                        act.wait_ge(s_(f"max_put{c % QK_BUFS}"), 48 * (c // QK_BUFS))
                    if c >= 2:
                        act.wait_ge(s_(f"max_put{(c - 2) % QK_BUFS}"), 48 * ((c - 2) // QK_BUFS + 1))
                    act.copy(mT[par(c)][:, :], gb[0:3 * H, :].bitcast(BF16)[:, 0:S]).then_inc(s_("mT_ev"), 1)
                m = n - 12
                if 0 <= m < NSLOT * NB:
                    act.wait_ge(s_("e_mm"), m + 1)
                    if m >= 2:
                        act.wait_ge(s_("pv_mm"), m - 1)
                    act.activation(pr[m % 2][:, :, :].rearrange("p g s -> p (g s)"), pairs[2][:, :], ACT.Exp, scale=SC) \
                        .then_inc(s_("exp_done"), 1)
                if k == 2 and 0 <= b - 3 < NB:
                    c = b - 3
                    act.wait_ge(s_("x2T_mm"), c + 1)
                    act.copy(x2T[:, :], gb[:, 0:S]).then_inc(s_("x2T_ev"), 1)
                if k == 5 and 0 <= b - 3 < NB:
                    c = b - 3
                    act.wait_ge(s_("dv_done"), c + 1)
                    act.activation(ev[:, :], dv[:, :], ACT.Exp).then_inc(s_("ev_done"), 1)

            for e in range(E):
                def take_xeT(e):
                    act.wait_ge(s_("xeT_mm"), 2 * e + 1)
                    act.copy(xeT[par(e)][:, 0:4 * P], BK[0][:, :]).then_inc(s_("xeT_ev"), 1)
                    act.wait_ge(s_("xeT_mm"), 2 * e + 2)
                    act.copy(xeT[par(e)][:, 4 * P:CAP], BK[1][:, 0:P]).then_inc(s_("xeT_ev"), 1)
                if e == 0:
                    take_xeT(0)
                for f in range(FT):
                    for half in range(2):
                        n = (e * FT + f) * 2 + half
                        act.wait_ge(s_("gu_mm"), n + 1)
                        if n >= 2:
                            act.wait_ge(s_("hid_done"), n - 1)
                        act.activation(sil[n % 2], pairs[n % 2][:, 0:HALF], ACT.Silu).then_inc(s_("silu_done"), 1)
                if e + 1 < E:
                    take_xeT(e + 1)

        @block.vector
        def _(dve):
            b_T, b_Q, b_KV, b_V2, b_ST, b_O, b_R1, b_R2 = BK
            tt, ts, stt = dve.tensor_tensor, dve.tensor_scalar, dve.scalar_tensor_tensor
            chain = [0]

            def link(ins):
                chain[0] += 1
                ins.then_inc(s_("dve_chain"), 1)
                dve.wait_ge(s_("dve_chain"), chain[0])

            def keep(ins):
                chain[0] += 1
                ins.then_inc(s_("dve_chain"), 1)
                return chain[0]

            def need(at):
                dve.wait_ge(s_("dve_chain"), at)

            for i in range(2):
                dve.memset(feat[i][:, 0, :, :], 1.0)
                dve.memset(wbd[i][:, :, :], 0.0)
            dve.memset(on[:, :, :], 0.0)
            dve.memset(onesb[:, :], 1.0)
            dve.memset(cnt[0][:, :], 0.0).then_inc(s_("cnt_done"), 1)
            dve.wait_ge(s_("const_in"), 16)
            dve.tensor_copy(idb[:, :], ident)
            link(dve.tensor_copy(trib[:, :], cn[:, C_TRI:C_TRI + P]))
            need(chain[0])
            dve.wait_ge(s_("small_in"), 16 * 7)
            dve.wait_ge(s_("wa_in"), 16)
            sgn = cn[:, C_SGN:C_SGN + P]
            tt(wa[:, W_XQR:W_XQR + D], wa[:, W_XQR:W_XQR + D], sgn, ALU.mult).then_inc(s_("rot_signs"), 1)
            tt(wa[:, W_XKR:W_XKR + D], wa[:, W_XKR:W_XKR + D], sgn, ALU.mult).then_inc(s_("rot_signs"), 1)
            sc = cn[:, C_SGNC:C_SGNC + 1]
            link(ts(bias[:, 2:4], bias[:, 2:4], sc, None, ALU.mult))
            link(ts(betas[:, 1:2], betas[:, 1:2], SC * SC, None, ALU.mult))
            link(ts(betas[:, 6:7], betas[:, 6:7], 2.0, None, ALU.mult))
            link(ts(betas[:, 10:11], betas[:, 10:11], 2.0, None, ALU.mult))
            for m in range(M):
                ins = ts(bm[:, m, :], cn[:, C_BLK:C_BLK + 32], betas[:, m:m + 1], None, ALU.mult)
            link(ins)
            link(ts(tmask[:, :], mcol8[:, :], 1.0, None, ALU.mult))
            ts(maskb[:, :], mrow8[:, :], -1.0, MASKED, ALU.add, ALU.mult).then_inc(s_("maskb_set"), 1)

            def clip(b):
                dve.wait_ge(s_("qkv_mm"), b + 1)
                y = feat[par(b)]
                ts(y[:, 1, 0, :], b_Q[:, 0:S], 1.0 / SC, -1.0 / SC, ALU.min, ALU.max).then_inc(s_("y_clip"), 1)
                ts(y[:, 1, 1, :].rearrange("p (t n) -> p t n", t=NT),
                   b_KV.rearrange("p (t k n) -> p t k n", t=NT, k=2)[:, :, 0, :],
                   1.0 / SC, -1.0 / SC, ALU.min, ALU.max).then_inc(s_("y_clip"), 1)

            def features(b):
                dve.wait_ge(s_("y_clip"), 2 * (b + 1))
                dve.wait_ge(s_("t2"), b + 1)
                stt(fl(b, 3), fl(b, 1), 2 * SC, fl(b, 2), ALU.mult, ALU.mult).then_inc(s_("f_dve"), 1)
                dve.wait_ge(s_("t4"), b + 1)
                stt(fl(b, 5), fl(b, 1), 2 * SC, fl(b, 4), ALU.mult, ALU.mult).then_inc(s_("f_dve"), 1)
                dve.wait_ge(s_("f_dve"), 4 * b + 1)
                stt(fl(b, 7), fl(b, 3), 2.0, fl(b, 4), ALU.mult, ALU.mult).then_inc(s_("f_dve"), 1)
                dve.wait_ge(s_("f8"), b + 1)
                stt(fl(b, 9), fl(b, 1), 2 * SC, fl(b, 8), ALU.mult, ALU.mult).then_inc(s_("f_dve"), 1)

            def combine(b):
                dve.wait_ge(s_("kv_mm"), b + 1)
                dve.transpose(kvt[:, :, :].rearrange("p j v -> p (j v)"), b_ST[:, 0:32 * M]).then_inc(s_("kvt_ev"), 1)
                dve.wait_ge(s_("kvt_ev"), b + 1)
                k = lambda j: kvt[:, j, :]
                w = lambda j: wq_[:, j, :]
                a3 = keep(stt(k(3), k(1), -SC, k(3), ALU.mult, ALU.add))
                a7 = keep(tt(k(7), k(7), k(5), ALU.subtract))
                keep(tt(k(8), k(8), k(0), ALU.subtract))
                a6 = keep(stt(k(6), k(6), 2.0, k(2), ALU.mult, ALU.subtract))
                a9 = keep(stt(k(9), k(1), -2.0 * SC, k(9), ALU.mult, ALU.add))
                need(a7)
                keep(tt(k(5), k(5), k(3), ALU.subtract))
                a7 = keep(stt(k(7), k(1), -SC, k(7), ALU.mult, ALU.add))
                need(a6)
                a10 = keep(stt(k(10), k(10), 2.0, k(6), ALU.mult, ALU.subtract))
                need(a7)
                keep(tt(k(9), k(9), k(7), ALU.subtract))
                need(a10)
                link(stt(k(10), k(2), -2.0, k(10), ALU.mult, ALU.add))
                if b >= 1:
                    dve.wait_ge(s_("wbd_set"), 4 * b)
                link(tt(wq_[:, :, :], kvt[:, :, :], bm[:, :, :], ALU.mult))
                v, y, x = tmp32[:, 0, :], tmp32[:, 1, :], tmp32[:, 2, :]
                keep(tt(v, w(7), w(9), ALU.add))
                b3 = keep(tt(w(3), w(3), w(5), ALU.subtract))
                b7 = keep(tt(w(7), w(7), w(9), ALU.subtract))
                bx = keep(tt(x, w(6), w(10), ALU.add))
                need(b3)
                by = keep(tt(y, w(3), v, ALU.add))
                need(b7)
                keep(tt(w(5), w(5), w(7), ALU.subtract))
                need(bx)
                keep(stt(w(2), x, -0.5, w(2), ALU.mult, ALU.add))
                keep(tt(w(6), w(6), w(10), ALU.subtract))
                need(by)
                keep(stt(w(1), y, -SC, w(1), ALU.mult, ALU.add))
                keep(tt(w(0), w(0), w(8), ALU.subtract))
                need(chain[0])
                dve.tensor_copy(tmp32[:, 0, 0:1], w(0)[:, 0:1]).then_inc(s_("w_done"), 1)

            def values(b):
                dve.wait_ge(s_("v2_mm"), b + 1)
                tt(v2[:, b].rearrange("p t n -> p (t n)").rearrange("p (t n) -> p t n", t=NT),
                   b_V2[:, 0:S].rearrange("p (t n) -> p t n", t=NT),
                   brow[:, None, 0:D].to_broadcast([P, NT, D]), ALU.add).then_inc(s_("v2_ev"), 1)

            def rope(b):
                dve.wait_ge(s_("rope_mm"), b + 1)
                if b >= 1:
                    dve.wait_ge(s_("rope_sum"), b)
                for w in range(2):
                    for bank, table, off, dst in ((b_R1, C_COS, 0, rc), (b_R2, C_SIN, 2, rs)):
                        stt(dst[:, w, :], bank[:, w * S:(w + 1) * S], bias[:, off + w:off + w + 1],
                            cn[:, table:table + S], ALU.add, ALU.mult).then_inc(s_("rope_mul"), 1)

            def norm_stats(src, st, mvt, done):
                for t in range(NT):
                    at = keep(dve.bn_stats(st[:, t, :], src[:, t, :]))
                need(at)
                for t in range(NT):
                    dve.bn_aggr(mvt[:, t, :], st[:, t, :]).then_inc(s_(done), 1)

            def norm1(b):
                dve.wait_ge(s_("y_mm"), b + 1)
                tt(ypre[:, :, :], b_V2[:, 0:S].rearrange("p (t n) -> p t n", t=NT), xin[b % X_BUFS][:, :, :], ALU.add) \
                    .then_inc(s_("x1_sum"), 1)
                dve.wait_ge(s_("x1_sum"), b + 1)
                norm_stats(ypre, st6, mv, "mv1")

            def norm1_end(b):
                dve.wait_ge(s_("rstd1"), b + 1)
                for t in range(NT):
                    ts(xres[:, b, t, :], ypre[:, t, :], mv[:, t, 0:1], rstd[:, t:t + 1], ALU.subtract, ALU.mult) \
                        .then_inc(s_("x1_done"), 1)

            for i in A_STEPS:
                if 0 <= i + 2 < NB:
                    clip(i + 2)
                if 0 <= i + 1 < NB:
                    combine(i + 1)
                if 0 <= i - LAG < NB:
                    values(i - LAG)
                if 0 <= i + 2 < NB:
                    features(i + 2)
                if 0 <= i < NB:
                    norm1(i)
                if 0 <= i - LAG < NB:
                    rope(i - LAG)
                if 0 <= i < NB:
                    norm1_end(i)

            od, gb = BK[0], BK[1]

            def row_max(n):
                b, k = divmod(n, NSLOT)
                c, hq = divmod(k, 4)
                dve.wait_ge(s_("m_mm"), n + 1)
                dve.tensor_reduce(mx[par(b)][:, c, 4 * hq:4 * hq + 4],
                                  pairs[n % 2][:, :].rearrange("p (g s) -> p g s", g=4), AX.X, ALU.max) \
                    .then_inc(s_("max_done"), 1)

            def split_max(b):
                dve.wait_ge(s_("max_done"), NSLOT * (b + 1))
                if b >= 1:
                    dve.wait_ge(s_("mT_mm"), b)
                m = mx[par(b)][:, :, :]
                link(ts(nm[:, :, 0, :], m, -1.0, None, ALU.mult))
                link(stt(mr[:, :, :], m, -1.0, nm[:, :, 0, :], ALU.mult, ALU.subtract))
                link(dve.tensor_copy(nm[:, :, 1, :], mr[:, :, :]))
                tt(nm[:, :, 2, :], mr[:, :, :], nm[:, :, 1, :], ALU.subtract).then_inc(s_("nm_done"), 1)

            def normalise(b):
                dve.wait_ge(s_("pv_mm"), NSLOT * (b + 1))
                dve.transpose(ot[:, :, :].rearrange("p a c -> p (a c)"), od).then_inc(s_("od_read"), 1)
                dve.wait_ge(s_("od_read"), b + 1)
                link(dve.reciprocal(rden[:, :, :], ot[:, :, 16:18]))
                link(tt(on[:, :, 0:16].rearrange("p a (j d) -> p a j d", j=2),
                        ot[:, :, 0:16].rearrange("p a (j d) -> p a j d", j=2),
                        rden[:, :, :, None].to_broadcast([P, 16, 2, DH]), ALU.mult))
                if b >= 1:
                    dve.wait_ge(s_("wp_mm"), b)
                dve.transpose(odn[:, :], on[:, :, :].rearrange("p a c -> p (a c)")).then_inc(s_("odn_done"), 1)

            def norm2(b):
                dve.wait_ge(s_("wp_mm"), b + 1)
                tt(u1[:, :, :], gb[:, 0:S].rearrange("p (t n) -> p t n", t=NT),
                   brow[:, None, D:2 * D].to_broadcast([P, NT, D]), ALU.add).then_inc(s_("u1_done"), 1)
                dve.wait_ge(s_("u1_done"), b + 1)
                for t in range(NT):
                    at = keep(stt(x2p[:, t, :], u1[:, t, :], tmask[:, b * NT + t:b * NT + t + 1], xres[:, b, t, :],
                                  ALU.mult, ALU.add))
                need(at)
                norm_stats(x2p, st6b, mvb, "mv2")

            def norm2_end(b):
                dve.wait_ge(s_("rstd2"), b + 1)
                for t in range(NT):
                    ts(x2[:, b, t, :], x2p[:, t, :], mvb[:, t, 0:1], rstdb[:, t:t + 1], ALU.subtract, ALU.mult) \
                        .then_inc(s_("x2_done"), 1)

            def route(b):
                dve.wait_ge(s_("lg_mm"), b + 1)
                ts(lg[:, :, :], gb[:, 0:NT * E].rearrange("p (t e) -> p t e", t=NT), CLAMP, -CLAMP, ALU.min, ALU.max) \
                    .then_inc(s_("lg_done"), 1)
                dve.wait_ge(s_("lg_done"), b + 1)
                for t in range(NT):
                    at = keep(dve.max(v8[:, t, :], lg[:, t, :]))
                need(at)
                if b >= 1:
                    dve.wait_ge(s_("w_all"), b)
                tt(dv[:, :], v8[:, :, 1], v8[:, :, 0], ALU.subtract).then_inc(s_("dv_done"), 1)
                for t in range(NT):
                    at = keep(dve.max_index(i8[:, t, :], v8[:, t, :], lg[:, t, :]))
                need(at)
                link(dve.tensor_copy(idf[:, :, :], i8[:, :, 0:K]))
                link(tt(oh[:, :, :, :].rearrange("p t k e -> p (t k) e"),
                        cn[:, C_IOTA:C_IOTA + 32].rearrange("p (a e) -> p a e", e=E),
                        idf[:, :, :].rearrange("p t k -> p (t k)")[:, :, None].to_broadcast([P, NT * K, E]),
                        ALU.is_equal))
                if b >= 1:
                    dve.wait_ge(s_("pos_mm"), b)
                tt(ohs[:, :, :], oh[:, :, 0, :], oh[:, :, 1, :], ALU.add).then_inc(s_("ohs_done"), 1)

            def place(b):
                dve.wait_ge(s_("pos_mm"), b + 1)
                for t in range(NT):
                    at = tt(pm[:, t * K:(t + 1) * K, :], gb[:, None, t * E:(t + 1) * E].to_broadcast([P, K, E]),
                            oh[:, t, :, :], ALU.mult)
                at.then_inc(s_("pm_done"), 1)
                dve.wait_ge(s_("pm_done"), b + 1)
                link(dve.tensor_reduce(pos[:, :], pm[:, :, :], AX.X, ALU.add))
                keep(ts(over[:, :], pos[:, :], float(CAP), FAR, ALU.is_ge, ALU.mult))
                link(stt(slf[:, :], idf[:, :, :].rearrange("p t k -> p (t k)"), float(CAP), pos[:, :],
                         ALU.mult, ALU.add))
                if b >= 2:
                    dve.wait_ge(s_(f"rows_out{par(b)}"), 16 * NT * K * (b // 2))
                tt(slot[par(b)][:, :], slf[:, :], over[:, :], ALU.add).then_inc(s_("slot_done"), 1)
                dve.wait_ge(s_("ev_done"), b + 1)
                link(ts(ev1[:, :], ev[:, :], 1.0, 1e-12, ALU.add, ALU.add))
                link(dve.reciprocal(ev1[:, :], ev1[:, :]))
                dve.tensor_copy(xp[par(b)][:, :, 0, D], ev1[:, :])
                tt(xp[par(b)][:, :, 1, D], ev[:, :], ev1[:, :], ALU.mult).then_inc(s_("w_all"), 1)

            for n in range(NSLOT * (NB + 3)):
                b, k = divmod(n, NSLOT)
                if k == 0 and 0 <= b - 1 < NB:
                    split_max(b - 1)
                if k == 1 and 0 <= b - 3 < NB:
                    norm2_end(b - 3)
                if n < NSLOT * NB:
                    row_max(n)
                if k == 5 and 0 <= b - 2 < NB:
                    normalise(b - 2)
                if k == 7 and 0 <= b - 2 < NB:
                    norm2(b - 2)
                if k == 4 and 0 <= b - 3 < NB:
                    route(b - 3)
                if k == 6 and 0 <= b - 3 < NB:
                    place(b - 3)

            def hid_mul(n):
                e, r = divmod(n, 2 * FT)
                f, half = divmod(r, 2)
                dve.wait_ge(s_("silu_done"), n + 1)
                if r == 0 and e >= 2:
                    dve.wait_ge(s_("ye_mm"), CT * (e - 1))
                tt(hid[par(e)][:, f, half * HALF:(half + 1) * HALF], sil[n % 2], pairs[n % 2][:, 512:512 + HALF],
                   ALU.mult).then_inc(s_("hid_done"), 1)

            def take_y(e):
                for c in range(CT):
                    dve.wait_ge(s_("ye_mm"), CT * e + (4 if c < 4 else CT))
                    if c == 0 and e >= 2:
                        dve.wait_ge(s_(f"ye_out{par(e)}"), 16 * CT * (e // 2))
                    ts(ye[par(e)][:, c, :], pairs[2][:, c * P:(c + 1) * P], xe[par(e)][:, c, D:D + 1], None, ALU.mult) \
                        .then_inc(s_("ye_ev"), 1)

            for e in range(E):
                for r in range(2 * FT):
                    hid_mul(e * 2 * FT + r)
                    if r == 1 and e >= 1:
                        take_y(e - 1)
            take_y(E - 1)

            for c in range(4):
                dve.wait_ge(s_(f"y_in{par(c)}"), 32 * (c // 2 + 1))
                if c >= 2:
                    dve.wait_ge(s_(f"out_done{par(c)}"), 16)
                tt(fin[par(c)][:, :, :], yl[par(c)][0][:, :, :], yl[par(c)][1][:, :, :], ALU.add).then_inc(s_("y_sum"), 1)
                dve.wait_ge(s_("y_sum"), c + 1)
                link(tt(fin[par(c)][:, :, :], fin[par(c)][:, :, :],
                        x2[:, 2 * c:2 * c + 2].rearrange("p b t d -> p (b t) d"), ALU.add))
                for t in range(4):
                    at = keep(dve.bn_stats(st6d[:, 4 * c + t, :], fin[par(c)][:, t, :]))
                need(at)
                for t in range(4):
                    dve.bn_aggr(mvd[:, 4 * c + t, :], st6d[:, 4 * c + t, :]).then_inc(s_("mv3"), 1)
                dve.wait_ge(s_("rstd3"), c + 1)
                for t in range(4):
                    ts(fin[par(c)][:, t, :], fin[par(c)][:, t, :], mvd[:, 4 * c + t, 0:1],
                       rstdd[:, 4 * c + t:4 * c + t + 1], ALU.subtract, ALU.mult).then_inc(s_("fin_done"), 1)

        @block.gpsimd
        def _(pool):
            tt, ts = pool.tensor_tensor, pool.tensor_scalar

            def copy(out, src):
                return ts(out, src, 1.0, 0.0, ALU.mult, ALU.add)

            pool.memset(zrow[:, :], 0.0).then_inc(s_("zrow_set"), 1)
            pool.wait_ge(s_("zrow_set"), 1)
            pool.memset(zrow[:, :].rearrange("p (r n) -> p r n", r=4)[:, :, D + 1].bitcast(U32), NOWHERE) \
                .then_inc(s_("zrow_set"), 1)
            pool.memset(halfs[:, :], -0.5).then_inc(s_("halfs_set"), 1)
            pool.memset(minus1[:, :], -1.0).then_inc(s_("halfs_set"), 1)
            for i in range(QK_BUFS):
                for tile in (qb[i], kb[i]):
                    pool.memset(tile[:, :, :].rearrange("p h s -> p (h s)").bitcast(U32), 0) \
                        .then_inc(s_("qk_cleared"), 1)
            for i in range(2):
                pool.memset(vp[i][:, :, :, :], 0.0).then_inc(s_("vp_const"), 1)
            pool.wait_ge(s_("vp_const"), 2)
            for i in range(2):
                for j in range(2):
                    pool.memset(vp[i][:, :, :, :].rearrange("p c (u j g) n -> p (c u) j g n", u=2, j=2)
                                [:, :, j, :, 16 + j:17 + j], 1.0).then_inc(s_("vp_const"), 1)
            pool.wait_ge(s_("halfs_set"), 1)

            def rsqrt(b, count, dst_v, mvt, dst, sem_mv, name, at, n):
                pool.wait_ge(s_(sem_mv), count)
                ts(dst_v, mvt, EPS, None, ALU.add).then_inc(s_("var_eps"), 1)
                at[0] += 1
                pool.wait_ge(s_("var_eps"), at[0])
                tt(dst, dst_v, halfs[:, 0:n], ALU.pow).then_inc(s_(name), 1)

            at = [0]

            for i in A_STEPS:
                f, r = i + 2, i - LAG
                if 0 <= f < NB:
                    pool.wait_ge(s_("t4"), f + 1)
                    tt(fl(f, 6), fl(f, 2), fl(f, 4), ALU.mult).then_inc(s_("f_pool"), 1)
                    pool.wait_ge(s_("f8"), f + 1)
                    tt(fl(f, 10), fl(f, 2), fl(f, 8), ALU.mult).then_inc(s_("f_pool"), 1)
                if 0 <= i < NB:
                    rsqrt(i, NT * (i + 1), ve[:, :], mv[:, :, 1], rstd[:, :], "mv1", "rstd1", at, NT)
                if 0 <= r < NB:
                    pool.wait_ge(s_("rope_mul"), 4 * (r + 1))
                    tt(rsum[:, :, :], rc[:, :, :], rs[:, :, :], ALU.add).then_inc(s_("rope_sum"), 1)
                    pool.wait_ge(s_("rope_hi"), r + 1)
                    tt(rr[:, :, :], rsum[:, :, :], parts[par(r)][:, 0], ALU.subtract).then_inc(s_("rope_r"), 1)
                    pool.wait_ge(s_("rope_mid"), r + 1)
                    tt(parts[par(r)][:, 2], rr[:, :, :], parts[par(r)][:, 1], ALU.subtract).then_inc(s_("rope_lo"), 1)

            pool.wait_ge(s_("xe_cleared"), 16 * (NROWS // (4 * P)))
            for n in range(NSLOT * (NB + 3)):
                b, k = divmod(n, NSLOT)
                if k == 0 and 0 <= b < NB:
                    pool.wait_ge(s_("v2_ev"), b + 1)
                    if b == 0:
                        pool.wait_ge(s_("vp_const"), 6)
                    if b >= 2:
                        pool.wait_ge(s_("pv_mm"), NSLOT * (b - 1))
                    src = v2[:, b].rearrange("p c (u j g d) -> p (c u) j g d", u=2, j=2, g=4)
                    dst = vp[par(b)][:, :, :, :].rearrange("p c (u j g) n -> p (c u) j g n", u=2, j=2)
                    for j in range(2):
                        copy(dst[:, :, j, :, DH * j:DH * j + DH], src[:, :, j]).then_inc(s_("vp_set"), 1)
                if k == 7 and 0 <= b - 2 < NB:
                    c = b - 2
                    rsqrt(c, NT * (c + 1), veb[:, :], mvb[:, :, 1], rstdb[:, :], "mv2", "rstd2", at, NT)
                if k == 1 and 0 <= b - 3 < NB:
                    c = b - 3
                    pool.wait_ge(s_("x2_done"), NT * (c + 1))
                    if c >= 2:
                        pool.wait_ge(s_(f"rows_out{par(c)}"), 16 * NT * K * (c // 2))
                    for k_ in range(K):
                        copy(xp[par(c)][:, :, k_, 0:D], x2[:, c]).then_inc(s_("xp_set"), 1)
                    pool.tensor_copy(xp[par(c)][:, :, :, D + 1].bitcast(U32), dest[:, c]).then_inc(s_("xp_set"), 1)
                if k == 4 and 0 <= b - 3 < NB:
                    c = b - 3
                    pool.wait_ge(s_("ohs_done"), c + 1)
                    if c == 0:
                        pool.wait_ge(s_("cnt_done"), 1)
                    tt(ohsum[:, :], ohs[:, 0, :], ohs[:, 1, :], ALU.add).then_inc(s_("ohsum"), 1)
                    pool.wait_ge(s_("ohsum"), c + 1)
                    if c >= 1:
                        pool.wait_ge(s_("pos_mm"), c)
                    tt(cnt[par(c + 1)][:, :], cnt[par(c)][:, :], ohsum[:, :], ALU.add).then_inc(s_("cnt_next"), 1)
                if k == 6 and 0 <= b - 3 < NB:
                    c = b - 3
                    pool.wait_ge(s_("slot_done"), c + 1)
                    pool.wait_ge(s_("w_all"), c + 1)
                    pool.wait_ge(s_("xp_set"), 3 * (c + 1))
                    for t in range(NT):
                        for k_ in range(K):
                            pool.indirect_dma_start(
                                out=xe_d, out_offset=bass.IndirectOffsetOnAxis(ap=slot[par(c)][:, t * K + k_:t * K + k_ + 1], axis=0),
                                in_=xp[par(c)][:, t, k_, :], in_offset=None, bounds_check=NROWS - 1, oob_is_err=False) \
                                .then_inc(s_(f"rows_out{par(c)}"), 16)

            pool.wait_ge(s_("y_cleared"), 16 * (K * T // (4 * P)))
            for e in range(E):
                for c in range(CT):
                    pool.wait_ge(s_("ye_ev"), CT * e + c + 1)
                    pool.indirect_dma_start(
                        out=yb_d, out_offset=bass.IndirectOffsetOnAxis(ap=xe[par(e)][:, c, D + 1:D + 2].bitcast(U32), axis=0),
                        in_=ye[par(e)][:, c, :], in_offset=None, bounds_check=K * T - 1, oob_is_err=False) \
                        .then_inc(s_(f"ye_out{par(e)}"), 16)

            for c in range(4):
                rsqrt(c, 4 * (c + 1), ved[:, 4 * c:4 * c + 4], mvd[:, 4 * c:4 * c + 4, 1], rstdd[:, 4 * c:4 * c + 4],
                      "mv3", "rstd3", at, 4)


def kernel(**inputs):
    import numpy as _np
    import concourse.bacc as _bacc
    from concourse import mybir as _mybir
    from concourse.bass_utils import run_bass_kernel_spmd as _run

    a = {k: _np.asarray(v) for k, v in inputs.items()}
    swap = _np.arange(D).reshape(H, 2, DH // 2)[:, ::-1].reshape(-1)
    wq, wk = a["L0_xattn_Wq"], a["L0_xattn_Wk"]
    wp_t = a["L0_xattn_Wp"].T
    wp_rows = _np.zeros((2, 4, 32, D), wp_t.dtype)
    wp_rows[:, :, 0:2 * DH] = wp_t.reshape(2, 2, 4, DH, D).transpose(0, 2, 1, 3, 4).reshape(2, 4, 2 * DH, D)
    w_in_t = a["L0_attn_w_in"].T
    wa = _np.concatenate([w_in_t, a["L0_attn_w_out"].T, wq.T, wq[swap].T, wk.T, wk[swap].T,
                          a["L0_xattn_Wv"].T, wp_rows[0].reshape(P, D), wp_rows[1].reshape(P, D)], axis=1)
    bq, bk = a["L0_xattn_bq"], a["L0_xattn_bk"]
    bias = _np.stack([bq, bk, bq[swap], bk[swap]], axis=1)
    brow = _np.broadcast_to(_np.concatenate([a["L0_xattn_bv"], a["L0_xattn_bp"]])[None], (P, 2 * D))
    mask = a["mask_BxS2_bf1"].view(_np.uint8)
    const, dest = constants()
    ones_zeros = _np.zeros((6, H * S), _mybir.dt.np(_mybir.dt.bfloat16))
    ones_zeros[0:3] = 1
    arrays = {
        "x": a["x"].reshape(T, D), "ctx": a["ctx_1024"].reshape(T, D), "mrow": mask,
        "mcol": mask.reshape(NB * NT, P).T, "beta": _np.repeat(a["L0_attn_beta"], DH, axis=0), "wa": wa,
        "bias": bias, "brow": brow, "wr": a["L0_ffn_Wr"], "w1": a["L0_ffn_W1"], "w3": a["L0_ffn_W3"],
        "w2": a["L0_ffn_W2"], "const": const, "dest": dest, "rows": ones_zeros,
    }
    arrays = {f"in_{k}": _np.ascontiguousarray(v) for k, v in arrays.items()}
    nc = _bacc.Bacc("TRN2", target_bir_lowering=False, num_devices=1)
    args = [nc.dram_tensor(k, v.shape, _mybir.dt.from_np(v.dtype), kind="ExternalInput").ap() for k, v in arrays.items()]
    out = nc.dram_tensor("out", (T, D), F32, kind="ExternalOutput").ap()
    build(nc, *args, out)
    r = _run(nc, [arrays], core_ids=[0])
    return r.results[0]["out"].reshape(NB, S, D)
```

```python
from contextlib import ExitStack

import numpy as np

import concourse.bass as bass
from concourse import mybir

ALU = mybir.AluOpType
ACT = mybir.ActivationFunctionType
AX = mybir.AxisListType
F32 = mybir.dt.float32
BF16 = mybir.dt.bfloat16
U32 = mybir.dt.uint32
U8 = mybir.dt.uint8

P = 128
NB, S, D = 8, 256, 128
T = NB * S
NT = S // P
H, DH = 16, 8
M = 11
SC = float(np.float32(DH ** -0.5))
E, K, F = 8, 2, 512
CAP = 640
CT = CAP // P
FT = F // P
HALF = CAP // 2
ROW = D + 2
NROWS = E * CAP
EPS = 1e-5
CLAMP = 10000.0
FAR = 1.0e6
NOWHERE = 1 << 20
MASKED = 1.0e30
BIAS_COL = 2 * DH
E_LAG = 12
NSLOT = 8
QK_BUFS = 3
E_BUFS = 3
DC = 4
DT = T // P // DC
X_BUFS = 4
R2 = float(np.sqrt(2.0))
PRODS = 6
Q_PUT = ((0, 0, 3, 1), (1, 3, 5, 1), (2, 5, 6, 1))
K_PUT = ((0, 0, 5, 4), (0, 5, 6, 1), (2, 1, 2, 1), (1, 2, 4, 1))
PUTS = 16 * (len(Q_PUT) + len(K_PUT))
MASK_ROW = PRODS * DH
MAX_ROW = MASK_ROW + 1

C_ID, C_COS, C_SIN, C_TRI, C_BLK, C_SGN, C_IOTA, C_SGNC = 0, 128, 384, 640, 768, 800, 928, 960
NCONST = 961
W_Q, W_KV, W_O, W_XQ, W_XQR, W_XK, W_XKR, W_XV, W_XP = (128 * i for i in (0, 1, 3, 4, 5, 6, 7, 8, 9))
NWA = 128 * 11


def constants():
    c = np.zeros((P, NCONST), np.float32)
    p = np.arange(P)
    c[:, C_ID:C_ID + P] = np.eye(P)
    inv = (1.0 / np.float32(10000.0) ** (np.arange(0, DH, 2, dtype=np.float32) / np.float32(DH))).astype(np.float32)
    fr = np.outer(np.arange(S, dtype=np.float32), inv).astype(np.float32)
    ang = np.concatenate([fr, fr], axis=1).T[p % DH]
    c[:, C_COS:C_COS + S] = np.cos(ang.astype(np.float64))
    c[:, C_SIN:C_SIN + S] = np.sin(ang.astype(np.float64))
    c[:, C_TRI:C_TRI + P] = p[:, None] < p[None, :]
    c[:, C_BLK:C_BLK + 32] = (p[:, None] % 32) // DH == np.arange(32)[None, :] // DH
    c[:, C_SGN:C_SGN + P] = np.where(p % DH < DH // 2, -1.0, 1.0)[None, :]
    c[:, C_IOTA:C_IOTA + 32] = np.arange(32)[None, :] % E
    c[:, C_SGNC] = np.where(p % DH < DH // 2, -1.0, 1.0)
    b, t, k = np.meshgrid(np.arange(NB), np.arange(NT), np.arange(K), indexing="ij")
    dest = (k * T + b * S + t * P)[None] + p[:, None, None, None]
    return c, dest.reshape(P, -1).astype(np.uint32)


def build(nc, x_d, ctx_d, mrow_d, mcol_d, beta_d, wa_d, bias_d, brow_d, wr_d, w1_d, w3_d, w2_d, const_d, dest_d,
          rows_d, out_d):
    ctx = ExitStack()
    with ctx:
        def sb(name, shape, dt=F32):
            return ctx.enter_context(nc.sbuf_tensor(name, shape, dt))

        def sem(name):
            return ctx.enter_context(nc.semaphore(name))

        def dram(name, shape, dt=F32):
            return nc.dram_tensor(name, shape, dt, kind="Internal").ap()

        packed_d = dram("packed_scratch", [NB, 2, H * DH, PRODS, S], BF16)
        xe_d = dram("xe_scratch", [NROWS, ROW])
        yb_d = dram("y_scratch", [K * T, D])

        banks = [ctx.enter_context(nc.psum_tensor(f"bank{i}", [P, 512], F32)) for i in range(2)]
        pairs = [ctx.enter_context(nc.psum_tensor(f"pair{i}", [P, 1024], F32)) for i in range(3)]
        BK = [banks[0][:, :], banks[1][:, :]] + [pairs[i // 2][:, 512 * (i % 2):512 * (i % 2) + 512] for i in range(6)]

        cn = sb("cn", [P, NCONST])
        wa = sb("wa", [P, NWA])
        wr = sb("wr", [P, E])
        bias = sb("bias", [P, 4])
        brow = sb("brow", [P, D])
        betas = sb("betas", [P, M])
        bm = sb("bm", [P, M, 32])
        mrow8 = sb("mrow8", [NB, S], U8)
        maskb = sb("maskb", [NB, S], BF16)
        mcol8 = sb("mcol8", [P, NB * NT], U8)
        tmask = sb("tmask", [P, NB * NT])
        dest = sb("dest", [P, NB, NT, K], U32)
        idb = sb("idb", [P, P], BF16)
        trib = sb("trib", [P, P], BF16)
        onesb = sb("onesb", [P, P], BF16)
        halfs = sb("halfs", [P, 16])
        minus1 = sb("minus1", [P, 1])
        zrow = sb("zrow", [P, 4 * ROW])
        ident = cn[:, C_ID:C_ID + P]

        xin = [sb(f"xin{i}", [P, NT, D]) for i in range(X_BUFS)]
        xres = sb("xres", [P, NB, NT, D])
        cin = [sb(f"cin{i}", [P, NT, D]) for i in range(2)]
        xT = sb("xT", [P, S])
        cT = sb("cT", [P, S])
        x1T = sb("x1T", [P, S])
        feat = [sb(f"feat{i}", [P, M, 2, S]) for i in range(2)]
        sq = sb("sq", [P, 2, 2 * S])
        val = [sb(f"val{i}", [P, NT, D]) for i in range(2)]
        kvt = sb("kvt", [P, M, 32])
        wq_ = sb("wcomb", [P, M, 32])
        tmp32 = sb("tmp32", [P, 3, 32])
        wbd = [sb(f"wbd{i}", [P, M, P]) for i in range(2)]
        oT = sb("oT", [P, S])
        ypre = sb("ypre", [P, NT, D])
        st6 = sb("st6", [P, NT, 6])
        mv = sb("mv", [P, NT, 2])
        ve = sb("ve", [P, NT])
        rstd = sb("rstd", [P, NT])
        v2 = sb("v2", [P, NB, NT, D])
        rc = sb("rc", [P, 2, S])
        rs = sb("rs", [P, 2, S])
        rsum = sb("rsum", [P, 2, S])
        rr = sb("rr", [P, 2, S])
        parts = [sb(f"parts{i}", [P, 3, 2, S], BF16) for i in range(2)]

        qb = [sb(f"qb{i}", [P, H, S], BF16) for i in range(QK_BUFS)]
        kb = [sb(f"kb{i}", [P, H, S], BF16) for i in range(QK_BUFS)]
        mx = [sb(f"mx{i}", [P, NT, H]) for i in range(2)]
        mr = sb("mr", [P, NT, H])
        nm = sb("nm", [P, NT, 3, H], BF16)
        mT = [sb(f"mT{i}", [3 * H, S], BF16) for i in range(2)]
        pr = [sq[:, :, :].rearrange("p a (g s) -> p (a g) s", g=2), sb("pr1", [P, 4, S])]
        vp = [sb(f"vp{i}", [P, NT, H, 32]) for i in range(2)]
        ot = sb("ot", [P, 16, 32])
        on = sb("on", [P, 16, 32])
        rden = sb("rden", [P, 16, 2])
        odn = sb("odn", [P, 512])
        shift2 = sb("shift2", [P, NT])
        x2p = sb("x2p", [P, NT, D])
        st6b = sb("st6b", [P, NT, 6])
        mvb = sb("mvb", [P, NT, 2])
        veb = sb("veb", [P, NT])
        rstdb = sb("rstdb", [P, NT])
        x2 = sb("x2", [P, NB, NT, D])
        x2T = sb("x2T", [P, S])
        lg = sb("lg", [P, NT, E])
        v8 = sb("v8", [P, NT, 8])
        i8 = sb("i8", [P, NT, 8], U32)
        idf = sb("idf", [P, NT, K])
        oh = sb("oh", [P, NT, K, E])
        ohs = sb("ohs", [P, NT, E], BF16)
        cnt = [sb(f"cnt{i}", [P, E], BF16) for i in range(2)]
        ohsum = sb("ohsum", [P, E], BF16)
        dv = sb("dv", [P, NT])
        ev = sb("ev", [P, NT])
        ev1 = sb("ev1", [P, NT])
        pm = sb("pm", [P, NT * K, E])
        pos = sb("pos", [P, NT * K])
        over = sb("over", [P, NT * K])
        slf = sb("slf", [P, NT * K])
        slot = [sb(f"slot{i}", [P, NT * K], U32) for i in range(2)]
        xp = [sb(f"xp{i}", [P, NT, K, ROW]) for i in range(2)]

        def carve(tile, at, n):
            return tile[:, :, :, :].rearrange("p a b c -> p (a b c)")[:, at:at + n]

        def half_words(tile):
            return tile[:, :, :].rearrange("p h s -> p (h s)").bitcast(F32)

        xe = [carve(feat[i], 0, CT * ROW) for i in range(2)] + [half_words(qb[2])[:, 0:CT * ROW]]
        xe = [t.rearrange("p (c r) -> p c r", c=CT) for t in xe]
        xeT = [carve(feat[i], 700, CAP) for i in range(2)]
        hid = [carve(feat[i], 1400, FT * CAP).rearrange("p (f c) -> p f c", f=FT) for i in range(2)]
        ye = [carve(feat[i], 4000, CT * D).rearrange("p (c d) -> p c d", c=CT) for i in range(2)]
        sil = [carve(feat[i], 4700, HALF) for i in range(2)]
        w1 = [wbd[i][:, 0:4, :].rearrange("p m n -> p (m n)") for i in range(2)] + [half_words(kb[2])[:, 0:F]]
        w3 = [wbd[i][:, 4:8, :].rearrange("p m n -> p (m n)") for i in range(2)] + [half_words(kb[2])[:, F:2 * F]]
        w2 = [carve(feat[i], 5100, F) for i in range(2)] + [half_words(kb[2])[:, 2 * F:3 * F]]
        w2 = [t.rearrange("p (f d) -> p f d", f=FT) for t in w2]

        def spare(tile, at):
            return half_words(tile)[:, at * DT * D:(at + 1) * DT * D].rearrange("p (t d) -> p t d", d=D)
        yl = [[spare(qb[k], c) for k in range(K)] for c in range(DC)]
        fin = [spare(kb[0], c) for c in range(DC)]
        shift = sb("shift", [P, T // P])
        st6d = sb("st6d", [P, 16, 6])
        mvd = sb("mvd", [P, 16, 2])
        ved = sb("ved", [P, 16])
        rstdd = sb("rstdd", [P, 16])

        PRE = {NB: 2, NB + 1: 2}
        PRE_N = sum(PRE.values())
        assert PRE_N % 2 == 0 and PRE_N <= NSLOT

        def pre_slots(i):
            first = sum(v for k, v in PRE.items() if k < i)
            return range(first, first + PRE.get(i, 0))

        def m_pair(n):
            return 1 if n < PRE_N else n % 2

        def e_pair(n):
            return 0 if n + E_LAG >= NSLOT * NB and n % 2 else 2

        def before(pair, n):
            return max([j + 1 for j in range(n) if pair(j) == pair(n)], default=0)

        names = {}

        def s_(name):
            if name not in names:
                names[name] = sem(name)
            return names[name]

        par = lambda b: b % 2

        def fl(b, m):
            return feat[par(b)][:, m].rearrange("p a s -> p (a s)")

        LAG = 2
        A_STEPS = range(-3, NB + LAG)

        block = ctx.enter_context(nc.Block())

        @block.sync
        def _(sp):
            def load_x(b):
                if b >= X_BUFS:
                    sp.wait_ge(s_("x1_sum"), b - X_BUFS + 1)
                sp.dma_start(xin[b % X_BUFS][:, :, :], x_d[b * S:(b + 1) * S, :].rearrange("(t p) d -> p t d", p=P)) \
                    .then_inc(s_(f"x_in{b % X_BUFS}"), 16)

            def load_c(b):
                if b >= 2:
                    sp.wait_ge(s_("cT_mm"), b - 1)
                sp.dma_start(cin[par(b)][:, :, :], ctx_d[b * S:(b + 1) * S, :].rearrange("(t p) d -> p t d", p=P)) \
                    .then_inc(s_(f"c_in{par(b)}"), 16)

            def store_parts(b):
                sp.wait_ge(s_("rope_hi"), b + 1)
                sp.wait_ge(s_("rope_mid"), b + 1)
                sp.wait_ge(s_("rope_lo"), b + 1)
                for w, puts in enumerate((Q_PUT, K_PUT)):
                    for part, first, end, step in puts:
                        dst = packed_d[b, w, :, first:end:step, :]
                        sp.dma_start(dst, parts[par(b)][:, part, w, None, :].to_broadcast(list(dst.shape))) \
                            .then_inc(s_(f"parts_out{par(b)}"), 16)

            def pack(b):
                qd, kd = qb[b % QK_BUFS], kb[b % QK_BUFS]
                if b == 0:
                    sp.wait_ge(s_("qk_rows"), 32 * QK_BUFS)
                    sp.wait_ge(s_("maskb_set"), 1)
                if b >= QK_BUFS:
                    sp.wait_ge(s_("e_mm"), NSLOT * (b - QK_BUFS + 1))
                sp.wait_ge(s_(f"parts_out{par(b)}"), PUTS * (b // 2 + 1))
                for w, dst in enumerate((qd, kd)):
                    src = packed_d[b, w].rearrange("(h d) r s -> h (d r) s", d=DH).rearrange("h p s -> p h s")
                    sp.dma_start(dst[0:MASK_ROW, :, :], src).then_inc(s_(f"packed{b % QK_BUFS}"), 16)
                sp.dma_start(qd[MAX_ROW:MAX_ROW + 3, :, :].rearrange("p h s -> p (h s)"), rows_d[3:6, :]) \
                    .then_inc(s_(f"packed{b % QK_BUFS}"), 16)
                sp.dma_start(kd[MASK_ROW:MASK_ROW + 1, :, :], maskb[b:b + 1, None, :].to_broadcast([1, H, S])) \
                    .then_inc(s_(f"packed{b % QK_BUFS}"), 16)

            load_x(0)
            sp.dma_start(cn[:, :], const_d).then_inc(s_("const_in"), 16)
            sp.dma_start(wa[:, :], wa_d).then_inc(s_("wa_in"), 16)
            load_x(1)
            for tile, src in ((bias, bias_d), (brow, brow_d), (betas, beta_d), (mrow8, mrow_d), (mcol8, mcol_d),
                              (wr, wr_d)):
                sp.dma_start(tile[:, :], src).then_inc(s_("small_in"), 16)
            sp.dma_start(dest[:, :, :, :].rearrange("p b t k -> p (b t k)"), dest_d).then_inc(s_("small_in"), 16)
            load_x(2)
            load_x(3)
            load_c(0)
            load_c(1)
            sp.wait_ge(s_("zrow_set"), 2)
            for i in range(NROWS // (P * 4)):
                sp.dma_start(xe_d[i * 4 * P:(i + 1) * 4 * P, :].rearrange("(p r) n -> p (r n)", p=P), zrow[:, :]) \
                    .then_inc(s_("xe_cleared"), 16)
            for i in range(K * T // (P * 4)):
                sp.dma_start(yb_d[i * 4 * P:(i + 1) * 4 * P, :].rearrange("(p r) n -> p r n", p=P),
                             zrow[:, :].rearrange("p (r n) -> p r n", r=4)[:, :, 0:D]).then_inc(s_("y_cleared"), 16)
            sp.wait_ge(s_("qk_cleared"), 2 * QK_BUFS)
            for i in range(QK_BUFS):
                sp.dma_start(qb[i][MASK_ROW:MASK_ROW + 1, :, :].rearrange("p h s -> p (h s)"), rows_d[0:1, :]) \
                    .then_inc(s_("qk_rows"), 16)
                sp.dma_start(kb[i][MAX_ROW:MAX_ROW + 3, :, :].rearrange("p h s -> p (h s)"), rows_d[0:3, :]) \
                    .then_inc(s_("qk_rows"), 16)

            def put_max(b):
                sp.wait_ge(s_("mT_ev"), b + 1)
                sp.wait_ge(s_("m_mm"), NSLOT * (b + 1))
                for r in range(3):
                    sp.dma_start(qb[b % QK_BUFS][MAX_ROW + r:MAX_ROW + r + 1, :, :], mT[par(b)][H * r:H * r + H, :]) \
                        .then_inc(s_(f"max_put{b % QK_BUFS}"), 16)

            for i in A_STEPS:
                if 4 <= i + 4 < NB:
                    load_x(i + 4)
                if 2 <= i - LAG + 2 < NB:
                    load_c(i - LAG + 2)
                if 0 <= i - LAG < NB:
                    store_parts(i - LAG)
                if 0 <= i - LAG - 1 < QK_BUFS:
                    pack(i - LAG - 1)

            put_max(0)
            for b in range(NB):
                if b + 1 < NB:
                    put_max(b + 1)
                if b + QK_BUFS < NB:
                    pack(b + QK_BUFS)

            def load_w(e):
                if e == 2:
                    sp.wait_ge(s_("e_mm"), NSLOT * NB)
                if e >= E_BUFS:
                    sp.wait_ge(s_("ye_mm"), CT * (e - E_BUFS + 1))
                sm, i = s_(f"w_in{e % E_BUFS}"), e % E_BUFS
                sp.dma_start(w1[i], w1_d[e]).then_inc(sm, 16)
                sp.dma_start(w3[i], w3_d[e]).then_inc(sm, 16)
                sp.dma_start(w2[i][:, :, :], w2_d[e].rearrange("(f p) d -> p f d", p=P)).then_inc(sm, 16)

            def load_xe(e):
                if e >= E_BUFS:
                    sp.wait_ge(s_(f"ye_out{par(e - E_BUFS)}"), 16 * CT * ((e - E_BUFS) // 2 + 1))
                sp.dma_start(xe[e % E_BUFS], xe_d[e * CAP:(e + 1) * CAP, :].rearrange("(c p) r -> p c r", p=P)) \
                    .then_inc(s_(f"xe_in{e % E_BUFS}"), 16)

            for e in range(E_BUFS):
                load_w(e)
            sp.wait_ge(s_("rows_out0"), 8 * NB * NT * K)
            sp.wait_ge(s_("rows_out1"), 8 * NB * NT * K)
            for e in range(E_BUFS):
                load_xe(e)
            for e in range(E_BUFS, E):
                load_w(e)
                load_xe(e)
            sp.wait_ge(s_("ye_out0"), 8 * CT * E)
            sp.wait_ge(s_("ye_out1"), 8 * CT * E)
            for c in range(DC):
                for k in range(K):
                    r = k * T + c * DT * P
                    sp.dma_start(yl[c][k][:, :, :], yb_d[r:r + DT * P, :].rearrange("(t p) d -> p t d", p=P)) \
                        .then_inc(s_(f"y_in{c}"), 16)
            for c in range(DC):
                sp.wait_ge(s_("fin_done"), DT * (c + 1))
                sp.dma_start(out_d[c * DT * P:(c + 1) * DT * P, :].rearrange("(t p) d -> p t d", p=P), fin[c][:, :, :]) \
                    .then_inc(s_("out_done"), 16)
            sp.wait_ge(s_("out_done"), 16 * DC)
            sp.wait_ge(s_("xe_cleared"), 16 * (NROWS // (4 * P)))
            sp.wait_ge(s_("y_cleared"), 16 * (K * T // (4 * P)))

        @block.tensor
        def _(pe):
            b_T, b_Q, b_KV, b_V2, b_ST, b_O, b_R1, b_R2 = BK

            def mm(out, lhsT, rhs, start=True, stop=True):
                return pe.matmul(out, lhsT, rhs, start=start, stop=stop)

            def transposes(i):
                if 0 <= i + 3 < NB:
                    b = i + 3
                    pe.wait_ge(s_(f"x_in{b % X_BUFS}"), 16 * (b // X_BUFS + 1))
                    if b == 0:
                        pe.wait_ge(s_("const_in"), 16)
                    else:
                        pe.wait_ge(s_("xT_ev"), b)
                    if b >= 3 + LAG:
                        pe.wait_ge(s_("cT_ev"), b - 2 - LAG)
                    for t in range(NT):
                        ins = pe.transpose(b_T[:, t * P:(t + 1) * P], xin[b % X_BUFS][:, t, :], ident)
                    ins.then_inc(s_("xT_mm"), 1)
                if 0 <= i + 1 - LAG < NB:
                    b = i + 1 - LAG
                    pe.wait_ge(s_(f"c_in{par(b)}"), 16 * (b // 2 + 1))
                    pe.wait_ge(s_("xT_ev"), min(NB, b + LAG + 1))
                    if b >= 1:
                        pe.wait_ge(s_("cT_ev"), b)
                    for t in range(NT):
                        ins = pe.transpose(b_T[:, 256 + t * P:256 + (t + 1) * P], cin[par(b)][:, t, :], ident)
                    ins.then_inc(s_("cT_mm"), 1)

            def x1_transpose(i):
                if 0 <= i + 1 - LAG < NB:
                    b = i + 1 - LAG
                    pe.wait_ge(s_("x1_done"), NT * (b + 1))
                    pe.wait_ge(s_("y_clip"), 2 * min(NB, b + LAG + 2))
                    for t in range(NT):
                        ins = pe.transpose(b_Q[:, t * P:(t + 1) * P], xres[:, b, t, :], ident)
                    ins.then_inc(s_("x1T_mm"), 1)

            def out_features(b, ms):
                if ms[0] == 1:
                    pe.wait_ge(s_("wbd_set"), 4 * (b + 1))
                    if b >= 1:
                        pe.wait_ge(s_("oT_ev"), b)
                for m in ms:
                    ins = mm(b_O[:, 0:S], wbd[par(b)][:, m, :], feat[par(b)][:, m, 0, :], m == 1, m == 0)
                if ms[-1] == 0:
                    ins.then_inc(s_("out_mm"), 1)

            def key_value(b):
                pe.wait_ge(s_("f_dve"), 3 * (b + 1))
                pe.wait_ge(s_("f_pool"), 3 * (b + 1))
                pe.wait_ge(s_("f8"), b + 1)
                pe.wait_ge(s_("val_ev"), b + 1)
                if b >= 1:
                    pe.wait_ge(s_("kvt_ev"), b)
                for t in range(NT):
                    for g in range(4):
                        ins = mm(b_ST[32 * g:32 * g + 32, 0:32 * M].rearrange("p (j v) -> p j v", j=M),
                                 val[par(b)][:, t, 32 * g:32 * g + 32],
                                 feat[par(b)][:, :, 1, t * P + 32 * g:t * P + 32 * g + 32], t == 0, t == NT - 1)
                ins.then_inc(s_("kv_mm"), 1)

            def project(b):
                pe.wait_ge(s_("xT_ev"), b + 1)
                if b == 0:
                    pe.wait_ge(s_("wa_in"), 16)
                if b >= 2 + LAG:
                    pe.wait_ge(s_("x1T_ev"), b - 1 - LAG)
                if b >= 1:
                    pe.wait_ge(s_("y_clip"), 2 * b)
                    pe.wait_ge(s_("val_ev"), b)
                mm(b_Q[:, 0:S], wa[:, W_Q:W_Q + D], xT[:, :])
                for t in range(NT):
                    ins = mm(b_KV[:, t * 256:(t + 1) * 256], xT[:, t * P:(t + 1) * P], wa[:, W_KV:W_KV + 2 * D])
                ins.then_inc(s_("qkv_mm"), 1)

            def rope_project(b):
                pe.wait_ge(s_("cT_ev"), b + 1)
                pe.wait_ge(s_("x1_sum"), min(NB, b + LAG))
                if b == 0:
                    pe.wait_ge(s_("rot_signs"), 2)
                else:
                    pe.wait_ge(s_("v2_ev"), b)
                for t in range(NT):
                    ins = mm(b_V2[:, t * P:(t + 1) * P], cT[:, t * P:(t + 1) * P], wa[:, W_XV:W_XV + D])
                ins.then_inc(s_("v2_mm"), 1)
                if b >= 1:
                    pe.wait_ge(s_("rope_mul"), 4 * b)
                mm(b_R1[:, S:2 * S], wa[:, W_XK:W_XK + D], cT[:, :])
                mm(b_R2[:, S:2 * S], wa[:, W_XKR:W_XKR + D], cT[:, :])
                pe.wait_ge(s_("x1T_ev"), b + 1)
                mm(b_R1[:, 0:S], wa[:, W_XQ:W_XQ + D], x1T[:, :])
                mm(b_R2[:, 0:S], wa[:, W_XQR:W_XQR + D], x1T[:, :]).then_inc(s_("rope_mm"), 1)

            def out_project(b):
                pe.wait_ge(s_("oT_ev"), b + 1)
                if b >= 1:
                    pe.wait_ge(s_("x1_sum"), b)
                if b >= LAG:
                    pe.wait_ge(s_("v2_ev"), b - LAG + 1)
                for t in range(NT):
                    ins = mm(b_V2[:, t * P:(t + 1) * P], oT[:, t * P:(t + 1) * P], wa[:, W_O:W_O + D])
                ins.then_inc(s_("y_mm"), 1)

            def m_slot(n):
                b, k = divmod(n, NSLOT)
                c, hq = divmod(k, 4)
                if n == 0:
                    pe.wait_ge(s_("oT_ev"), NB)
                    pe.wait_ge(s_("kvt_ev"), NB)
                if n == PRE_N:
                    pe.wait_ge(s_("rope_mul"), 4 * NB)
                    pe.wait_ge(s_("v2_ev"), NB)
                    pe.wait_ge(s_("x1_sum"), NB)
                if k == 0:
                    pe.wait_ge(s_(f"packed{b % QK_BUFS}"), 16 * 4 * (b // QK_BUFS + 1))
                if before(m_pair, n):
                    pe.wait_ge(s_("max_done"), before(m_pair, n))
                for g in range(4):
                    h = 4 * hq + g
                    ins = mm(pairs[m_pair(n)][:, g * S:(g + 1) * S], qb[b % QK_BUFS][:, h, c * P:(c + 1) * P],
                             kb[b % QK_BUFS][:, h, :])
                ins.then_inc(s_("m_mm"), 1)

            for i in A_STEPS:
                if 0 <= i < NB:
                    out_features(i, [1, 2, 3, 4])
                if 0 <= i + 2 < NB:
                    project(i + 2)
                if 0 <= i + 1 < NB:
                    key_value(i + 1)
                if 0 <= i < NB:
                    out_features(i, [5, 6, 7, 8, 9, 10, 0])
                if 0 <= i - LAG < NB:
                    rope_project(i - LAG)
                transposes(i)
                x1_transpose(i)
                if 0 <= i < NB:
                    out_project(i)
                for n in pre_slots(i):
                    m_slot(n)

            od, gb = BK[0], BK[1]

            def max_transpose(b):
                pe.wait_ge(s_("nm_done"), b + 1)
                g_free(("mt", b))
                for c in range(NT):
                    ins = pe.transpose(gb[0:3 * H, :].bitcast(BF16)[:, c * P:(c + 1) * P],
                                       nm[:, c, :, :].rearrange("p r h -> p (r h)"), idb[:, :])
                ins.then_inc(s_("mT_mm"), 1)

            def e_slot(n):
                b, k = divmod(n, NSLOT)
                hq, kc = divmod(k, 2)
                if k == 0:
                    pe.wait_ge(s_(f"max_put{b % QK_BUFS}"), 48 * (b // QK_BUFS + 1))
                if before(e_pair, n):
                    pe.wait_ge(s_("exp_done"), before(e_pair, n))
                if e_pair(n) != 2:
                    pe.wait_ge(s_("max_done"), NSLOT * NB)
                for g in range(4):
                    h = 4 * hq + g
                    ins = mm(pairs[e_pair(n)][:, g * S:(g + 1) * S], kb[b % QK_BUFS][:, h, kc * P:(kc + 1) * P],
                             qb[b % QK_BUFS][:, h, :])
                ins.then_inc(s_("e_mm"), 1)

            def pv_slot(n):
                b, k = divmod(n, NSLOT)
                hq, kc = divmod(k, 2)
                tt, j = divmod(hq, 2)
                pe.wait_ge(s_("exp_done"), n + 1)
                if k == 0:
                    pe.wait_ge(s_("vp_set"), 2 * (b + 1))
                    if b >= 1:
                        pe.wait_ge(s_("od_read"), b)
                for g in range(4):
                    ins = mm(od[32 * g:32 * g + 32, tt * S:(tt + 1) * S], vp[par(b)][:, kc, 4 * hq + g, :],
                             pr[n % 2][:, g, :], j == 0 and kc == 0, j == 1 and kc == 1)
                ins.then_inc(s_("pv_mm"), 1)

            readers = {"mt": ("mT_ev", 1), "x2t": ("x2T_ev", 1), "log": ("lg_done", 1), "pos": ("pm_done", 1),
                       "wp": ("x2_sum", 1)}
            last = [None]

            def g_free(use):
                if last[0] is not None:
                    name, c = last[0]
                    pe.wait_ge(s_(readers[name][0]), readers[name][1] * (c + 1))
                last[0] = use

            def wp(b):
                pe.wait_ge(s_("odn_done"), b + 1)
                g_free(("wp", b))
                for t in range(NT):
                    for tt in range(2):
                        ins = mm(gb[:, t * P:(t + 1) * P], odn[:, tt * S + t * P:tt * S + (t + 1) * P],
                                 wa[:, W_XP + tt * D:W_XP + (tt + 1) * D], tt == 0, tt == 1)
                ins.then_inc(s_("wp_mm"), 1)

            def x2_transpose(b):
                pe.wait_ge(s_("x2_done"), NT * (b + 1))
                g_free(("x2t", b))
                for t in range(NT):
                    ins = pe.transpose(gb[:, t * P:(t + 1) * P], x2[:, b, t, :], ident)
                ins.then_inc(s_("x2T_mm"), 1)

            def logits(b):
                pe.wait_ge(s_("x2T_ev"), b + 1)
                g_free(("log", b))
                for t in range(NT):
                    ins = mm(gb[:, t * E:(t + 1) * E], x2T[:, t * P:(t + 1) * P], wr[:, :])
                ins.then_inc(s_("lg_mm"), 1)

            def positions(b):
                pe.wait_ge(s_("ohs_done"), b + 1)
                if b == 0:
                    pe.wait_ge(s_("cnt_done"), 1)
                else:
                    pe.wait_ge(s_("cnt_next"), b)
                g_free(("pos", b))
                for t in range(NT):
                    mm(gb[:, t * E:(t + 1) * E], trib[:, :], ohs[:, t, :], True, False)
                    if t == 1:
                        mm(gb[:, t * E:(t + 1) * E], onesb[:, :], ohs[:, 0, :], False, False)
                    ins = mm(gb[:, t * E:(t + 1) * E], onesb[:, :], cnt[par(b)][:, :], False, True)
                ins.then_inc(s_("pos_mm"), 1)

            for n in range(NSLOT * (NB + 3)):
                b, k = divmod(n, NSLOT)
                if PRE_N <= n < NSLOT * NB:
                    m_slot(n)
                if k == 7 and 0 <= b - 2 < NB:
                    wp(b - 2)
                if k == 1 and 0 <= b - 1 < NB:
                    max_transpose(b - 1)
                if 0 <= n - E_LAG < NSLOT * NB:
                    e_slot(n - E_LAG)
                if 0 <= n - E_LAG - 1 < NSLOT * NB:
                    pv_slot(n - E_LAG - 1)
                if k == 2 and 0 <= b - 3 < NB:
                    x2_transpose(b - 3)
                if k == 3 and 0 <= b - 3 < NB:
                    logits(b - 3)
                if k == 6 and 0 <= b - 3 < NB:
                    positions(b - 3)

            def xe_transpose(e):
                pe.wait_ge(s_(f"xe_in{e % E_BUFS}"), 16 * (e // E_BUFS + 1))
                if e == 0:
                    pe.wait_ge(s_("pm_done"), NB)
                else:
                    pe.wait_ge(s_("xeT_ev"), 2 * e)
                for c in range(CT):
                    ins = pe.transpose(BK[c // 4][:, (c % 4) * P:(c % 4 + 1) * P], xe[e % E_BUFS][:, c, 0:D], ident)
                    if c >= 3:
                        ins.then_inc(s_("xeT_mm"), 1)

            def hidden(n):
                e, k = divmod(n, 2 * FT)
                f, half = divmod(k, 2)
                if k == 0:
                    pe.wait_ge(s_(f"w_in{e % E_BUFS}"), 48 * (e // E_BUFS + 1))
                    pe.wait_ge(s_("xeT_ev"), 2 * (e + 1))
                if n >= 2:
                    pe.wait_ge(s_("hid_done"), n - 1)
                gu = pairs[n % 2]
                r = xeT[par(e)][:, half * HALF:(half + 1) * HALF]
                mm(gu[:, 0:HALF], w1[e % E_BUFS][:, f * P:(f + 1) * P], r)
                mm(gu[:, 512:512 + HALF], w3[e % E_BUFS][:, f * P:(f + 1) * P], r).then_inc(s_("gu_mm"), 1)

            def down(e, c):
                n = CT * e + c
                if c == 0:
                    pe.wait_ge(s_("hid_done"), 2 * FT * (e + 1))
                if n >= 2:
                    pe.wait_ge(s_("ye_ev"), n - 1)
                for f in range(FT):
                    ins = mm(BK[6 + n % 2][:, 0:P], hid[par(e)][:, f, c * P:(c + 1) * P], w2[e % E_BUFS][:, f, :],
                             f == 0, f == FT - 1)
                ins.then_inc(s_("ye_mm"), 1)

            xe_transpose(0)
            for e in range(E):
                for k in range(2 * FT):
                    hidden(2 * FT * e + k)
                    if e >= 1 and 1 <= k <= CT:
                        down(e - 1, k - 1)
                    if e + 1 < E and k == CT + 1:
                        xe_transpose(e + 1)
            for c in range(CT):
                down(E - 1, c)

        @block.scalar
        def _(act):
            b_T, b_Q, b_KV, b_V2, b_ST, b_O, b_R1, b_R2 = BK

            for i in A_STEPS:
                f, r = i + 2, i - LAG
                if 0 <= f < NB:
                    act.wait_ge(s_("qkv_mm"), f + 1)
                    act.wait_ge(s_("y_clip"), 2 * (f + 1))
                    act.activation(sq[:, 0, :], fl(f, 1), ACT.Square, scale=0.5).then_inc(s_("sq2"), 1)
                    act.copy(val[par(f)][:, :, :],
                             b_KV.rearrange("p (t k n) -> p t k n", t=NT, k=2)[:, :, 1, :]).then_inc(s_("val_ev"), 1)
                    act.wait_ge(s_("sq2"), f + 1)
                    if f == 0:
                        act.wait_ge(s_("halfs_set"), 2)
                    act.activation(fl(f, 2), sq[:, 0, :], ACT.Identity, bias=minus1[:, :]).then_inc(s_("t2"), 1)
                if 0 <= f < NB:
                    act.wait_ge(s_("t2"), f + 1)
                    act.activation(sq[:, 1, :], fl(f, 2), ACT.Square, scale=R2).then_inc(s_("sq4"), 1)
                if 0 <= f < NB:
                    act.wait_ge(s_("sq4"), f + 1)
                    act.activation(fl(f, 4), sq[:, 1, :], ACT.Identity, bias=minus1[:, :]).then_inc(s_("t4"), 1)
                if 0 <= i < NB:
                    act.wait_ge(s_("out_mm"), i + 1)
                    if i >= 1:
                        act.wait_ge(s_("y_mm"), i)
                    act.copy(oT[:, :], b_O[:, 0:S]).then_inc(s_("oT_ev"), 1)
                if 0 <= f < NB:
                    act.wait_ge(s_("t4"), f + 1)
                    act.activation(fl(f, 8), fl(f, 4), ACT.Square, scale=R2).then_inc(s_("f8"), 1)
                if 0 <= i + 1 < NB:
                    b = i + 1
                    act.wait_ge(s_("w_done"), b + 1)
                    for g in range(4):
                        act.copy(wbd[par(b)][32 * g:32 * g + 32, :, 32 * g:32 * g + 32], wq_[32 * g:32 * g + 32, :, :]) \
                            .then_inc(s_("wbd_set"), 1)
                if 0 <= i + 3 < NB:
                    b = i + 3
                    act.wait_ge(s_("xT_mm"), b + 1)
                    if b >= 2 + LAG:
                        act.wait_ge(s_("cT_mm"), b - 1 - LAG)
                    if b >= 1:
                        act.wait_ge(s_("qkv_mm"), b)
                    act.copy(xT[:, :], b_T[:, 0:S]).then_inc(s_("xT_ev"), 1)
                if 0 <= r + 1 < NB:
                    act.wait_ge(s_("cT_mm"), r + 2)
                    if r + 1 >= 1:
                        act.wait_ge(s_("rope_mm"), r + 1)
                    act.copy(cT[:, :], b_T[:, S:2 * S]).then_inc(s_("cT_ev"), 1)
                    act.wait_ge(s_("x1T_mm"), r + 2)
                    act.copy(x1T[:, :], b_Q[:, 0:S]).then_inc(s_("x1T_ev"), 1)
                if 0 <= r < NB:
                    act.wait_ge(s_("rope_sum"), r + 1)
                    if r >= 2:
                        act.wait_ge(s_(f"parts_out{par(r)}"), PUTS * (r // 2))
                    act.copy(parts[par(r)][:, 0], rsum[:, :, :]).then_inc(s_("rope_hi"), 1)
                    act.wait_ge(s_("rope_r"), r + 1)
                    act.copy(parts[par(r)][:, 1], rr[:, :, :]).then_inc(s_("rope_mid"), 1)

            gb = BK[1]
            for n in range(NSLOT * (NB + 3)):
                b, k = divmod(n, NSLOT)
                if k == 1 and 0 <= b - 1 < NB:
                    c = b - 1
                    act.wait_ge(s_("mT_mm"), c + 1)
                    if c >= QK_BUFS:
                        act.wait_ge(s_(f"max_put{c % QK_BUFS}"), 48 * (c // QK_BUFS))
                    if c >= 2:
                        act.wait_ge(s_(f"max_put{(c - 2) % QK_BUFS}"), 48 * ((c - 2) // QK_BUFS + 1))
                    act.copy(mT[par(c)][:, :], gb[0:3 * H, :].bitcast(BF16)[:, 0:S]).then_inc(s_("mT_ev"), 1)
                m = n - E_LAG
                if 0 <= m < NSLOT * NB:
                    act.wait_ge(s_("e_mm"), m + 1)
                    if m >= 2:
                        act.wait_ge(s_("pv_mm"), m - 1)
                    act.activation(pr[m % 2][:, :, :].rearrange("p g s -> p (g s)"), pairs[e_pair(m)][:, :], ACT.Exp, scale=SC) \
                        .then_inc(s_("exp_done"), 1)
                if k == 1 and 0 <= b - 3 < NB:
                    c = b - 3
                    act.wait_ge(s_("shift2_done"), c + 1)
                    for t in range(NT):
                        act.activation(x2[:, c, t, :], x2p[:, t, :], ACT.Identity, bias=shift2[:, t:t + 1],
                                       scale=rstdb[:, t:t + 1]).then_inc(s_("x2_done"), 1)
                if k == 2 and 0 <= b - 3 < NB:
                    c = b - 3
                    act.wait_ge(s_("x2T_mm"), c + 1)
                    act.copy(x2T[:, :], gb[:, 0:S]).then_inc(s_("x2T_ev"), 1)
                if k == 5 and 0 <= b - 3 < NB:
                    c = b - 3
                    act.wait_ge(s_("dv_done"), c + 1)
                    act.activation(ev[:, :], dv[:, :], ACT.Exp).then_inc(s_("ev_done"), 1)

            for e in range(E):
                def take_xeT(e):
                    act.wait_ge(s_("xeT_mm"), 2 * e + 1)
                    act.copy(xeT[par(e)][:, 0:4 * P], BK[0][:, :]).then_inc(s_("xeT_ev"), 1)
                    act.wait_ge(s_("xeT_mm"), 2 * e + 2)
                    act.copy(xeT[par(e)][:, 4 * P:CAP], BK[1][:, 0:P]).then_inc(s_("xeT_ev"), 1)
                if e == 0:
                    take_xeT(0)
                for f in range(FT):
                    for half in range(2):
                        n = (e * FT + f) * 2 + half
                        act.wait_ge(s_("gu_mm"), n + 1)
                        if n >= 2:
                            act.wait_ge(s_("hid_done"), n - 1)
                        act.activation(sil[n % 2], pairs[n % 2][:, 0:HALF], ACT.Silu).then_inc(s_("silu_done"), 1)
                        if e + 1 < E and 2 * f + half == CT + 1:
                            take_xeT(e + 1)

            for c in range(DC):
                act.wait_ge(s_("shift_done"), c + 1)
                for t in range(DT):
                    i = DT * c + t
                    act.activation(fin[c][:, t, :], fin[c][:, t, :], ACT.Identity, bias=shift[:, i:i + 1],
                                   scale=rstdd[:, i:i + 1]).then_inc(s_("fin_done"), 1)

        @block.vector
        def _(dve):
            b_T, b_Q, b_KV, b_V2, b_ST, b_O, b_R1, b_R2 = BK
            tt, ts, stt = dve.tensor_tensor, dve.tensor_scalar, dve.scalar_tensor_tensor
            chain = [0]

            def link(ins):
                chain[0] += 1
                ins.then_inc(s_("dve_chain"), 1)
                dve.wait_ge(s_("dve_chain"), chain[0])

            def keep(ins):
                chain[0] += 1
                ins.then_inc(s_("dve_chain"), 1)
                return chain[0]

            def need(at):
                dve.wait_ge(s_("dve_chain"), at)

            for i in range(2):
                dve.memset(feat[i][:, 0, :, :], 1.0)
                dve.memset(wbd[i][:, :, :], 0.0)
            link(dve.memset(on[:, :, :], 0.0))
            dve.memset(on[:, 0:8, BIAS_COL:BIAS_COL + 1], 1.0)
            dve.memset(onesb[:, :], 1.0)
            dve.memset(cnt[0][:, :], 0.0).then_inc(s_("cnt_done"), 1)
            dve.wait_ge(s_("const_in"), 16)
            dve.tensor_copy(idb[:, :], ident)
            link(dve.tensor_copy(trib[:, :], cn[:, C_TRI:C_TRI + P]))
            need(chain[0])
            dve.wait_ge(s_("small_in"), 16 * 7)
            dve.wait_ge(s_("wa_in"), 16)
            sgn = cn[:, C_SGN:C_SGN + P]
            tt(wa[:, W_XQR:W_XQR + D], wa[:, W_XQR:W_XQR + D], sgn, ALU.mult).then_inc(s_("rot_signs"), 1)
            tt(wa[:, W_XKR:W_XKR + D], wa[:, W_XKR:W_XKR + D], sgn, ALU.mult).then_inc(s_("rot_signs"), 1)
            sc = cn[:, C_SGNC:C_SGNC + 1]
            link(ts(bias[:, 2:4], bias[:, 2:4], sc, None, ALU.mult))
            link(ts(betas[:, 1:2], betas[:, 1:2], SC * SC, None, ALU.mult))
            link(ts(betas[:, 6:8], betas[:, 6:8], 2.0, None, ALU.mult))
            link(ts(betas[:, 10:11], betas[:, 10:11], 2.0, None, ALU.mult))
            for m in range(M):
                ins = ts(bm[:, m, :], cn[:, C_BLK:C_BLK + 32], betas[:, m:m + 1], None, ALU.mult)
            link(ins)
            link(ts(tmask[:, :], mcol8[:, :], 1.0, None, ALU.mult))
            ts(maskb[:, :], mrow8[:, :], -1.0, MASKED, ALU.add, ALU.mult).then_inc(s_("maskb_set"), 1)

            def clip(b):
                dve.wait_ge(s_("qkv_mm"), b + 1)
                y = feat[par(b)]
                ts(y[:, 1, 0, :], b_Q[:, 0:S], 1.0 / SC, -1.0 / SC, ALU.min, ALU.max).then_inc(s_("y_clip"), 1)
                ts(y[:, 1, 1, :].rearrange("p (t n) -> p t n", t=NT),
                   b_KV.rearrange("p (t k n) -> p t k n", t=NT, k=2)[:, :, 0, :],
                   1.0 / SC, -1.0 / SC, ALU.min, ALU.max).then_inc(s_("y_clip"), 1)

            def features(b):
                dve.wait_ge(s_("y_clip"), 2 * (b + 1))
                dve.wait_ge(s_("t2"), b + 1)
                stt(fl(b, 3), fl(b, 1), 2 * SC, fl(b, 2), ALU.mult, ALU.mult).then_inc(s_("f_dve"), 1)
                dve.wait_ge(s_("t4"), b + 1)
                if b >= 2:
                    dve.wait_ge(s_("out_mm"), b - 1)
                stt(fl(b, 5), fl(b, 1), 2 * SC, fl(b, 4), ALU.mult, ALU.mult).then_inc(s_("f_dve"), 1)
                dve.wait_ge(s_("f8"), b + 1)
                stt(fl(b, 9), fl(b, 1), 2 * SC, fl(b, 8), ALU.mult, ALU.mult).then_inc(s_("f_dve"), 1)

            def combine(b):
                dve.wait_ge(s_("kv_mm"), b + 1)
                dve.transpose(kvt[:, :, :].rearrange("p j v -> p (j v)"), b_ST[:, 0:32 * M]).then_inc(s_("kvt_ev"), 1)
                dve.wait_ge(s_("kvt_ev"), b + 1)
                k = lambda j: kvt[:, j, :]
                w = lambda j: wq_[:, j, :]
                a3 = keep(stt(k(3), k(1), -SC, k(3), ALU.mult, ALU.add))
                a7 = keep(stt(k(7), k(7), 2.0, k(5), ALU.mult, ALU.subtract))
                keep(tt(k(8), k(8), k(0), ALU.subtract))
                a6 = keep(stt(k(6), k(6), 2.0, k(2), ALU.mult, ALU.subtract))
                a9 = keep(stt(k(9), k(1), -2.0 * SC, k(9), ALU.mult, ALU.add))
                need(a7)
                keep(tt(k(5), k(5), k(3), ALU.subtract))
                a7 = keep(stt(k(7), k(1), -SC, k(7), ALU.mult, ALU.add))
                need(a6)
                a10 = keep(stt(k(10), k(10), 2.0, k(6), ALU.mult, ALU.subtract))
                need(a7)
                keep(tt(k(9), k(9), k(7), ALU.subtract))
                need(a10)
                link(stt(k(10), k(2), -2.0, k(10), ALU.mult, ALU.add))
                if b >= 1:
                    dve.wait_ge(s_("wbd_set"), 4 * b)
                link(tt(wq_[:, :, :], kvt[:, :, :], bm[:, :, :], ALU.mult))
                v, y, x = tmp32[:, 0, :], tmp32[:, 1, :], tmp32[:, 2, :]
                keep(stt(v, w(7), 0.5, w(9), ALU.mult, ALU.add))
                b3 = keep(tt(w(3), w(3), w(5), ALU.subtract))
                b7 = keep(stt(w(7), w(9), -2.0, w(7), ALU.mult, ALU.add))
                bx = keep(tt(x, w(6), w(10), ALU.add))
                need(b3)
                by = keep(tt(y, w(3), v, ALU.add))
                need(b7)
                keep(stt(w(5), w(7), -0.5, w(5), ALU.mult, ALU.add))
                need(bx)
                keep(stt(w(2), x, -0.5, w(2), ALU.mult, ALU.add))
                keep(tt(w(6), w(6), w(10), ALU.subtract))
                need(by)
                keep(stt(w(1), y, -SC, w(1), ALU.mult, ALU.add))
                keep(tt(w(0), w(0), w(8), ALU.subtract))
                need(chain[0])
                dve.tensor_copy(tmp32[:, 0, 0:1], w(0)[:, 0:1]).then_inc(s_("w_done"), 1)

            def values(b):
                dve.wait_ge(s_("v2_mm"), b + 1)
                tt(v2[:, b].rearrange("p t n -> p (t n)").rearrange("p (t n) -> p t n", t=NT),
                   b_V2[:, 0:S].rearrange("p (t n) -> p t n", t=NT),
                   brow[:, None, 0:D].to_broadcast([P, NT, D]), ALU.add).then_inc(s_("v2_ev"), 1)

            def rope(b):
                dve.wait_ge(s_("rope_mm"), b + 1)
                if b >= 1:
                    dve.wait_ge(s_("rope_sum"), b)
                for w in range(2):
                    for bank, table, off, dst in ((b_R1, C_COS, 0, rc), (b_R2, C_SIN, 2, rs)):
                        stt(dst[:, w, :], bank[:, w * S:(w + 1) * S], bias[:, off + w:off + w + 1],
                            cn[:, table:table + S], ALU.add, ALU.mult).then_inc(s_("rope_mul"), 1)

            def norm_stats(src, st, mvt, done):
                for t in range(NT):
                    at = keep(dve.bn_stats(st[:, t, :], src[:, t, :]))
                need(at)
                for t in range(NT):
                    dve.bn_aggr(mvt[:, t, :], st[:, t, :]).then_inc(s_(done), 1)

            def norm1(b):
                dve.wait_ge(s_("y_mm"), b + 1)
                tt(ypre[:, :, :], b_V2[:, 0:S].rearrange("p (t n) -> p t n", t=NT), xin[b % X_BUFS][:, :, :], ALU.add) \
                    .then_inc(s_("x1_sum"), 1)
                dve.wait_ge(s_("x1_sum"), b + 1)
                norm_stats(ypre, st6, mv, "mv1")

            def norm1_end(b):
                dve.wait_ge(s_("rstd1"), b + 1)
                for t in range(NT):
                    ts(xres[:, b, t, :], ypre[:, t, :], mv[:, t, 0:1], rstd[:, t:t + 1], ALU.subtract, ALU.mult) \
                        .then_inc(s_("x1_done"), 1)

            def row_max(n):
                b, k = divmod(n, NSLOT)
                c, hq = divmod(k, 4)
                dve.wait_ge(s_("m_mm"), n + 1)
                dve.tensor_reduce(mx[par(b)][:, c, 4 * hq:4 * hq + 4],
                                  pairs[m_pair(n)][:, :].rearrange("p (g s) -> p g s", g=4), AX.X, ALU.max) \
                    .then_inc(s_("max_done"), 1)

            for i in A_STEPS:
                if 0 <= i + 2 < NB:
                    clip(i + 2)
                if 0 <= i + 1 < NB:
                    combine(i + 1)
                if 0 <= i - LAG < NB:
                    values(i - LAG)
                if 0 <= i + 2 < NB:
                    features(i + 2)
                if 0 <= i < NB:
                    norm1(i)
                if 0 <= i - LAG < NB:
                    rope(i - LAG)
                if 0 <= i < NB:
                    norm1_end(i)
                for n in pre_slots(i):
                    row_max(n)

            od, gb = BK[0], BK[1]

            def norm2_and_split(b, c):
                do_b, do_c = 0 <= b < NB, 0 <= c < NB
                if do_b:
                    dve.wait_ge(s_("wp_mm"), b + 1)
                    if b >= 1:
                        dve.wait_ge(s_("x2_done"), NT * b)
                    for t in range(NT):
                        ins = stt(x2p[:, t, :], gb[:, t * P:(t + 1) * P], tmask[:, b * NT + t:b * NT + t + 1],
                                  xres[:, b, t, :], ALU.mult, ALU.add)
                    ins.then_inc(s_("x2_sum"), 1)
                if do_c:
                    m = mx[par(c)][:, :, :]
                    dve.wait_ge(s_("max_done"), NSLOT * (c + 1))
                    if c >= 1:
                        dve.wait_ge(s_("mT_mm"), c)
                    hi = keep(ts(nm[:, :, 0, :], m, -1.0, None, ALU.mult))
                if do_b:
                    dve.wait_ge(s_("x2_sum"), b + 1)
                    keep(dve.bn_stats(st6b[:, 0, :], x2p[:, 0, :]))
                if do_c:
                    need(hi)
                    rest = keep(stt(mr[:, :, :], m, -1.0, nm[:, :, 0, :], ALU.mult, ALU.subtract))
                if do_b:
                    stats = keep(dve.bn_stats(st6b[:, 1, :], x2p[:, 1, :]))
                if do_c:
                    need(rest)
                    mid = keep(dve.tensor_copy(nm[:, :, 1, :], mr[:, :, :]))
                if do_b:
                    need(stats)
                    for t in range(NT):
                        dve.bn_aggr(mvb[:, t, :], st6b[:, t, :]).then_inc(s_("mv2"), 1)
                if do_c:
                    need(mid)
                    tt(nm[:, :, 2, :], mr[:, :, :], nm[:, :, 1, :], ALU.subtract).then_inc(s_("nm_done"), 1)

            def take_outputs(b):
                dve.wait_ge(s_("pv_mm"), NSLOT * (b + 1))
                dve.transpose(ot[:, :, :].rearrange("p a c -> p (a c)"), od).then_inc(s_("od_read"), 1)

            def norm2_shift(b):
                dve.wait_ge(s_("rstd2"), b + 1)
                stt(shift2[:, :], mvb[:, :, 0], -1.0, rstdb[:, :], ALU.mult, ALU.mult).then_inc(s_("shift2_done"), 1)

            chosen = [0]

            def choose(b):
                dve.wait_ge(s_("lg_mm"), b + 1)
                ts(lg[:, :, :], gb[:, 0:NT * E].rearrange("p (t e) -> p t e", t=NT), CLAMP, -CLAMP, ALU.min, ALU.max) \
                    .then_inc(s_("lg_done"), 1)
                dve.wait_ge(s_("lg_done"), b + 1)
                for t in range(NT):
                    at = keep(dve.max(v8[:, t, :], lg[:, t, :]))
                need(at)
                for t in range(NT):
                    chosen[0] = keep(dve.max_index(i8[:, t, :], v8[:, t, :], lg[:, t, :]))
                if b >= 1:
                    dve.wait_ge(s_("w_all"), b)
                tt(dv[:, :], v8[:, :, 1], v8[:, :, 0], ALU.subtract).then_inc(s_("dv_done"), 1)

            def normalise_and_mark(b, c):
                do_b, do_c = 0 <= b < NB, 0 <= c < NB
                if do_c:
                    need(chosen[0])
                    index = keep(dve.tensor_copy(idf[:, :, :], i8[:, :, 0:K]))
                if do_b:
                    dve.wait_ge(s_("od_read"), b + 1)
                    den = keep(dve.reciprocal(rden[:, :, :], ot[:, :, 16:18]))
                if do_c:
                    need(index)
                    marks = keep(tt(oh[:, :, :, :].rearrange("p t k e -> p (t k) e"),
                                    cn[:, C_IOTA:C_IOTA + 32].rearrange("p (a e) -> p a e", e=E),
                                    idf[:, :, :].rearrange("p t k -> p (t k)")[:, :, None].to_broadcast([P, NT * K, E]),
                                    ALU.is_equal))
                if do_b:
                    need(den)
                    out = keep(tt(on[:, :, 0:16].rearrange("p a (j d) -> p a j d", j=2),
                                  ot[:, :, 0:16].rearrange("p a (j d) -> p a j d", j=2),
                                  rden[:, :, :, None].to_broadcast([P, 16, 2, DH]), ALU.mult))
                if do_c:
                    need(marks)
                    if c >= 1:
                        dve.wait_ge(s_("pos_mm"), c)
                    tt(ohs[:, :, :], oh[:, :, 0, :], oh[:, :, 1, :], ALU.add).then_inc(s_("ohs_done"), 1)
                if do_b:
                    need(out)
                    if b >= 1:
                        dve.wait_ge(s_("wp_mm"), b)
                    dve.transpose(odn[:, :], on[:, :, :].rearrange("p a c -> p (a c)")).then_inc(s_("odn_done"), 1)

            def take_positions(b):
                dve.wait_ge(s_("pos_mm"), b + 1)
                tt(pm[:, :, :].rearrange("p (t k) e -> p t k e", t=NT),
                   gb[:, 0:NT * E].rearrange("p (t e) -> p t e", t=NT)[:, :, None, :].to_broadcast([P, NT, K, E]),
                   oh[:, :, :, :], ALU.mult).then_inc(s_("pm_done"), 1)

            def place(b):
                w = xp[par(b)]
                dve.wait_ge(s_("ev_done"), b + 1)
                total = keep(ts(ev1[:, :], ev[:, :], 1.0, 1e-12, ALU.add, ALU.add))
                dve.wait_ge(s_("pm_done"), b + 1)
                rank = keep(dve.tensor_reduce(pos[:, :], pm[:, :, :], AX.X, ALU.add))
                if b >= 2:
                    dve.wait_ge(s_(f"rows_out{par(b)}"), 16 * NT * K * (b // 2))
                need(total)
                first = keep(dve.reciprocal(w[:, :, 0, D], ev1[:, :]))
                need(rank)
                keep(ts(over[:, :], pos[:, :], float(CAP), FAR, ALU.is_ge, ALU.mult))
                row = keep(stt(slf[:, :], idf[:, :, :].rearrange("p t k -> p (t k)"), float(CAP), pos[:, :],
                               ALU.mult, ALU.add))
                need(first)
                tt(w[:, :, 1, D], ev[:, :], w[:, :, 0, D], ALU.mult).then_inc(s_("w_all"), 1)
                need(row)
                tt(slot[par(b)][:, :], slf[:, :], over[:, :], ALU.add).then_inc(s_("slot_done"), 1)

            for n in range(NSLOT * (NB + 3)):
                b, k = divmod(n, NSLOT)
                if k == 1 and 0 <= b - 3 < NB:
                    norm2_shift(b - 3)
                if k == 5 and 0 <= b - 2 < NB:
                    take_outputs(b - 2)
                if k == 6 and 0 <= b - 3 < NB:
                    take_positions(b - 3)
                if PRE_N <= n < NSLOT * NB:
                    row_max(n)
                if k == 4 and 0 <= b - 3 < NB:
                    choose(b - 3)
                if k == 5:
                    normalise_and_mark(b - 2, b - 3)
                if k == 6 and 0 <= b - 3 < NB:
                    place(b - 3)
                if k == 7:
                    norm2_and_split(b - 2, b)

            def hid_mul(n):
                e, r = divmod(n, 2 * FT)
                f, half = divmod(r, 2)
                dve.wait_ge(s_("silu_done"), n + 1)
                if r == 0 and e >= 2:
                    dve.wait_ge(s_("ye_mm"), CT * (e - 1))
                tt(hid[par(e)][:, f, half * HALF:(half + 1) * HALF], sil[n % 2], pairs[n % 2][:, 512:512 + HALF],
                   ALU.mult).then_inc(s_("hid_done"), 1)

            def take_y(e, c):
                n = CT * e + c
                dve.wait_ge(s_("ye_mm"), n + 1)
                if c == 0 and e >= 2:
                    dve.wait_ge(s_(f"ye_out{par(e)}"), 16 * CT * (e // 2))
                ts(ye[par(e)][:, c, :], BK[6 + n % 2][:, 0:P], xe[e % E_BUFS][:, c, D:D + 1], None, ALU.mult) \
                    .then_inc(s_("ye_ev"), 1)

            for e in range(E):
                for k in range(2 * FT):
                    hid_mul(e * 2 * FT + k)
                    if e >= 1 and 1 <= k <= CT:
                        take_y(e - 1, k - 1)
            for c in range(CT):
                take_y(E - 1, c)

            def sum_stats(c):
                dve.wait_ge(s_(f"y_in{c}"), 16 * K)
                link(tt(fin[c][:, :, :], yl[c][0][:, :, :], yl[c][1][:, :, :], ALU.add))
                link(tt(fin[c][:, :, :], fin[c][:, :, :], x2[:, 2 * c:2 * c + 2].rearrange("p b t d -> p (b t) d"), ALU.add))
                for t in range(DT):
                    at = keep(dve.bn_stats(st6d[:, DT * c + t, :], fin[c][:, t, :]))
                need(at)
                for t in range(DT):
                    dve.bn_aggr(mvd[:, DT * c + t, :], st6d[:, DT * c + t, :]).then_inc(s_("mv3"), 1)

            def shifts(c):
                dve.wait_ge(s_("rstd3"), c + 1)
                stt(shift[:, DT * c:DT * (c + 1)], mvd[:, DT * c:DT * (c + 1), 0], -1.0, rstdd[:, DT * c:DT * (c + 1)],
                    ALU.mult, ALU.mult).then_inc(s_("shift_done"), 1)

            for c in range(DC):
                sum_stats(c)
                if c >= 1:
                    shifts(c - 1)
            shifts(DC - 1)

        @block.gpsimd
        def _(pool):
            tt, ts = pool.tensor_tensor, pool.tensor_scalar

            def copy(out, src):
                return ts(out, src, 1.0, 0.0, ALU.mult, ALU.add)

            pool.memset(zrow[:, :], 0.0).then_inc(s_("zrow_set"), 1)
            pool.wait_ge(s_("zrow_set"), 1)
            pool.memset(zrow[:, :].rearrange("p (r n) -> p r n", r=4)[:, :, D + 1].bitcast(U32), NOWHERE) \
                .then_inc(s_("zrow_set"), 1)
            pool.memset(halfs[:, :], -0.5).then_inc(s_("halfs_set"), 1)
            pool.memset(minus1[:, :], -1.0).then_inc(s_("halfs_set"), 1)
            for i in range(QK_BUFS):
                for tile in (qb[i], kb[i]):
                    pool.memset(tile[:, :, :].rearrange("p h s -> p (h s)").bitcast(U32), 0) \
                        .then_inc(s_("qk_cleared"), 1)
            for i in range(2):
                pool.memset(vp[i][:, :, :, :], 0.0).then_inc(s_("vp_const"), 1)
            pool.wait_ge(s_("vp_const"), 2)
            for i in range(2):
                for j in range(2):
                    pool.memset(vp[i][:, :, :, :].rearrange("p c (u j g) n -> p (c u) j g n", u=2, j=2)
                                [:, :, j, :, 16 + j:17 + j], 1.0).then_inc(s_("vp_const"), 1)
            pool.wait_ge(s_("halfs_set"), 1)

            def rsqrt(b, count, dst_v, mvt, dst, sem_mv, name, at, n):
                pool.wait_ge(s_(sem_mv), count)
                ts(dst_v, mvt, EPS, None, ALU.add).then_inc(s_("var_eps"), 1)
                at[0] += 1
                pool.wait_ge(s_("var_eps"), at[0])
                tt(dst, dst_v, halfs[:, 0:n], ALU.pow).then_inc(s_(name), 1)

            at = [0]

            for i in A_STEPS:
                f, r = i + 2, i - LAG
                if 0 <= f < NB:
                    pool.wait_ge(s_("t4"), f + 1)
                    if f >= 2:
                        pool.wait_ge(s_("out_mm"), f - 1)
                    tt(fl(f, 6), fl(f, 2), fl(f, 4), ALU.mult).then_inc(s_("f_pool"), 1)
                    pool.wait_ge(s_("f_dve"), 3 * f + 1)
                    tt(fl(f, 7), fl(f, 3), fl(f, 4), ALU.mult).then_inc(s_("f_pool"), 1)
                    pool.wait_ge(s_("f8"), f + 1)
                    tt(fl(f, 10), fl(f, 2), fl(f, 8), ALU.mult).then_inc(s_("f_pool"), 1)
                if 0 <= i < NB:
                    rsqrt(i, NT * (i + 1), ve[:, :], mv[:, :, 1], rstd[:, :], "mv1", "rstd1", at, NT)
                if 0 <= r < NB:
                    pool.wait_ge(s_("rope_mul"), 4 * (r + 1))
                    tt(rsum[:, :, :], rc[:, :, :], rs[:, :, :], ALU.add).then_inc(s_("rope_sum"), 1)
                    pool.wait_ge(s_("rope_hi"), r + 1)
                    tt(rr[:, :, :], rsum[:, :, :], parts[par(r)][:, 0], ALU.subtract).then_inc(s_("rope_r"), 1)
                    pool.wait_ge(s_("rope_mid"), r + 1)
                    tt(parts[par(r)][:, 2], rr[:, :, :], parts[par(r)][:, 1], ALU.subtract).then_inc(s_("rope_lo"), 1)

            pool.wait_ge(s_("xe_cleared"), 16 * (NROWS // (4 * P)))
            for n in range(NSLOT * (NB + 3)):
                b, k = divmod(n, NSLOT)
                if k == 0 and 0 <= b < NB:
                    pool.wait_ge(s_("v2_ev"), b + 1)
                    if b == 0:
                        pool.wait_ge(s_("vp_const"), 6)
                    if b >= 2:
                        pool.wait_ge(s_("pv_mm"), NSLOT * (b - 1))
                    src = v2[:, b].rearrange("p c (u j g d) -> p (c u) j g d", u=2, j=2, g=4)
                    dst = vp[par(b)][:, :, :, :].rearrange("p c (u j g) n -> p (c u) j g n", u=2, j=2)
                    for j in range(2):
                        copy(dst[:, :, j, :, DH * j:DH * j + DH], src[:, :, j]).then_inc(s_("vp_set"), 1)
                if k == 7 and 0 <= b - 2 < NB:
                    c = b - 2
                    rsqrt(c, NT * (c + 1), veb[:, :], mvb[:, :, 1], rstdb[:, :], "mv2", "rstd2", at, NT)
                if k == 7 and 0 <= b - 3 < NB:
                    c = b - 3
                    pool.wait_ge(s_("slot_done"), c + 1)
                    pool.wait_ge(s_("w_all"), c + 1)
                    pool.wait_ge(s_("xp_set"), 3 * (c + 1))
                    for t in range(NT):
                        for k_ in range(K):
                            pool.indirect_dma_start(
                                out=xe_d, out_offset=bass.IndirectOffsetOnAxis(ap=slot[par(c)][:, t * K + k_:t * K + k_ + 1], axis=0),
                                in_=xp[par(c)][:, t, k_, :], in_offset=None, bounds_check=NROWS - 1, oob_is_err=False) \
                                .then_inc(s_(f"rows_out{par(c)}"), 16)
                if k == 1 and 0 <= b - 3 < NB:
                    c = b - 3
                    pool.wait_ge(s_("x2_done"), NT * (c + 1))
                    if c >= 2:
                        pool.wait_ge(s_(f"rows_out{par(c)}"), 16 * NT * K * (c // 2))
                    for k_ in range(K):
                        copy(xp[par(c)][:, :, k_, 0:D], x2[:, c]).then_inc(s_("xp_set"), 1)
                    pool.tensor_copy(xp[par(c)][:, :, :, D + 1].bitcast(U32), dest[:, c]).then_inc(s_("xp_set"), 1)
                if k == 4 and 0 <= b - 3 < NB:
                    c = b - 3
                    pool.wait_ge(s_("ohs_done"), c + 1)
                    if c == 0:
                        pool.wait_ge(s_("cnt_done"), 1)
                    tt(ohsum[:, :], ohs[:, 0, :], ohs[:, 1, :], ALU.add).then_inc(s_("ohsum"), 1)
                    pool.wait_ge(s_("ohsum"), c + 1)
                    if c >= 1:
                        pool.wait_ge(s_("pos_mm"), c)
                    tt(cnt[par(c + 1)][:, :], cnt[par(c)][:, :], ohsum[:, :], ALU.add).then_inc(s_("cnt_next"), 1)
            pool.wait_ge(s_("y_cleared"), 16 * (K * T // (4 * P)))
            for e in range(E):
                for c in range(CT):
                    pool.wait_ge(s_("ye_ev"), CT * e + c + 1)
                    pool.indirect_dma_start(
                        out=yb_d, out_offset=bass.IndirectOffsetOnAxis(ap=xe[e % E_BUFS][:, c, D + 1:D + 2].bitcast(U32), axis=0),
                        in_=ye[par(e)][:, c, :], in_offset=None, bounds_check=K * T - 1, oob_is_err=False) \
                        .then_inc(s_(f"ye_out{par(e)}"), 16)

            for c in range(DC):
                i, j = DT * c, DT * (c + 1)
                rsqrt(c, DT * (c + 1), ved[:, i:j], mvd[:, i:j, 1], rstdd[:, i:j], "mv3", "rstd3", at, DT)


def kernel(**inputs):
    import numpy as _np
    import concourse.bacc as _bacc
    from concourse import mybir as _mybir
    from concourse.bass_utils import run_bass_kernel_spmd as _run

    a = {k: _np.asarray(v) for k, v in inputs.items()}
    swap = _np.arange(D).reshape(H, 2, DH // 2)[:, ::-1].reshape(-1)
    wq, wk = a["L0_xattn_Wq"], a["L0_xattn_Wk"]
    wp_t = a["L0_xattn_Wp"].T
    wp_rows = _np.zeros((2, 4, 32, D), wp_t.dtype)
    wp_rows[:, :, 0:2 * DH] = wp_t.reshape(2, 2, 4, DH, D).transpose(0, 2, 1, 3, 4).reshape(2, 4, 2 * DH, D)
    wp_rows[0, 0, BIAS_COL] = a["L0_xattn_bp"]
    w_in_t = a["L0_attn_w_in"].T
    wa = _np.concatenate([w_in_t, a["L0_attn_w_out"].T, wq.T, wq[swap].T, wk.T, wk[swap].T,
                          a["L0_xattn_Wv"].T, wp_rows[0].reshape(P, D), wp_rows[1].reshape(P, D)], axis=1)
    bq, bk = a["L0_xattn_bq"], a["L0_xattn_bk"]
    bias = _np.stack([bq, bk, bq[swap], bk[swap]], axis=1)
    brow = _np.broadcast_to(a["L0_xattn_bv"][None], (P, D))
    mask = a["mask_BxS2_bf1"].view(_np.uint8)
    const, dest = constants()
    ones_zeros = _np.zeros((6, H * S), _mybir.dt.np(_mybir.dt.bfloat16))
    ones_zeros[0:3] = 1
    arrays = {
        "x": a["x"].reshape(T, D), "ctx": a["ctx_1024"].reshape(T, D), "mrow": mask,
        "mcol": mask.reshape(NB * NT, P).T, "beta": _np.repeat(a["L0_attn_beta"], DH, axis=0), "wa": wa,
        "bias": bias, "brow": brow, "wr": a["L0_ffn_Wr"], "w1": a["L0_ffn_W1"], "w3": a["L0_ffn_W3"],
        "w2": a["L0_ffn_W2"], "const": const, "dest": dest, "rows": ones_zeros,
    }
    arrays = {f"in_{k}": _np.ascontiguousarray(v) for k, v in arrays.items()}
    nc = _bacc.Bacc("TRN2", target_bir_lowering=False, num_devices=1)
    args = [nc.dram_tensor(k, v.shape, _mybir.dt.from_np(v.dtype), kind="ExternalInput").ap() for k, v in arrays.items()]
    out = nc.dram_tensor("out", (T, D), F32, kind="ExternalOutput").ap()
    build(nc, *args, out)
    r = _run(nc, [arrays], core_ids=[0])
    return r.results[0]["out"].reshape(NB, S, D)
```

```python
from contextlib import ExitStack

import numpy as np

import concourse.bass as bass
from concourse import mybir

ALU = mybir.AluOpType
ACT = mybir.ActivationFunctionType
AX = mybir.AxisListType
F32 = mybir.dt.float32
BF16 = mybir.dt.bfloat16
F16 = mybir.dt.float16
U32 = mybir.dt.uint32
U8 = mybir.dt.uint8

P = 128
NB, S, D = 8, 256, 128
T = NB * S
NT = S // P
H, DH = 16, 8
M = 11
SC = float(np.float32(DH ** -0.5))
E, K, F = 8, 2, 512
CAP = 640
CT = CAP // P
FT = F // P
HALF = CAP // 2
ROW = D + 2
NROWS = E * CAP
EPS = 1e-5
CLAMP = 10000.0
FAR = 1.0e6
NOWHERE = 1 << 20
MASKED = 1.0e30
BIAS_COL = 2 * DH
E_LAG = 12
OFFSETS = {
    "values": 5,
    "split": 8, "turn": 10,
    "out": 20, "normal": 21, "back": 22,
    "project": 26, "norm2": 27, "x2": 29,
    "x2_turn": 31, "logits": 32, "clip": 33,
    "choose": 34, "place": 36,
}
LATE = {
    NB - 3: {"x2": 28, "x2_turn": 29, "logits": 30, "clip": 31, "choose": 32, "place": 34},
    NB - 2: {"project": 24, "norm2": 25, "x2": 26, "x2_turn": 28, "logits": 29, "clip": 30, "choose": 30, "place": 32},
    NB - 1: {"back": 21, "project": 23, "norm2": 24, "x2": 25, "x2_turn": 26, "logits": 27, "clip": 28, "choose": 28,
             "place": 29},
}
NSLOT = 8
QK_BUFS = 3
E_BUFS = 3
DOWN_AT = {1: [0], 2: [1], 3: [2, 3], 4: [4]}
ROWS_STEP = 5
W_STEPS = (2, 4)
X_UP, W_UP = 4.0, 16.0
DC = 4
DT = T // P // DC
DVE_LAST = 2
X_BUFS = 4
R2 = float(np.sqrt(2.0))
PRODS = 6
Q_PUT = ((0, 0, 3, 1), (1, 3, 5, 1), (2, 5, 6, 1))
K_PUT = ((0, 0, 5, 4), (0, 5, 6, 1), (2, 1, 2, 1), (1, 2, 4, 1))
PUTS = 16 * (len(Q_PUT) + len(K_PUT))
MASK_ROW = PRODS * DH
MAX_ROW = MASK_ROW + 1

C_ID, C_COS, C_SIN, C_TRI, C_BLK, C_SGN, C_IOTA, C_SGNC = 0, 128, 384, 640, 768, 800, 928, 960
NCONST = 961
W_Q, W_KV, W_O, W_XQ, W_XQR, W_XK, W_XKR, W_XV, W_XP = (128 * i for i in (0, 1, 3, 4, 5, 6, 7, 8, 9))
NWA = 128 * 11


def constants():
    c = np.zeros((P, NCONST), np.float32)
    p = np.arange(P)
    c[:, C_ID:C_ID + P] = np.eye(P)
    inv = (1.0 / np.float32(10000.0) ** (np.arange(0, DH, 2, dtype=np.float32) / np.float32(DH))).astype(np.float32)
    fr = np.outer(np.arange(S, dtype=np.float32), inv).astype(np.float32)
    ang = np.concatenate([fr, fr], axis=1).T[p % DH]
    c[:, C_COS:C_COS + S] = np.cos(ang.astype(np.float64))
    c[:, C_SIN:C_SIN + S] = np.sin(ang.astype(np.float64))
    c[:, C_TRI:C_TRI + P] = p[:, None] < p[None, :]
    c[:, C_BLK:C_BLK + 32] = (p[:, None] % 32) // DH == np.arange(32)[None, :] // DH
    c[:, C_SGN:C_SGN + P] = np.where(p % DH < DH // 2, -1.0, 1.0)[None, :]
    c[:, C_IOTA:C_IOTA + 32] = np.arange(32)[None, :] % E
    c[:, C_SGNC] = np.where(p % DH < DH // 2, -1.0, 1.0)
    b, t, k = np.meshgrid(np.arange(NB), np.arange(NT), np.arange(K), indexing="ij")
    dest = (k * T + b * S + t * P)[None] + p[:, None, None, None]
    return c, dest.reshape(P, -1).astype(np.uint32)


def build(nc, x_d, ctx_d, mrow_d, mcol_d, beta_d, wa_d, bias_d, brow_d, wr_d, w1_d, w3_d, w2_d, const_d, dest_d,
          rows_d, out_d):
    ctx = ExitStack()
    with ctx:
        def sb(name, shape, dt=F32):
            return ctx.enter_context(nc.sbuf_tensor(name, shape, dt))

        def sem(name):
            return ctx.enter_context(nc.semaphore(name))

        def dram(name, shape, dt=F32):
            return nc.dram_tensor(name, shape, dt, kind="Internal").ap()

        packed_d = dram("packed_scratch", [NB, 2, H * DH, PRODS, S], BF16)
        xe_d = dram("xe_scratch", [NROWS, ROW])
        yb_d = dram("y_scratch", [K * T, D])

        banks = [ctx.enter_context(nc.psum_tensor(f"bank{i}", [P, 512], F32)) for i in range(2)]
        pairs = [ctx.enter_context(nc.psum_tensor(f"pair{i}", [P, 1024], F32)) for i in range(3)]
        BK = [banks[0][:, :], banks[1][:, :]] + [pairs[i // 2][:, 512 * (i % 2):512 * (i % 2) + 512] for i in range(6)]

        cn = sb("cn", [P, NCONST])
        wa = sb("wa", [P, NWA])
        wr = sb("wr", [P, E])
        bias = sb("bias", [P, 4])
        brow = sb("brow", [P, D])
        betas = sb("betas", [P, M])
        bm = sb("bm", [P, M, 32])
        mrow8 = sb("mrow8", [NB, S], U8)
        maskb = sb("maskb", [NB, S], BF16)
        mcol8 = sb("mcol8", [P, NB * NT], U8)
        tmask = sb("tmask", [P, NB * NT])
        dest = sb("dest", [P, NB, NT, K], U32)
        idb = sb("idb", [P, P], BF16)
        trib = sb("trib", [P, P], BF16)
        onesb = sb("onesb", [P, P], BF16)
        halfs = sb("halfs", [P, 16])
        minus1 = sb("minus1", [P, 1])
        zrow = sb("zrow", [P, 4 * ROW])
        ident = cn[:, C_ID:C_ID + P]

        xin = [sb(f"xin{i}", [P, NT, D]) for i in range(X_BUFS)]
        xres = sb("xres", [P, NB, NT, D])
        cin = [sb(f"cin{i}", [P, NT, D]) for i in range(2)]
        xT = sb("xT", [P, S])
        cT = sb("cT", [P, S])
        x1T = sb("x1T", [P, S])
        feat = [sb(f"feat{i}", [P, M, 2, S]) for i in range(2)]
        sq = sb("sq", [P, 2, 2 * S])
        val = [sb(f"val{i}", [P, NT, D]) for i in range(2)]
        kvt = sb("kvt", [P, M, 32])
        wq_ = sb("wcomb", [P, M, 32])
        tmp32 = sb("tmp32", [P, 3, 32])
        wbd = [sb(f"wbd{i}", [P, M, P]) for i in range(2)]
        oT = sb("oT", [P, S])
        ypre = sb("ypre", [P, NT, D])
        st6 = sb("st6", [P, NT, 6])
        mv = sb("mv", [P, NT, 2])
        ve = sb("ve", [P, NT])
        rstd = sb("rstd", [P, NT])
        v2 = sb("v2", [P, NB, NT, D])
        rc = sb("rc", [P, 2, S])
        rs = sb("rs", [P, 2, S])
        rsum = sb("rsum", [P, 2, S])
        rr = sb("rr", [P, 2, S])
        parts = [sb(f"parts{i}", [P, 3, 2, S], BF16) for i in range(2)]

        qb = [sb(f"qb{i}", [P, H, S], BF16) for i in range(QK_BUFS)]
        kb = [sb(f"kb{i}", [P, H, S], BF16) for i in range(QK_BUFS)]
        mx = [sb(f"mx{i}", [P, NT, H]) for i in range(2)]
        mr = sb("mr", [P, NT, H])
        nm = sb("nm", [P, NT, 3, H], BF16)
        mT = [sb(f"mT{i}", [3 * H, S], BF16) for i in range(2)]
        pr = [sq[:, :, :].rearrange("p a (g s) -> p (a g) s", g=2), sb("pr1", [P, 4, S])]
        vp = [sb(f"vp{i}", [P, NT, H, 32]) for i in range(2)]
        ot = sb("ot", [P, 16, 32])
        on = sb("on", [P, 16, 32])
        rden = sb("rden", [P, 16, 2])
        odn = sb("odn", [P, 512])
        shift2 = sb("shift2", [P, NT])
        x2p = sb("x2p", [P, NT, D])
        st6b = sb("st6b", [P, NT, 6])
        mvb = sb("mvb", [P, NT, 2])
        veb = sb("veb", [P, NT])
        rstdb = sb("rstdb", [P, NT])
        x2 = sb("x2", [P, NB, NT, D])
        x2T = sb("x2T", [P, S])
        lg = sb("lg", [P, NT, E])
        v8 = sb("v8", [P, NT, 8])
        i8 = sb("i8", [P, NT, 8], U32)
        idf = sb("idf", [P, NT, K])
        oh = sb("oh", [P, NT, K, E])
        ohs = sb("ohs", [P, NT, E], BF16)
        cnt = [sb(f"cnt{i}", [P, E], BF16) for i in range(2)]
        ohsum = sb("ohsum", [P, E], BF16)
        dv = sb("dv", [P, NT])
        ev = sb("ev", [P, NT])
        ev1 = sb("ev1", [P, NT])
        pm = sb("pm", [P, NT * K, E])
        pos = sb("pos", [P, NT * K])
        over = sb("over", [P, NT * K])
        slf = sb("slf", [P, NT * K])
        slot = [sb(f"slot{i}", [P, NT * K], U32) for i in range(2)]
        xp = [sb(f"xp{i}", [P, NT, K, ROW]) for i in range(2)]

        def carve(tile, at, n):
            return tile[:, :, :, :].rearrange("p a b c -> p (a b c)")[:, at:at + n]

        def half_words(tile):
            return tile[:, :, :].rearrange("p h s -> p (h s)").bitcast(F32)

        xe = [carve(feat[i], 0, CT * ROW) for i in range(2)] + [half_words(qb[2])[:, 0:CT * ROW]]
        xe = [t.rearrange("p (c r) -> p c r", c=CT) for t in xe]
        xeT = [carve(feat[i], 700, CAP).bitcast(F16).rearrange("p (a c) -> p a c", a=2) for i in range(2)]
        wparts = [v2[:, 4 * i:4 * i + 4].rearrange("p b t n -> p (b t n)").bitcast(F16)
                  .rearrange("p (a w n) -> p a w n", a=2, w=2) for i in range(2)]
        hid = [carve(feat[i], 1400, FT * CAP).rearrange("p (f c) -> p f c", f=FT) for i in range(2)]
        ye = [carve(feat[i], 4000, CT * D).rearrange("p (c d) -> p c d", c=CT) for i in range(2)]
        sil = [carve(feat[i], 4700, HALF) for i in range(2)]
        w13 = [wbd[i][:, 0:8, :].rearrange("p m n -> p (m n)") for i in range(2)] + [half_words(kb[2])[:, 0:2 * F]]
        w13 = [t.rearrange("p (w n) -> p w n", w=2) for t in w13]
        w2 = [carve(feat[i], 5100, F) for i in range(2)] + [half_words(kb[2])[:, 2 * F:3 * F]]
        w2 = [t.rearrange("p (f d) -> p f d", f=FT) for t in w2]

        def spare(tile, at):
            return half_words(tile)[:, at * DT * D:(at + 1) * DT * D].rearrange("p (t d) -> p t d", d=D)
        yl = [[spare(qb[k], c) for k in range(K)] for c in range(DC)]
        fin = [spare(kb[0], c) for c in range(DC)]
        shift = sb("shift", [P, T // P])
        st6d = sb("st6d", [P, 16, 6])
        mvd = sb("mvd", [P, 16, 2])
        ved = sb("ved", [P, 16])
        rstdd = sb("rstdd", [P, 16])

        PRE = {NB: 2, NB + 1: 2}
        PRE_N = sum(PRE.values())
        assert PRE_N % 2 == 0 and PRE_N <= NSLOT

        def pre_slots(i):
            first = sum(v for k, v in PRE.items() if k < i)
            return range(first, first + PRE.get(i, 0))

        at_slot = {step: {NSLOT * b + LATE.get(b, {}).get(step, offset): b for b in range(NB)}
                   for step, offset in OFFSETS.items()}
        SLOTS = range(max(at_slot["place"]) + 1)

        def batch_at(n, step):
            return at_slot[step].get(n)

        def m_pair(n):
            return 1 if n < PRE_N else n % 2

        def e_pair(n):
            return 0 if n + E_LAG >= NSLOT * NB and n % 2 else 2

        def before(pair, n):
            return max([j + 1 for j in range(n) if pair(j) == pair(n)], default=0)

        def x2_chunk(c):
            return x2[:, 2 * c:2 * c + 2].rearrange("p b t d -> p (b t) d")

        GU = 3

        def downs_after(e, k):
            done = [(e - 1, c) for c in DOWN_AT.get(k, [])] if e >= 1 else []
            return done + ([(e, k - 6)] if e == E - 1 and k >= 6 else [])

        def gu_banks(n):
            i = 2 * (n % GU + 1) if n % GU < 2 else 0
            return BK[i], BK[i + 1]

        names = {}

        def s_(name):
            if name not in names:
                names[name] = sem(name)
            return names[name]

        par = lambda b: b % 2

        def fl(b, m):
            return feat[par(b)][:, m].rearrange("p a s -> p (a s)")

        LAG = 2
        A_STEPS = range(-3, NB + LAG)

        block = ctx.enter_context(nc.Block())

        @block.sync
        def _(sp):
            def load_x(b):
                if b >= X_BUFS:
                    sp.wait_ge(s_("x1_sum"), b - X_BUFS + 1)
                sp.dma_start(xin[b % X_BUFS][:, :, :], x_d[b * S:(b + 1) * S, :].rearrange("(t p) d -> p t d", p=P)) \
                    .then_inc(s_(f"x_in{b % X_BUFS}"), 16)

            def load_c(b):
                if b >= 2:
                    sp.wait_ge(s_("cT_mm"), b - 1)
                sp.dma_start(cin[par(b)][:, :, :], ctx_d[b * S:(b + 1) * S, :].rearrange("(t p) d -> p t d", p=P)) \
                    .then_inc(s_(f"c_in{par(b)}"), 16)

            def store_parts(b):
                sp.wait_ge(s_("rope_hi"), b + 1)
                sp.wait_ge(s_("rope_mid"), b + 1)
                sp.wait_ge(s_("rope_lo"), b + 1)
                for w, puts in enumerate((Q_PUT, K_PUT)):
                    for part, first, end, step in puts:
                        dst = packed_d[b, w, :, first:end:step, :]
                        sp.dma_start(dst, parts[par(b)][:, part, w, None, :].to_broadcast(list(dst.shape))) \
                            .then_inc(s_(f"parts_out{par(b)}"), 16)

            def pack(b):
                qd, kd = qb[b % QK_BUFS], kb[b % QK_BUFS]
                if b == 0:
                    sp.wait_ge(s_("qk_rows"), 32 * QK_BUFS)
                    sp.wait_ge(s_("maskb_set"), 1)
                if b >= QK_BUFS:
                    sp.wait_ge(s_("e_mm"), NSLOT * (b - QK_BUFS + 1))
                sp.wait_ge(s_(f"parts_out{par(b)}"), PUTS * (b // 2 + 1))
                for w, dst in enumerate((qd, kd)):
                    src = packed_d[b, w].rearrange("(h d) r s -> h (d r) s", d=DH).rearrange("h p s -> p h s")
                    sp.dma_start(dst[0:MASK_ROW, :, :], src).then_inc(s_(f"packed{b % QK_BUFS}"), 16)
                sp.dma_start(qd[MAX_ROW:MAX_ROW + 3, :, :].rearrange("p h s -> p (h s)"), rows_d[3:6, :]) \
                    .then_inc(s_(f"packed{b % QK_BUFS}"), 16)
                sp.dma_start(kd[MASK_ROW:MASK_ROW + 1, :, :], maskb[b:b + 1, None, :].to_broadcast([1, H, S])) \
                    .then_inc(s_(f"packed{b % QK_BUFS}"), 16)

            load_x(0)
            sp.dma_start(cn[:, :], const_d).then_inc(s_("const_in"), 16)
            sp.dma_start(wa[:, :], wa_d).then_inc(s_("wa_in"), 16)
            load_x(1)
            for tile, src in ((bias, bias_d), (brow, brow_d), (betas, beta_d), (mrow8, mrow_d), (mcol8, mcol_d),
                              (wr, wr_d)):
                sp.dma_start(tile[:, :], src).then_inc(s_("small_in"), 16)
            sp.dma_start(dest[:, :, :, :].rearrange("p b t k -> p (b t k)"), dest_d).then_inc(s_("small_in"), 16)
            load_x(2)
            load_x(3)
            load_c(0)
            load_c(1)
            sp.wait_ge(s_("zrow_set"), 2)
            for i in range(NROWS // (P * 4)):
                sp.dma_start(xe_d[i * 4 * P:(i + 1) * 4 * P, :].rearrange("(p r) n -> p (r n)", p=P), zrow[:, :]) \
                    .then_inc(s_("xe_cleared"), 16)
            for i in range(K * T // (P * 4)):
                sp.dma_start(yb_d[i * 4 * P:(i + 1) * 4 * P, :].rearrange("(p r) n -> p r n", p=P),
                             zrow[:, :].rearrange("p (r n) -> p r n", r=4)[:, :, 0:D]).then_inc(s_("y_cleared"), 16)
            sp.wait_ge(s_("qk_cleared"), 2 * QK_BUFS)
            for i in range(QK_BUFS):
                sp.dma_start(qb[i][MASK_ROW:MASK_ROW + 1, :, :].rearrange("p h s -> p (h s)"), rows_d[0:1, :]) \
                    .then_inc(s_("qk_rows"), 16)
                sp.dma_start(kb[i][MAX_ROW:MAX_ROW + 3, :, :].rearrange("p h s -> p (h s)"), rows_d[0:3, :]) \
                    .then_inc(s_("qk_rows"), 16)

            def put_max(b):
                sp.wait_ge(s_("mT_ev"), b + 1)
                sp.wait_ge(s_("m_mm"), NSLOT * (b + 1))
                for r in range(3):
                    sp.dma_start(qb[b % QK_BUFS][MAX_ROW + r:MAX_ROW + r + 1, :, :], mT[par(b)][H * r:H * r + H, :]) \
                        .then_inc(s_(f"max_put{b % QK_BUFS}"), 16)

            for i in A_STEPS:
                if 4 <= i + 4 < NB:
                    load_x(i + 4)
                if 2 <= i - LAG + 2 < NB:
                    load_c(i - LAG + 2)
                if 0 <= i - LAG < NB:
                    store_parts(i - LAG)
                if 0 <= i - LAG - 1 < QK_BUFS:
                    pack(i - LAG - 1)

            put_max(0)
            for b in range(NB):
                if b + 1 < NB:
                    put_max(b + 1)
                if b + QK_BUFS < NB:
                    pack(b + QK_BUFS)

            def load_w(e):
                if e == 2:
                    sp.wait_ge(s_("e_mm"), NSLOT * NB)
                if e >= E_BUFS:
                    sp.wait_ge(s_("ye_mm"), CT * (e - E_BUFS + 1))
                sm, i = s_(f"w_in{e % E_BUFS}"), e % E_BUFS
                sp.dma_start(w13[i][:, 0, :], w1_d[e]).then_inc(sm, 16)
                sp.dma_start(w13[i][:, 1, :], w3_d[e]).then_inc(sm, 16)
                sp.dma_start(w2[i][:, :, :], w2_d[e].rearrange("(f p) d -> p f d", p=P)).then_inc(sm, 16)

            def load_xe(e):
                if e >= E_BUFS:
                    sp.wait_ge(s_(f"ye_out{par(e - E_BUFS)}"), 16 * CT * ((e - E_BUFS) // 2 + 1))
                sp.dma_start(xe[e % E_BUFS], xe_d[e * CAP:(e + 1) * CAP, :].rearrange("(c p) r -> p c r", p=P)) \
                    .then_inc(s_(f"xe_in{e % E_BUFS}"), 16)

            for e in range(E_BUFS):
                load_w(e)
            sp.wait_ge(s_("rows_out0"), 8 * NB * NT * K)
            sp.wait_ge(s_("rows_out1"), 8 * NB * NT * K)
            for e in range(E_BUFS):
                load_xe(e)
            for e in range(E_BUFS, E):
                load_w(e)
                load_xe(e)
            sp.wait_ge(s_("ye_out0"), 8 * CT * E)
            sp.wait_ge(s_("ye_out1"), 8 * CT * E)
            for c in range(DC):
                for k in range(K):
                    r = k * T + c * DT * P
                    sp.dma_start(yl[c][k][:, :, :], yb_d[r:r + DT * P, :].rearrange("(t p) d -> p t d", p=P)) \
                        .then_inc(s_(f"y_in{c}"), 16)
            for c in range(DC):
                sp.wait_ge(s_("fin_done"), DT * (c + 1) - (DVE_LAST if c == DC - 1 else 0))
                if c == DC - 1:
                    sp.wait_ge(s_("fin_last"), DVE_LAST)
                sp.dma_start(out_d[c * DT * P:(c + 1) * DT * P, :].rearrange("(t p) d -> p t d", p=P), fin[c][:, :, :]) \
                    .then_inc(s_("out_done"), 16)
            sp.wait_ge(s_("out_done"), 16 * DC)
            sp.wait_ge(s_("xe_cleared"), 16 * (NROWS // (4 * P)))
            sp.wait_ge(s_("y_cleared"), 16 * (K * T // (4 * P)))

        @block.tensor
        def _(pe):
            b_T, b_Q, b_KV, b_V2, b_ST, b_O, b_R1, b_R2 = BK

            def mm(out, lhsT, rhs, start=True, stop=True):
                return pe.matmul(out, lhsT, rhs, start=start, stop=stop)

            def transposes(i):
                if 0 <= i + 3 < NB:
                    b = i + 3
                    pe.wait_ge(s_(f"x_in{b % X_BUFS}"), 16 * (b // X_BUFS + 1))
                    if b == 0:
                        pe.wait_ge(s_("const_in"), 16)
                    else:
                        pe.wait_ge(s_("xT_ev"), b)
                    if b >= 3 + LAG:
                        pe.wait_ge(s_("cT_ev"), b - 2 - LAG)
                    for t in range(NT):
                        ins = pe.transpose(b_T[:, t * P:(t + 1) * P], xin[b % X_BUFS][:, t, :], ident)
                    ins.then_inc(s_("xT_mm"), 1)
                if 0 <= i + 1 - LAG < NB:
                    b = i + 1 - LAG
                    pe.wait_ge(s_(f"c_in{par(b)}"), 16 * (b // 2 + 1))
                    pe.wait_ge(s_("xT_ev"), min(NB, b + LAG + 1))
                    if b >= 1:
                        pe.wait_ge(s_("cT_ev"), b)
                    for t in range(NT):
                        ins = pe.transpose(b_T[:, 256 + t * P:256 + (t + 1) * P], cin[par(b)][:, t, :], ident)
                    ins.then_inc(s_("cT_mm"), 1)

            def x1_transpose(i):
                if 0 <= i + 1 - LAG < NB:
                    b = i + 1 - LAG
                    pe.wait_ge(s_("x1_done"), NT * (b + 1))
                    pe.wait_ge(s_("y_clip"), 2 * min(NB, b + LAG + 2))
                    for t in range(NT):
                        ins = pe.transpose(b_Q[:, t * P:(t + 1) * P], xres[:, b, t, :], ident)
                    ins.then_inc(s_("x1T_mm"), 1)

            def out_features(b, ms):
                if ms[0] == 1:
                    pe.wait_ge(s_("wbd_set"), 4 * (b + 1))
                    if b >= 1:
                        pe.wait_ge(s_("oT_ev"), b)
                for m in ms:
                    ins = mm(b_O[:, 0:S], wbd[par(b)][:, m, :], feat[par(b)][:, m, 0, :], m == 1, m == 0)
                if ms[-1] == 0:
                    ins.then_inc(s_("out_mm"), 1)

            def key_value(b):
                pe.wait_ge(s_("f_dve"), 3 * (b + 1))
                pe.wait_ge(s_("f_pool"), 3 * (b + 1))
                pe.wait_ge(s_("f8"), b + 1)
                pe.wait_ge(s_("val_ev"), b + 1)
                if b >= 1:
                    pe.wait_ge(s_("kvt_ev"), b)
                for t in range(NT):
                    for g in range(4):
                        ins = mm(b_ST[32 * g:32 * g + 32, 0:32 * M].rearrange("p (j v) -> p j v", j=M),
                                 val[par(b)][:, t, 32 * g:32 * g + 32],
                                 feat[par(b)][:, :, 1, t * P + 32 * g:t * P + 32 * g + 32], t == 0, t == NT - 1)
                ins.then_inc(s_("kv_mm"), 1)

            def project(b):
                pe.wait_ge(s_("xT_ev"), b + 1)
                if b == 0:
                    pe.wait_ge(s_("wa_in"), 16)
                if b >= 2 + LAG:
                    pe.wait_ge(s_("x1T_ev"), b - 1 - LAG)
                if b >= 1:
                    pe.wait_ge(s_("y_clip"), 2 * b)
                    pe.wait_ge(s_("val_ev"), b)
                mm(b_Q[:, 0:S], wa[:, W_Q:W_Q + D], xT[:, :])
                for t in range(NT):
                    ins = mm(b_KV[:, t * 256:(t + 1) * 256], xT[:, t * P:(t + 1) * P], wa[:, W_KV:W_KV + 2 * D])
                ins.then_inc(s_("qkv_mm"), 1)

            def rope_project(b):
                pe.wait_ge(s_("cT_ev"), b + 1)
                pe.wait_ge(s_("x1_sum"), min(NB, b + LAG))
                if b == 0:
                    pe.wait_ge(s_("rot_signs"), 2)
                else:
                    pe.wait_ge(s_("v2_ev"), b)
                for t in range(NT):
                    ins = mm(b_V2[:, t * P:(t + 1) * P], cT[:, t * P:(t + 1) * P], wa[:, W_XV:W_XV + D])
                ins.then_inc(s_("v2_mm"), 1)
                if b >= 1:
                    pe.wait_ge(s_("rope_mul"), 4 * b)
                mm(b_R1[:, S:2 * S], wa[:, W_XK:W_XK + D], cT[:, :])
                mm(b_R2[:, S:2 * S], wa[:, W_XKR:W_XKR + D], cT[:, :])
                pe.wait_ge(s_("x1T_ev"), b + 1)
                mm(b_R1[:, 0:S], wa[:, W_XQ:W_XQ + D], x1T[:, :])
                mm(b_R2[:, 0:S], wa[:, W_XQR:W_XQR + D], x1T[:, :]).then_inc(s_("rope_mm"), 1)

            def out_project(b):
                pe.wait_ge(s_("oT_ev"), b + 1)
                if b >= 1:
                    pe.wait_ge(s_("x1_sum"), b)
                if b >= LAG:
                    pe.wait_ge(s_("v2_ev"), b - LAG + 1)
                for t in range(NT):
                    ins = mm(b_V2[:, t * P:(t + 1) * P], oT[:, t * P:(t + 1) * P], wa[:, W_O:W_O + D])
                ins.then_inc(s_("y_mm"), 1)

            def m_slot(n):
                b, k = divmod(n, NSLOT)
                c, hq = divmod(k, 4)
                if n == 0:
                    pe.wait_ge(s_("oT_ev"), NB)
                    pe.wait_ge(s_("kvt_ev"), NB)
                if n == PRE_N:
                    pe.wait_ge(s_("rope_mul"), 4 * NB)
                    pe.wait_ge(s_("v2_ev"), NB)
                    pe.wait_ge(s_("x1_sum"), NB)
                if k == 0:
                    pe.wait_ge(s_(f"packed{b % QK_BUFS}"), 16 * 4 * (b // QK_BUFS + 1))
                if before(m_pair, n):
                    pe.wait_ge(s_("max_done"), before(m_pair, n))
                for g in range(4):
                    h = 4 * hq + g
                    ins = mm(pairs[m_pair(n)][:, g * S:(g + 1) * S], qb[b % QK_BUFS][:, h, c * P:(c + 1) * P],
                             kb[b % QK_BUFS][:, h, :])
                ins.then_inc(s_("m_mm"), 1)

            for i in A_STEPS:
                if 0 <= i < NB:
                    out_features(i, [1, 2, 3, 4])
                if 0 <= i + 2 < NB:
                    project(i + 2)
                if 0 <= i + 1 < NB:
                    key_value(i + 1)
                if 0 <= i < NB:
                    out_features(i, [5, 6, 7, 8, 9, 10, 0])
                if 0 <= i - LAG < NB:
                    rope_project(i - LAG)
                transposes(i)
                x1_transpose(i)
                if 0 <= i < NB:
                    out_project(i)
                for n in pre_slots(i):
                    m_slot(n)

            od, gb = BK[0], BK[1]

            def max_transpose(b):
                pe.wait_ge(s_("nm_done"), b + 1)
                g_free(("mt", b))
                for c in range(NT):
                    ins = pe.transpose(gb[0:3 * H, :].bitcast(BF16)[:, c * P:(c + 1) * P],
                                       nm[:, c, :, :].rearrange("p r h -> p (r h)"), idb[:, :])
                ins.then_inc(s_("mT_mm"), 1)

            def e_slot(n):
                b, k = divmod(n, NSLOT)
                hq, kc = divmod(k, 2)
                if k == 0:
                    pe.wait_ge(s_(f"max_put{b % QK_BUFS}"), 48 * (b // QK_BUFS + 1))
                if before(e_pair, n):
                    pe.wait_ge(s_("exp_done"), before(e_pair, n))
                if e_pair(n) != 2:
                    pe.wait_ge(s_("max_done"), NSLOT * NB)
                for g in range(4):
                    h = 4 * hq + g
                    ins = mm(pairs[e_pair(n)][:, g * S:(g + 1) * S], kb[b % QK_BUFS][:, h, kc * P:(kc + 1) * P],
                             qb[b % QK_BUFS][:, h, :])
                ins.then_inc(s_("e_mm"), 1)

            def pv_slot(n):
                b, k = divmod(n, NSLOT)
                hq, kc = divmod(k, 2)
                tt, j = divmod(hq, 2)
                pe.wait_ge(s_("exp_done"), n + 1)
                if k == 0:
                    pe.wait_ge(s_("vp_set"), 2 * (b + 1))
                    if b >= 1:
                        pe.wait_ge(s_("od_read"), b)
                for g in range(4):
                    ins = mm(od[32 * g:32 * g + 32, tt * S:(tt + 1) * S], vp[par(b)][:, kc, 4 * hq + g, :],
                             pr[n % 2][:, g, :], j == 0 and kc == 0, j == 1 and kc == 1)
                ins.then_inc(s_("pv_mm"), 1)

            readers = {"mt": ("mT_ev", 1), "x2t": ("x2T_ev", 1), "log": ("lg_done", 1), "pos": ("pm_done", 1),
                       "wp": ("x2_sum", 1)}
            last = [None]

            def g_free(use):
                if last[0] is not None:
                    name, c = last[0]
                    pe.wait_ge(s_(readers[name][0]), readers[name][1] * (c + 1))
                last[0] = use

            def wp(b):
                pe.wait_ge(s_("odn_done"), b + 1)
                g_free(("wp", b))
                for t in range(NT):
                    for tt in range(2):
                        ins = mm(gb[:, t * P:(t + 1) * P], odn[:, tt * S + t * P:tt * S + (t + 1) * P],
                                 wa[:, W_XP + tt * D:W_XP + (tt + 1) * D], tt == 0, tt == 1)
                ins.then_inc(s_("wp_mm"), 1)

            def x2_transpose(b):
                pe.wait_ge(s_("x2_done"), NT * (b + 1))
                g_free(("x2t", b))
                for t in range(NT):
                    ins = pe.transpose(gb[:, t * P:(t + 1) * P], x2[:, b, t, :], ident)
                ins.then_inc(s_("x2T_mm"), 1)

            def logits(b):
                pe.wait_ge(s_("x2T_ev"), b + 1)
                g_free(("log", b))
                for t in range(NT):
                    ins = mm(gb[:, t * E:(t + 1) * E], x2T[:, t * P:(t + 1) * P], wr[:, :])
                ins.then_inc(s_("lg_mm"), 1)

            def positions(b):
                pe.wait_ge(s_("ohs_done"), b + 1)
                if b == 0:
                    pe.wait_ge(s_("cnt_done"), 1)
                else:
                    pe.wait_ge(s_("cnt_next"), b)
                g_free(("pos", b))
                for t in range(NT):
                    mm(gb[:, t * E:(t + 1) * E], trib[:, :], ohs[:, t, :], True, False)
                    if t == 1:
                        mm(gb[:, t * E:(t + 1) * E], onesb[:, :], ohs[:, 0, :], False, False)
                    ins = mm(gb[:, t * E:(t + 1) * E], onesb[:, :], cnt[par(b)][:, :], False, True)
                ins.then_inc(s_("pos_mm"), 1)

            for n in SLOTS:
                if PRE_N <= n < NSLOT * NB:
                    m_slot(n)
                if (b := batch_at(n, "turn")) is not None:
                    max_transpose(b)
                if 0 <= n - E_LAG < NSLOT * NB:
                    e_slot(n - E_LAG)
                if 0 <= n - E_LAG - 1 < NSLOT * NB:
                    pv_slot(n - E_LAG - 1)
                if (b := batch_at(n, "project")) is not None:
                    wp(b)
                if (b := batch_at(n, "place")) is not None:
                    positions(b)
                if (b := batch_at(n, "x2_turn")) is not None:
                    x2_transpose(b)
                if (b := batch_at(n, "logits")) is not None:
                    logits(b)

            def xe_transpose(e):
                pe.wait_ge(s_(f"xe_in{e % E_BUFS}"), 16 * (e // E_BUFS + 1))
                if e == 0:
                    pe.wait_ge(s_("pm_done"), NB)
                if e >= 2:
                    pe.wait_ge(s_("ye_ev"), CT * (e - 1))
                for c in range(CT):
                    ins = pe.transpose(BK[6 + c // 4][:, (c % 4) * P:(c % 4 + 1) * P], xe[e % E_BUFS][:, c, 0:D], ident)
                    if c >= 3:
                        ins.then_inc(s_("xeT_mm"), 1)

            def hidden(n):
                e, k = divmod(n, 2 * FT)
                half, f = divmod(k, FT)
                if k == 0:
                    pe.wait_ge(s_("xeT_lo"), 2 * (e + 1))
                    pe.wait_ge(s_("w_lo"), 2 * (e + 1))
                if n >= GU:
                    pe.wait_ge(s_("hid_done"), n - GU + 1)
                for w in range(2):
                    for i, (wp_, xp_) in enumerate(((0, 0), (0, 1), (1, 0))):
                        ins = mm(gu_banks(n)[w][:, 0:HALF], wparts[par(e)][:, wp_, w, f * P:(f + 1) * P],
                                 xeT[par(e)][:, xp_, half * HALF:(half + 1) * HALF], i == 0, i == 2)
                ins.then_inc(s_("gu_mm"), 1)

            def down(e, c):
                n = CT * e + c
                pe.wait_ge(s_("hid_done"), 2 * FT * e + (FT if (c + 1) * P <= HALF else 2 * FT))
                if c == 0:
                    pe.wait_ge(s_(f"w_in{e % E_BUFS}"), 48 * (e // E_BUFS + 1))
                if n >= 2:
                    pe.wait_ge(s_("ye_ev"), n - 1)
                for f in range(FT):
                    ins = mm(BK[6 + n % 2][:, 0:P], hid[par(e)][:, f, c * P:(c + 1) * P], w2[e % E_BUFS][:, f, :],
                             f == 0, f == FT - 1)
                ins.then_inc(s_("ye_mm"), 1)

            xe_transpose(0)
            for e in range(E):
                for k in range(2 * FT):
                    hidden(2 * FT * e + k)
                    for e_, c in downs_after(e, k):
                        down(e_, c)
                    if e + 1 < E and k == ROWS_STEP:
                        xe_transpose(e + 1)
            for c in range(CT - 3, CT):
                down(E - 1, c)

        @block.scalar
        def _(act):
            b_T, b_Q, b_KV, b_V2, b_ST, b_O, b_R1, b_R2 = BK

            def take_xT(b):
                if 0 <= b < NB:
                    act.wait_ge(s_("xT_mm"), b + 1)
                    if b >= 2 + LAG:
                        act.wait_ge(s_("cT_mm"), b - 1 - LAG)
                    if b >= 1:
                        act.wait_ge(s_("qkv_mm"), b)
                    act.copy(xT[:, :], b_T[:, 0:S]).then_inc(s_("xT_ev"), 1)

            for i in A_STEPS:
                f, r = i + 2, i - LAG
                if i < -1:
                    take_xT(i + 3)
                if 0 <= f < NB:
                    act.wait_ge(s_("qkv_mm"), f + 1)
                    act.wait_ge(s_("y_clip"), 2 * (f + 1))
                    act.activation(sq[:, 0, :], fl(f, 1), ACT.Square, scale=0.5).then_inc(s_("sq2"), 1)
                    act.copy(val[par(f)][:, :, :],
                             b_KV.rearrange("p (t k n) -> p t k n", t=NT, k=2)[:, :, 1, :]).then_inc(s_("val_ev"), 1)
                    act.wait_ge(s_("sq2"), f + 1)
                    if f == 0:
                        act.wait_ge(s_("halfs_set"), 2)
                    act.activation(fl(f, 2), sq[:, 0, :], ACT.Identity, bias=minus1[:, :]).then_inc(s_("t2"), 1)
                if 0 <= f < NB:
                    act.wait_ge(s_("t2"), f + 1)
                    act.activation(sq[:, 1, :], fl(f, 2), ACT.Square, scale=R2).then_inc(s_("sq4"), 1)
                if 0 <= f < NB:
                    act.wait_ge(s_("sq4"), f + 1)
                    act.activation(fl(f, 4), sq[:, 1, :], ACT.Identity, bias=minus1[:, :]).then_inc(s_("t4"), 1)
                if 0 <= i < NB:
                    act.wait_ge(s_("out_mm"), i + 1)
                    if i >= 1:
                        act.wait_ge(s_("y_mm"), i)
                    act.copy(oT[:, :], b_O[:, 0:S]).then_inc(s_("oT_ev"), 1)
                if 0 <= f < NB:
                    act.wait_ge(s_("t4"), f + 1)
                    act.activation(fl(f, 8), fl(f, 4), ACT.Square, scale=R2).then_inc(s_("f8"), 1)
                if i == -1:
                    take_xT(i + 3)
                if 0 <= i + 1 < NB:
                    b = i + 1
                    act.wait_ge(s_("w_done"), b + 1)
                    for g in range(4):
                        act.copy(wbd[par(b)][32 * g:32 * g + 32, :, 32 * g:32 * g + 32], wq_[32 * g:32 * g + 32, :, :]) \
                            .then_inc(s_("wbd_set"), 1)
                if i >= 0:
                    take_xT(i + 3)
                if 0 <= r + 1 < NB:
                    act.wait_ge(s_("cT_mm"), r + 2)
                    if r + 1 >= 1:
                        act.wait_ge(s_("rope_mm"), r + 1)
                    act.copy(cT[:, :], b_T[:, S:2 * S]).then_inc(s_("cT_ev"), 1)
                    act.wait_ge(s_("x1T_mm"), r + 2)
                    act.copy(x1T[:, :], b_Q[:, 0:S]).then_inc(s_("x1T_ev"), 1)
                if 0 <= r < NB:
                    act.wait_ge(s_("rope_sum"), r + 1)
                    if r >= 2:
                        act.wait_ge(s_(f"parts_out{par(r)}"), PUTS * (r // 2))
                    act.copy(parts[par(r)][:, 0], rsum[:, :, :]).then_inc(s_("rope_hi"), 1)
                    act.wait_ge(s_("rope_r"), r + 1)
                    act.copy(parts[par(r)][:, 1], rr[:, :, :]).then_inc(s_("rope_mid"), 1)

            gb = BK[1]
            for n in SLOTS:
                if (c := batch_at(n, "turn")) is not None:
                    act.wait_ge(s_("mT_mm"), c + 1)
                    if c >= 2:
                        act.wait_ge(s_(f"max_put{(c - 2) % QK_BUFS}"), 48 * ((c - 2) // QK_BUFS + 1))
                    act.copy(mT[par(c)][:, :], gb[0:3 * H, :].bitcast(BF16)[:, 0:S]).then_inc(s_("mT_ev"), 1)
                m = n - E_LAG
                if 0 <= m < NSLOT * NB:
                    act.wait_ge(s_("e_mm"), m + 1)
                    if m >= 2:
                        act.wait_ge(s_("pv_mm"), m - 1)
                    act.activation(pr[m % 2][:, :, :].rearrange("p g s -> p (g s)"), pairs[e_pair(m)][:, :], ACT.Exp,
                                   scale=SC).then_inc(s_("exp_done"), 1)
                if (c := batch_at(n, "x2")) is not None:
                    act.wait_ge(s_("shift2_done"), c + 1)
                    for t in range(NT):
                        act.activation(x2[:, c, t, :], x2p[:, t, :], ACT.Identity, bias=shift2[:, t:t + 1],
                                       scale=rstdb[:, t:t + 1]).then_inc(s_("x2_done"), 1)
                if (c := batch_at(n, "x2_turn")) is not None:
                    act.wait_ge(s_("x2T_mm"), c + 1)
                    act.copy(x2T[:, :], gb[:, 0:S]).then_inc(s_("x2T_ev"), 1)
                if (c := batch_at(n, "choose")) is not None:
                    act.wait_ge(s_("dv_done"), c + 1)
                    act.activation(ev[:, :], dv[:, :], ACT.Exp).then_inc(s_("ev_done"), 1)

            def high_weights(e, w):
                if w == 0:
                    act.wait_ge(s_(f"w_in{e % E_BUFS}"), 48 * (e // E_BUFS + 1))
                    if e == 0:
                        act.wait_ge(s_("vp_set"), 2 * NB)
                    if e >= 2:
                        act.wait_ge(s_("gu_mm"), 2 * FT * (e - 1))
                act.activation(wparts[par(e)][:, 0, w, :], w13[e % E_BUFS][:, w, :], ACT.Copy, scale=W_UP) \
                    .then_inc(s_("w_hi"), 1)

            for w in range(2):
                high_weights(0, w)
            for e in range(E):
                def take_xeT(e):
                    for i, (bank, c, n) in enumerate(((BK[6], 0, 4 * P), (BK[7], 4 * P, P))):
                        act.wait_ge(s_("xeT_mm"), 2 * e + i + 1)
                        act.activation(xeT[par(e)][:, 0, c:c + n], bank[:, 0:n], ACT.Copy, scale=X_UP) \
                            .then_inc(s_("xeT_ev"), 1)
                if e == 0:
                    take_xeT(0)
                for k in range(2 * FT):
                    n = e * 2 * FT + k
                    act.wait_ge(s_("gu_mm"), n + 1)
                    if n >= 2:
                        act.wait_ge(s_("hid_done"), n - 1)
                    act.activation(sil[n % 2], gu_banks(n)[0][:, 0:HALF], ACT.Silu, scale=1 / (X_UP * W_UP)) \
                        .then_inc(s_("silu_done"), 1)
                    if e + 1 < E and k in W_STEPS:
                        high_weights(e + 1, W_STEPS.index(k))
                    if e + 1 < E and k == ROWS_STEP:
                        take_xeT(e + 1)

            for c in range(DC):
                act.wait_ge(s_("shift_done"), c + 1)
                for t in range(DT - (DVE_LAST if c == DC - 1 else 0)):
                    i = DT * c + t
                    act.activation(fin[c][:, t, :], fin[c][:, t, :], ACT.Identity, bias=shift[:, i:i + 1],
                                   scale=rstdd[:, i:i + 1]).then_inc(s_("fin_done"), 1)

        @block.vector
        def _(dve):
            b_T, b_Q, b_KV, b_V2, b_ST, b_O, b_R1, b_R2 = BK
            tt, ts, stt = dve.tensor_tensor, dve.tensor_scalar, dve.scalar_tensor_tensor
            chain = [0]

            def link(ins):
                chain[0] += 1
                ins.then_inc(s_("dve_chain"), 1)
                dve.wait_ge(s_("dve_chain"), chain[0])

            def keep(ins):
                chain[0] += 1
                ins.then_inc(s_("dve_chain"), 1)
                return chain[0]

            def need(at):
                dve.wait_ge(s_("dve_chain"), at)

            for i in range(2):
                dve.memset(feat[i][:, 0, :, :], 1.0)
                dve.memset(wbd[i][:, :, :], 0.0)
            link(dve.memset(on[:, :, :], 0.0))
            dve.memset(on[:, 0:8, BIAS_COL:BIAS_COL + 1], 1.0)
            dve.memset(onesb[:, :], 1.0)
            dve.memset(cnt[0][:, :], 0.0).then_inc(s_("cnt_done"), 1)
            dve.wait_ge(s_("const_in"), 16)
            dve.tensor_copy(idb[:, :], ident)
            link(dve.tensor_copy(trib[:, :], cn[:, C_TRI:C_TRI + P]))
            need(chain[0])
            dve.wait_ge(s_("small_in"), 16 * 7)
            dve.wait_ge(s_("wa_in"), 16)
            sgn = cn[:, C_SGN:C_SGN + P]
            tt(wa[:, W_XQR:W_XQR + D], wa[:, W_XQR:W_XQR + D], sgn, ALU.mult).then_inc(s_("rot_signs"), 1)
            tt(wa[:, W_XKR:W_XKR + D], wa[:, W_XKR:W_XKR + D], sgn, ALU.mult).then_inc(s_("rot_signs"), 1)
            sc = cn[:, C_SGNC:C_SGNC + 1]
            link(ts(bias[:, 2:4], bias[:, 2:4], sc, None, ALU.mult))
            def setup_rest():
                link(ts(betas[:, 1:2], betas[:, 1:2], SC * SC, None, ALU.mult))
                link(ts(betas[:, 6:8], betas[:, 6:8], 2.0, None, ALU.mult))
                link(ts(betas[:, 10:11], betas[:, 10:11], 2.0, None, ALU.mult))
                for m in range(M):
                    ins = ts(bm[:, m, :], cn[:, C_BLK:C_BLK + 32], betas[:, m:m + 1], None, ALU.mult)
                link(ins)
                link(ts(tmask[:, :], mcol8[:, :], 1.0, None, ALU.mult))
                ts(maskb[:, :], mrow8[:, :], -1.0, MASKED, ALU.add, ALU.mult).then_inc(s_("maskb_set"), 1)

            def clip(b):
                dve.wait_ge(s_("qkv_mm"), b + 1)
                y = feat[par(b)]
                ts(y[:, 1, 0, :], b_Q[:, 0:S], 1.0 / SC, -1.0 / SC, ALU.min, ALU.max).then_inc(s_("y_clip"), 1)
                ts(y[:, 1, 1, :].rearrange("p (t n) -> p t n", t=NT),
                   b_KV.rearrange("p (t k n) -> p t k n", t=NT, k=2)[:, :, 0, :],
                   1.0 / SC, -1.0 / SC, ALU.min, ALU.max).then_inc(s_("y_clip"), 1)

            def features(b):
                dve.wait_ge(s_("y_clip"), 2 * (b + 1))
                dve.wait_ge(s_("t2"), b + 1)
                stt(fl(b, 3), fl(b, 1), 2 * SC, fl(b, 2), ALU.mult, ALU.mult).then_inc(s_("f_dve"), 1)
                dve.wait_ge(s_("t4"), b + 1)
                if b >= 2:
                    dve.wait_ge(s_("out_mm"), b - 1)
                stt(fl(b, 5), fl(b, 1), 2 * SC, fl(b, 4), ALU.mult, ALU.mult).then_inc(s_("f_dve"), 1)
                dve.wait_ge(s_("f8"), b + 1)
                stt(fl(b, 9), fl(b, 1), 2 * SC, fl(b, 8), ALU.mult, ALU.mult).then_inc(s_("f_dve"), 1)

            def combine(b):
                dve.wait_ge(s_("kv_mm"), b + 1)
                dve.transpose(kvt[:, :, :].rearrange("p j v -> p (j v)"), b_ST[:, 0:32 * M]).then_inc(s_("kvt_ev"), 1)
                dve.wait_ge(s_("kvt_ev"), b + 1)
                k = lambda j: kvt[:, j, :]
                w = lambda j: wq_[:, j, :]
                a3 = keep(stt(k(3), k(1), -SC, k(3), ALU.mult, ALU.add))
                a7 = keep(stt(k(7), k(7), 2.0, k(5), ALU.mult, ALU.subtract))
                keep(tt(k(8), k(8), k(0), ALU.subtract))
                a6 = keep(stt(k(6), k(6), 2.0, k(2), ALU.mult, ALU.subtract))
                a9 = keep(stt(k(9), k(1), -2.0 * SC, k(9), ALU.mult, ALU.add))
                need(a7)
                keep(tt(k(5), k(5), k(3), ALU.subtract))
                a7 = keep(stt(k(7), k(1), -SC, k(7), ALU.mult, ALU.add))
                need(a6)
                a10 = keep(stt(k(10), k(10), 2.0, k(6), ALU.mult, ALU.subtract))
                need(a7)
                keep(tt(k(9), k(9), k(7), ALU.subtract))
                need(a10)
                link(stt(k(10), k(2), -2.0, k(10), ALU.mult, ALU.add))
                if b >= 1:
                    dve.wait_ge(s_("wbd_set"), 4 * b)
                link(tt(wq_[:, :, :], kvt[:, :, :], bm[:, :, :], ALU.mult))
                v, y, x = tmp32[:, 0, :], tmp32[:, 1, :], tmp32[:, 2, :]
                keep(stt(v, w(7), 0.5, w(9), ALU.mult, ALU.add))
                b3 = keep(tt(w(3), w(3), w(5), ALU.subtract))
                b7 = keep(stt(w(7), w(9), -2.0, w(7), ALU.mult, ALU.add))
                bx = keep(tt(x, w(6), w(10), ALU.add))
                need(b3)
                by = keep(tt(y, w(3), v, ALU.add))
                need(b7)
                keep(stt(w(5), w(7), -0.5, w(5), ALU.mult, ALU.add))
                need(bx)
                keep(stt(w(2), x, -0.5, w(2), ALU.mult, ALU.add))
                keep(tt(w(6), w(6), w(10), ALU.subtract))
                need(by)
                keep(stt(w(1), y, -SC, w(1), ALU.mult, ALU.add))
                keep(tt(w(0), w(0), w(8), ALU.subtract))
                need(chain[0])
                dve.tensor_copy(tmp32[:, 0, 0:1], w(0)[:, 0:1]).then_inc(s_("w_done"), 1)

            def values(b):
                dve.wait_ge(s_("v2_mm"), b + 1)
                tt(v2[:, b].rearrange("p t n -> p (t n)").rearrange("p (t n) -> p t n", t=NT),
                   b_V2[:, 0:S].rearrange("p (t n) -> p t n", t=NT),
                   brow[:, None, 0:D].to_broadcast([P, NT, D]), ALU.add).then_inc(s_("v2_ev"), 1)

            def rope(b):
                dve.wait_ge(s_("rope_mm"), b + 1)
                if b >= 1:
                    dve.wait_ge(s_("rope_sum"), b)
                for w in range(2):
                    for bank, table, off, dst in ((b_R1, C_COS, 0, rc), (b_R2, C_SIN, 2, rs)):
                        stt(dst[:, w, :], bank[:, w * S:(w + 1) * S], bias[:, off + w:off + w + 1],
                            cn[:, table:table + S], ALU.add, ALU.mult).then_inc(s_("rope_mul"), 1)

            def norm_stats(src, st, mvt, done):
                for t in range(NT):
                    at = keep(dve.bn_stats(st[:, t, :], src[:, t, :]))
                need(at)
                for t in range(NT):
                    dve.bn_aggr(mvt[:, t, :], st[:, t, :]).then_inc(s_(done), 1)

            def norm1(b):
                dve.wait_ge(s_("y_mm"), b + 1)
                tt(ypre[:, :, :], b_V2[:, 0:S].rearrange("p (t n) -> p t n", t=NT), xin[b % X_BUFS][:, :, :], ALU.add) \
                    .then_inc(s_("x1_sum"), 1)
                dve.wait_ge(s_("x1_sum"), b + 1)
                norm_stats(ypre, st6, mv, "mv1")

            def norm1_end(b):
                dve.wait_ge(s_("rstd1"), b + 1)
                for t in range(NT):
                    ts(xres[:, b, t, :], ypre[:, t, :], mv[:, t, 0:1], rstd[:, t:t + 1], ALU.subtract, ALU.mult) \
                        .then_inc(s_("x1_done"), 1)

            def row_max(n):
                b, k = divmod(n, NSLOT)
                c, hq = divmod(k, 4)
                dve.wait_ge(s_("m_mm"), n + 1)
                dve.tensor_reduce(mx[par(b)][:, c, 4 * hq:4 * hq + 4],
                                  pairs[m_pair(n)][:, :].rearrange("p (g s) -> p g s", g=4), AX.X, ALU.max) \
                    .then_inc(s_("max_done"), 1)

            for i in A_STEPS:
                if 0 <= i + 2 < NB:
                    clip(i + 2)
                if i + 2 == 0:
                    setup_rest()
                if 0 <= i + 1 < NB:
                    combine(i + 1)
                if 0 <= i - LAG < NB:
                    values(i - LAG)
                if 0 <= i + 2 < NB:
                    features(i + 2)
                if 0 <= i < NB:
                    norm1(i)
                if 0 <= i - LAG < NB:
                    rope(i - LAG)
                if 0 <= i < NB:
                    norm1_end(i)
                for n in pre_slots(i):
                    row_max(n)

            od, gb = BK[0], BK[1]

            def split_max(b):
                m = mx[par(b)][:, :, :]
                dve.wait_ge(s_("max_done"), NSLOT * (b + 1))
                if b >= 1:
                    dve.wait_ge(s_("mT_mm"), b)
                link(ts(nm[:, :, 0, :], m, -1.0, None, ALU.mult))
                link(stt(mr[:, :, :], m, -1.0, nm[:, :, 0, :], ALU.mult, ALU.subtract))
                link(dve.tensor_copy(nm[:, :, 1, :], mr[:, :, :]))
                tt(nm[:, :, 2, :], mr[:, :, :], nm[:, :, 1, :], ALU.subtract).then_inc(s_("nm_done"), 1)

            def norm2(b):
                dve.wait_ge(s_("wp_mm"), b + 1)
                if b >= 1:
                    dve.wait_ge(s_("x2_done"), NT * b)
                for t in range(NT):
                    ins = stt(x2p[:, t, :], gb[:, t * P:(t + 1) * P], tmask[:, b * NT + t:b * NT + t + 1],
                              xres[:, b, t, :], ALU.mult, ALU.add)
                ins.then_inc(s_("x2_sum"), 1)
                dve.wait_ge(s_("x2_sum"), b + 1)
                norm_stats(x2p, st6b, mvb, "mv2")

            def take_outputs(b):
                dve.wait_ge(s_("pv_mm"), NSLOT * (b + 1))
                dve.transpose(ot[:, :, :].rearrange("p a c -> p (a c)"), od).then_inc(s_("od_read"), 1)

            def normalise(b):
                dve.wait_ge(s_("od_read"), b + 1)
                link(dve.reciprocal(rden[:, :, :], ot[:, :, 16:18]))
                tt(on[:, :, 0:16].rearrange("p a (j d) -> p a j d", j=2),
                   ot[:, :, 0:16].rearrange("p a (j d) -> p a j d", j=2),
                   rden[:, :, :, None].to_broadcast([P, 16, 2, DH]), ALU.mult).then_inc(s_("on_done"), 1)

            def features_down(b):
                dve.wait_ge(s_("on_done"), b + 1)
                if b >= 1:
                    dve.wait_ge(s_("wp_mm"), b)
                dve.transpose(odn[:, :], on[:, :, :].rearrange("p a c -> p (a c)")).then_inc(s_("odn_done"), 1)

            def norm2_shift(b):
                dve.wait_ge(s_("rstd2"), b + 1)
                stt(shift2[:, :], mvb[:, :, 0], -1.0, rstdb[:, :], ALU.mult, ALU.mult).then_inc(s_("shift2_done"), 1)

            def clip_logits(b):
                dve.wait_ge(s_("lg_mm"), b + 1)
                ts(lg[:, :, :], gb[:, 0:NT * E].rearrange("p (t e) -> p t e", t=NT), CLAMP, -CLAMP, ALU.min, ALU.max) \
                    .then_inc(s_("lg_done"), 1)

            def choose(b):
                dve.wait_ge(s_("lg_done"), b + 1)
                for t in range(NT):
                    at = keep(dve.max(v8[:, t, :], lg[:, t, :]))
                need(at)
                for t in range(NT):
                    at = keep(dve.max_index(i8[:, t, :], v8[:, t, :], lg[:, t, :]))
                if b >= 1:
                    dve.wait_ge(s_("w_all"), b)
                tt(dv[:, :], v8[:, :, 1], v8[:, :, 0], ALU.subtract).then_inc(s_("dv_done"), 1)
                need(at)
                link(dve.tensor_copy(idf[:, :, :], i8[:, :, 0:K]))
                link(tt(oh[:, :, :, :].rearrange("p t k e -> p (t k) e"),
                        cn[:, C_IOTA:C_IOTA + 32].rearrange("p (a e) -> p a e", e=E),
                        idf[:, :, :].rearrange("p t k -> p (t k)")[:, :, None].to_broadcast([P, NT * K, E]),
                        ALU.is_equal))
                if b >= 1:
                    dve.wait_ge(s_("pos_mm"), b)
                    dve.wait_ge(s_("ohsum"), b)
                tt(ohs[:, :, :], oh[:, :, 0, :], oh[:, :, 1, :], ALU.add).then_inc(s_("ohs_done"), 1)

            def take_positions(b):
                dve.wait_ge(s_("pos_mm"), b + 1)
                tt(pm[:, :, :].rearrange("p (t k) e -> p t k e", t=NT),
                   gb[:, 0:NT * E].rearrange("p (t e) -> p t e", t=NT)[:, :, None, :].to_broadcast([P, NT, K, E]),
                   oh[:, :, :, :], ALU.mult).then_inc(s_("pm_done"), 1)

            def place(b):
                w = xp[par(b)]
                dve.wait_ge(s_("ev_done"), b + 1)
                total = keep(ts(ev1[:, :], ev[:, :], 1.0, 1e-12, ALU.add, ALU.add))
                dve.wait_ge(s_("pm_done"), b + 1)
                rank = keep(dve.tensor_reduce(pos[:, :], pm[:, :, :], AX.X, ALU.add))
                if b >= 2:
                    dve.wait_ge(s_(f"rows_out{par(b)}"), 16 * NT * K * (b // 2))
                need(total)
                first = keep(dve.reciprocal(w[:, :, 0, D], ev1[:, :]))
                need(rank)
                keep(ts(over[:, :], pos[:, :], float(CAP), FAR, ALU.is_ge, ALU.mult))
                row = keep(stt(slf[:, :], idf[:, :, :].rearrange("p t k -> p (t k)"), float(CAP), pos[:, :],
                               ALU.mult, ALU.add))
                need(first)
                tt(w[:, :, 1, D], ev[:, :], w[:, :, 0, D], ALU.mult).then_inc(s_("w_all"), 1)
                need(row)
                tt(slot[par(b)][:, :], slf[:, :], over[:, :], ALU.add).then_inc(s_("slot_done"), 1)

            for n in SLOTS:
                if (b := batch_at(n, "x2")) is not None:
                    norm2_shift(b)
                if (b := batch_at(n, "clip")) is not None:
                    clip_logits(b)
                if PRE_N <= n < NSLOT * NB:
                    row_max(n)
                if (b := batch_at(n, "out")) is not None:
                    take_outputs(b)
                if (b := batch_at(n, "split")) is not None:
                    split_max(b)
                if (b := batch_at(n, "normal")) is not None:
                    normalise(b)
                if (b := batch_at(n, "back")) is not None:
                    features_down(b)
                if (b := batch_at(n, "norm2")) is not None:
                    norm2(b)
                if (b := batch_at(n, "choose")) is not None:
                    choose(b)
                if (b := batch_at(n, "place")) is not None:
                    take_positions(b)
                    place(b)

            def hid_mul(n):
                e, r = divmod(n, 2 * FT)
                half, f = divmod(r, FT)
                dve.wait_ge(s_("silu_done"), n + 1)
                if r == 0 and e >= 2:
                    dve.wait_ge(s_("ye_mm"), CT * (e - 1))
                stt(hid[par(e)][:, f, half * HALF:(half + 1) * HALF], gu_banks(n)[1][:, 0:HALF],
                    1 / (X_UP * W_UP), sil[n % 2], ALU.mult, ALU.mult).then_inc(s_("hid_done"), 1)

            def low_weights(e, w):
                dve.wait_ge(s_("w_hi"), 2 * e + w + 1)
                stt(wparts[par(e)][:, 1, w, :], w13[e % E_BUFS][:, w, :], W_UP, wparts[par(e)][:, 0, w, :],
                    ALU.mult, ALU.subtract).then_inc(s_("w_lo"), 1)

            def low_rows(e):
                for i, (bank, c, n) in enumerate(((BK[6], 0, 4 * P), (BK[7], 4 * P, P))):
                    dve.wait_ge(s_("xeT_ev"), 2 * e + i + 1)
                    stt(xeT[par(e)][:, 1, c:c + n], bank[:, 0:n], X_UP, xeT[par(e)][:, 0, c:c + n],
                        ALU.mult, ALU.subtract).then_inc(s_("xeT_lo"), 1)

            def take_y(e, c):
                n = CT * e + c
                dve.wait_ge(s_("ye_mm"), n + 1)
                if c == 0 and e >= 2:
                    dve.wait_ge(s_(f"ye_out{par(e)}"), 16 * CT * (e // 2))
                ts(ye[par(e)][:, c, :], BK[6 + n % 2][:, 0:P], xe[e % E_BUFS][:, c, D:D + 1], None, ALU.mult) \
                    .then_inc(s_("ye_ev"), 1)

            for w in range(2):
                low_weights(0, w)
            low_rows(0)
            for e in range(E):
                for k in range(2 * FT):
                    hid_mul(e * 2 * FT + k)
                    for e_, c in downs_after(e, k):
                        take_y(e_, c)
                    if e + 1 < E and k in W_STEPS:
                        low_weights(e + 1, W_STEPS.index(k))
                    if e + 1 < E and k == ROWS_STEP:
                        low_rows(e + 1)
            for c in range(CT - 3, CT):
                take_y(E - 1, c)

            def sum_stats(c):
                dve.wait_ge(s_(f"y_in{c}"), 16 * K)
                if c == 0:
                    link(tt(fin[c][:, :, :], yl[c][0][:, :, :], x2_chunk(c), ALU.add))
                else:
                    dve.wait_ge(s_("residual_in"), c)
                link(tt(fin[c][:, :, :], fin[c][:, :, :], yl[c][1][:, :, :], ALU.add))
                for t in range(DT):
                    at = keep(dve.bn_stats(st6d[:, DT * c + t, :], fin[c][:, t, :]))
                need(at)
                for t in range(DT):
                    dve.bn_aggr(mvd[:, DT * c + t, :], st6d[:, DT * c + t, :]).then_inc(s_("mv3"), 1)

            def shifts(c):
                dve.wait_ge(s_("rstd3"), c + 1)
                stt(shift[:, DT * c:DT * (c + 1)], mvd[:, DT * c:DT * (c + 1), 0], -1.0, rstdd[:, DT * c:DT * (c + 1)],
                    ALU.mult, ALU.mult).then_inc(s_("shift_done"), 1)

            for c in range(DC):
                sum_stats(c)
                if c >= 1:
                    shifts(c - 1)
            shifts(DC - 1)
            last = DC - 1
            dve.wait_ge(s_("rstd3"), DC)
            for t in range(DT - DVE_LAST, DT):
                i = DT * last + t
                ts(fin[last][:, t, :], fin[last][:, t, :], mvd[:, i, 0:1], rstdd[:, i:i + 1], ALU.subtract, ALU.mult) \
                    .then_inc(s_("fin_last"), 1)

        @block.gpsimd
        def _(pool):
            tt, ts = pool.tensor_tensor, pool.tensor_scalar

            def copy(out, src):
                return ts(out, src, 1.0, 0.0, ALU.mult, ALU.add)

            pool.memset(zrow[:, :], 0.0).then_inc(s_("zrow_set"), 1)
            pool.wait_ge(s_("zrow_set"), 1)
            pool.memset(zrow[:, :].rearrange("p (r n) -> p r n", r=4)[:, :, D + 1].bitcast(U32), NOWHERE) \
                .then_inc(s_("zrow_set"), 1)
            pool.memset(halfs[:, :], -0.5).then_inc(s_("halfs_set"), 1)
            pool.memset(minus1[:, :], -1.0).then_inc(s_("halfs_set"), 1)
            for i in range(QK_BUFS):
                for tile in (qb[i], kb[i]):
                    pool.memset(tile[:, :, :].rearrange("p h s -> p (h s)").bitcast(U32), 0) \
                        .then_inc(s_("qk_cleared"), 1)
            for i in range(2):
                pool.memset(vp[i][:, :, :, :], 0.0).then_inc(s_("vp_const"), 1)
            pool.wait_ge(s_("vp_const"), 2)
            for i in range(2):
                for j in range(2):
                    pool.memset(vp[i][:, :, :, :].rearrange("p c (u j g) n -> p (c u) j g n", u=2, j=2)
                                [:, :, j, :, 16 + j:17 + j], 1.0).then_inc(s_("vp_const"), 1)
            pool.wait_ge(s_("halfs_set"), 1)

            def rsqrt(b, count, dst_v, mvt, dst, sem_mv, name, at, n):
                pool.wait_ge(s_(sem_mv), count)
                ts(dst_v, mvt, EPS, None, ALU.add).then_inc(s_("var_eps"), 1)
                at[0] += 1
                pool.wait_ge(s_("var_eps"), at[0])
                tt(dst, dst_v, halfs[:, 0:n], ALU.pow).then_inc(s_(name), 1)

            at = [0]

            for i in A_STEPS:
                f, r = i + 2, i - LAG
                if 0 <= f < NB:
                    pool.wait_ge(s_("t4"), f + 1)
                    if f >= 2:
                        pool.wait_ge(s_("out_mm"), f - 1)
                    tt(fl(f, 6), fl(f, 2), fl(f, 4), ALU.mult).then_inc(s_("f_pool"), 1)
                    pool.wait_ge(s_("f_dve"), 3 * f + 1)
                    tt(fl(f, 7), fl(f, 3), fl(f, 4), ALU.mult).then_inc(s_("f_pool"), 1)
                    pool.wait_ge(s_("f8"), f + 1)
                    tt(fl(f, 10), fl(f, 2), fl(f, 8), ALU.mult).then_inc(s_("f_pool"), 1)
                if 0 <= i < NB:
                    rsqrt(i, NT * (i + 1), ve[:, :], mv[:, :, 1], rstd[:, :], "mv1", "rstd1", at, NT)
                if 0 <= r < NB:
                    pool.wait_ge(s_("rope_mul"), 4 * (r + 1))
                    tt(rsum[:, :, :], rc[:, :, :], rs[:, :, :], ALU.add).then_inc(s_("rope_sum"), 1)
                    pool.wait_ge(s_("rope_hi"), r + 1)
                    tt(rr[:, :, :], rsum[:, :, :], parts[par(r)][:, 0], ALU.subtract).then_inc(s_("rope_r"), 1)
                    pool.wait_ge(s_("rope_mid"), r + 1)
                    tt(parts[par(r)][:, 2], rr[:, :, :], parts[par(r)][:, 1], ALU.subtract).then_inc(s_("rope_lo"), 1)

            pool.wait_ge(s_("xe_cleared"), 16 * (NROWS // (4 * P)))
            for n in SLOTS:
                if (b := batch_at(n, "values")) is not None:
                    pool.wait_ge(s_("v2_ev"), b + 1)
                    if b == 0:
                        pool.wait_ge(s_("vp_const"), 6)
                    if b >= 2:
                        pool.wait_ge(s_("pv_mm"), NSLOT * (b - 1))
                    src = v2[:, b].rearrange("p c (u j g d) -> p (c u) j g d", u=2, j=2, g=4)
                    dst = vp[par(b)][:, :, :, :].rearrange("p c (u j g) n -> p (c u) j g n", u=2, j=2)
                    for j in range(2):
                        copy(dst[:, :, j, :, DH * j:DH * j + DH], src[:, :, j]).then_inc(s_("vp_set"), 1)
                if (c := batch_at(n, "norm2")) is not None:
                    rsqrt(c, NT * (c + 1), veb[:, :], mvb[:, :, 1], rstdb[:, :], "mv2", "rstd2", at, NT)
                if (c := batch_at(n, "x2")) is not None:
                    pool.wait_ge(s_("x2_done"), NT * (c + 1))
                    if c >= 2:
                        pool.wait_ge(s_(f"rows_out{par(c)}"), 16 * NT * K * (c // 2))
                    for k_ in range(K):
                        copy(xp[par(c)][:, :, k_, 0:D], x2[:, c]).then_inc(s_("xp_set"), 1)
                    pool.tensor_copy(xp[par(c)][:, :, :, D + 1].bitcast(U32), dest[:, c]).then_inc(s_("xp_set"), 1)
                if (c := batch_at(n, "choose")) is not None:
                    pool.wait_ge(s_("ohs_done"), c + 1)
                    if c == 0:
                        pool.wait_ge(s_("cnt_done"), 1)
                    else:
                        pool.wait_ge(s_("cnt_next"), c)
                    tt(ohsum[:, :], ohs[:, 0, :], ohs[:, 1, :], ALU.add).then_inc(s_("ohsum"), 1)
                    pool.wait_ge(s_("ohsum"), c + 1)
                    if c >= 1:
                        pool.wait_ge(s_("pos_mm"), c)
                    tt(cnt[par(c + 1)][:, :], cnt[par(c)][:, :], ohsum[:, :], ALU.add).then_inc(s_("cnt_next"), 1)
                if (c := batch_at(n, "place")) is not None:
                    pool.wait_ge(s_("slot_done"), c + 1)
                    pool.wait_ge(s_("w_all"), c + 1)
                    pool.wait_ge(s_("xp_set"), 3 * (c + 1))
                    for t in range(NT):
                        for k_ in range(K):
                            i = t * K + k_
                            pool.indirect_dma_start(
                                out=xe_d, out_offset=bass.IndirectOffsetOnAxis(ap=slot[par(c)][:, i:i + 1], axis=0),
                                in_=xp[par(c)][:, t, k_, :], in_offset=None, bounds_check=NROWS - 1, oob_is_err=False) \
                                .then_inc(s_(f"rows_out{par(c)}"), 16)

            pool.wait_ge(s_("y_cleared"), 16 * (K * T // (4 * P)))
            for e in range(E):
                for c in range(CT):
                    pool.wait_ge(s_("ye_ev"), CT * e + c + 1)
                    pool.indirect_dma_start(
                        out=yb_d, out_offset=bass.IndirectOffsetOnAxis(ap=xe[e % E_BUFS][:, c, D + 1:D + 2].bitcast(U32), axis=0),
                        in_=ye[par(e)][:, c, :], in_offset=None, bounds_check=K * T - 1, oob_is_err=False) \
                        .then_inc(s_(f"ye_out{par(e)}"), 16)

            def residual(c):
                if c < DC:
                    pool.wait_ge(s_(f"y_in{c}"), 16 * K)
                    tt(fin[c][:, :, :], yl[c][0][:, :, :], x2_chunk(c), ALU.add).then_inc(s_("residual_in"), 1)

            residual(1)
            for c in range(DC):
                residual(c + 2)
                i, j = DT * c, DT * (c + 1)
                rsqrt(c, DT * (c + 1), ved[:, i:j], mvd[:, i:j, 1], rstdd[:, i:j], "mv3", "rstd3", at, DT)


def kernel(**inputs):
    import numpy as _np
    import concourse.bacc as _bacc
    from concourse import mybir as _mybir
    from concourse.bass_utils import run_bass_kernel_spmd as _run

    a = {k: _np.asarray(v) for k, v in inputs.items()}
    swap = _np.arange(D).reshape(H, 2, DH // 2)[:, ::-1].reshape(-1)
    wq, wk = a["L0_xattn_Wq"], a["L0_xattn_Wk"]
    wp_t = a["L0_xattn_Wp"].T
    wp_rows = _np.zeros((2, 4, 32, D), wp_t.dtype)
    wp_rows[:, :, 0:2 * DH] = wp_t.reshape(2, 2, 4, DH, D).transpose(0, 2, 1, 3, 4).reshape(2, 4, 2 * DH, D)
    wp_rows[0, 0, BIAS_COL] = a["L0_xattn_bp"]
    w_in_t = a["L0_attn_w_in"].T
    wa = _np.concatenate([w_in_t, a["L0_attn_w_out"].T, wq.T, wq[swap].T, wk.T, wk[swap].T,
                          a["L0_xattn_Wv"].T, wp_rows[0].reshape(P, D), wp_rows[1].reshape(P, D)], axis=1)
    bq, bk = a["L0_xattn_bq"], a["L0_xattn_bk"]
    bias = _np.stack([bq, bk, bq[swap], bk[swap]], axis=1)
    brow = _np.broadcast_to(a["L0_xattn_bv"][None], (P, D))
    mask = a["mask_BxS2_bf1"].view(_np.uint8)
    const, dest = constants()
    ones_zeros = _np.zeros((6, H * S), _mybir.dt.np(_mybir.dt.bfloat16))
    ones_zeros[0:3] = 1
    arrays = {
        "x": a["x"].reshape(T, D), "ctx": a["ctx_1024"].reshape(T, D), "mrow": mask,
        "mcol": mask.reshape(NB * NT, P).T, "beta": _np.repeat(a["L0_attn_beta"], DH, axis=0), "wa": wa,
        "bias": bias, "brow": brow, "wr": a["L0_ffn_Wr"], "w1": a["L0_ffn_W1"], "w3": a["L0_ffn_W3"],
        "w2": a["L0_ffn_W2"], "const": const, "dest": dest, "rows": ones_zeros,
    }
    arrays = {f"in_{k}": _np.ascontiguousarray(v) for k, v in arrays.items()}
    nc = _bacc.Bacc("TRN2", target_bir_lowering=False, num_devices=1)
    args = [nc.dram_tensor(k, v.shape, _mybir.dt.from_np(v.dtype), kind="ExternalInput").ap() for k, v in arrays.items()]
    out = nc.dram_tensor("out", (T, D), F32, kind="ExternalOutput").ap()
    build(nc, *args, out)
    r = _run(nc, [arrays], core_ids=[0])
    return r.results[0]["out"].reshape(NB, S, D)
```
